# Optimizing a Trainium2 kernel written in Bass

```python
import numpy as np
import jax
import jax.numpy as jnp

def _softmax(x, axis=-1):
    return jax.nn.softmax(x, axis=axis)

def _gelu(x):
    return jax.nn.gelu(x, approximate=True)

def _silu(x):
    return jax.nn.silu(x)

def _sigmoid(x):
    return jax.nn.sigmoid(x)

def _layernorm(x, axis=-1, eps=1e-05):
    m = jnp.mean(x, axis=axis, keepdims=True)
    v = jnp.var(x, axis=axis, keepdims=True)
    return (x - m) / jnp.sqrt(v + eps)

def _scatter_add(tgt, idx, src, axis=0):
    return tgt.at[idx].add(src)

def _segment_sum(src, seg, n):
    return jax.ops.segment_sum(src, seg, n)
kernel_name = 'mk_gps_d1_gnn_r8_fbecdb'

def setup_inputs(seed: int=0):
    np.random.seed(seed)
    _w = jnp.asarray

    def _rec_inputs():
        import jax
        import jax.numpy as jnp
        _gk = jax.random.key(seed)
        x = -0.0003713 + 1 * jax.random.normal(jax.random.fold_in(_gk, 1), (6250, 256), jnp.float32)
        src = jax.random.randint(jax.random.fold_in(_gk, 2), (200000,), 0, 6250, jnp.int32)
        dst = jax.random.randint(jax.random.fold_in(_gk, 3), (200000,), 0, 6250, jnp.int32)
        _o = jnp.argsort(dst, stable=True)
        src = src[_o]
        dst = dst[_o]
        return (x, src, dst)
    x, src, dst = _rec_inputs()

    def _L0_gnn_setup():
        import jax, jax.numpy as jnp
        import numpy as np
        N, DEG = (6250, 16)
        E = N * DEG
        IN_DIM, OUT_DIM, HEADS = (256, 64, 4)
        SLOPE = 0.01
        key = jax.random.key(seed)
        k1, k2, k3, k4, k5 = jax.random.split(key, 5)
        h = jax.random.normal(k1, (N, IN_DIM), dtype=jnp.float32)
        W = jax.random.normal(k2, (HEADS, IN_DIM, OUT_DIM), dtype=jnp.float32) * 0.05
        a_src = jax.random.normal(k3, (HEADS, OUT_DIM), dtype=jnp.float32) * 0.05
        a_dst = jax.random.normal(k4, (HEADS, OUT_DIM), dtype=jnp.float32) * 0.05
        src = jax.random.randint(k5, (E,), 0, N, dtype=jnp.int32)
        dst = jnp.repeat(jnp.arange(N, dtype=jnp.int32), DEG)
        return {'h': h, 'W': W, 'a_src': a_src, 'a_dst': a_dst, 'src': src, 'dst': dst}
    _L0_gnn_all = _L0_gnn_setup()
    _L0_gnn_in = {k: v for k, v in _L0_gnn_all.items() if k in ('W', 'a_src', 'a_dst')}
    del _L0_gnn_all

    def _L0_mix_setup():
        import jax, jax.numpy as jnp
        import numpy as np
        HEADS = 8
        DIM_HEAD = 32
        SCALE = DIM_HEAD ** (-0.5)
        EPS = 1e-05

        def _layernorm_gamma(x, gamma):
            mu = jnp.mean(x, axis=-1, keepdims=True)
            var = jnp.var(x, axis=-1, keepdims=True)
            return (x - mu) * jax.lax.rsqrt(var + EPS) * gamma
        key = jax.random.key(seed)
        k1, k2, k3 = jax.random.split(key, 3)
        B, N, D = (8, 2048, 256)
        hidden = HEADS * DIM_HEAD
        x = jax.random.normal(k1, (B, N, D), dtype=jnp.float32)
        Wqkv = jax.random.normal(k2, (D, 3 * hidden), dtype=jnp.float32) * D ** (-0.5)
        Wout = jax.random.normal(k3, (hidden, D), dtype=jnp.float32) * hidden ** (-0.5)
        gamma = jnp.ones((D,), dtype=jnp.float32)
        return {'x': x, 'Wqkv': Wqkv, 'Wout': Wout, 'gamma': gamma}
    _L0_mix_all = _L0_mix_setup()
    _L0_mix_in = {k: v for k, v in _L0_mix_all.items() if k in ('Wqkv', 'Wout', 'gamma')}
    del _L0_mix_all

    def _L0_ffn_setup():
        import jax, jax.numpy as jnp
        import numpy as np
        B, N, D = (16, 512, 256)
        NUM_EXPERTS, TOP_K, HEADS = (4, 2, 4)
        N_EDGES = 131072
        LN_EPS = 1e-05

        def _layernorm(x, g, b):
            mu = x.mean(-1, keepdims=True)
            var = ((x - mu) ** 2).mean(-1, keepdims=True)
            return (x - mu) * jax.lax.rsqrt(var + LN_EPS) * g + b

        def _forward(x, edge_index, W_gat, att_src, att_dst, b_gat, ln_gamma, ln_beta, W1, b1, W2, b2):
            Bc, Nc, Dc = x.shape
            M = Bc * Nc
            x_flat = x.reshape(M, Dc)
            h = (x_flat @ W_gat).reshape(M, HEADS, NUM_EXPERTS)
            loops = jnp.arange(M, dtype=edge_index.dtype)
            src = jnp.concatenate([edge_index[0], loops])
            dst = jnp.concatenate([edge_index[1], loops])
            a_src = (h * att_src).sum(-1)
            a_dst = (h * att_dst).sum(-1)
            e = jax.nn.leaky_relu(a_src[src] + a_dst[dst], negative_slope=0.2)
            e_max = jax.ops.segment_max(e, dst, num_segments=M)
            ee = jnp.exp(e - e_max[dst])
            denom = jax.ops.segment_sum(ee, dst, num_segments=M)
            alpha = ee / (denom[dst] + 1e-16)
            msg = h[src] * alpha[:, :, None]
            agg = jax.ops.segment_sum(msg, dst, num_segments=M).reshape(M, HEADS * NUM_EXPERTS) + b_gat
            scores = _layernorm(agg, ln_gamma, ln_beta).reshape(M, HEADS, NUM_EXPERTS).mean(1)
            scores = scores.reshape(Bc, Nc, NUM_EXPERTS)
            topk_s, topk_i = jax.lax.top_k(scores, TOP_K)
            w = jax.nn.softmax(topk_s, axis=-1)
            out = jnp.zeros_like(x)
            for ei in range(NUM_EXPERTS):
                g = jnp.where(topk_i == ei, w, 0.0).sum(-1)
                hh = jax.nn.gelu(x @ W1[ei] + b1[ei], approximate=False)
                out = out + g[..., None] * (hh @ W2[ei] + b2[ei])
            return out
        key = jax.random.key(seed)
        ks = jax.random.split(key, 8)
        s = 0.05
        return {'x': jax.random.normal(ks[0], (B, N, D), jnp.float32), 'W_gat': jax.random.normal(ks[1], (D, HEADS * NUM_EXPERTS), jnp.float32) * s, 'att_src': jax.random.normal(ks[2], (HEADS, NUM_EXPERTS), jnp.float32) * s, 'att_dst': jax.random.normal(ks[3], (HEADS, NUM_EXPERTS), jnp.float32) * s, 'b_gat': jnp.zeros((HEADS * NUM_EXPERTS,), jnp.float32), 'ln_gamma': jnp.ones((HEADS * NUM_EXPERTS,), jnp.float32), 'ln_beta': jnp.zeros((HEADS * NUM_EXPERTS,), jnp.float32), 'W1': jax.random.normal(ks[4], (NUM_EXPERTS, D, 2 * D), jnp.float32) * s, 'b1': jnp.zeros((NUM_EXPERTS, 2 * D), jnp.float32), 'W2': jax.random.normal(ks[5], (NUM_EXPERTS, 2 * D, D), jnp.float32) * s, 'b2': jnp.zeros((NUM_EXPERTS, D), jnp.float32), 'edge_index': jax.random.randint(ks[6], (2, N_EDGES), 0, B * N, jnp.int32)}
    _L0_ffn_all = _L0_ffn_setup()
    _L0_ffn_in = {k: v for k, v in _L0_ffn_all.items() if k in ('W_gat', 'att_src', 'att_dst', 'b_gat', 'ln_gamma', 'ln_beta', 'W1', 'b1', 'W2', 'b2', 'edge_index')}
    del _L0_ffn_all
    return {'x': x, 'src': src, 'dst': dst, 'L0_gnn_W': _L0_gnn_in['W'], 'L0_gnn_a_src': _L0_gnn_in['a_src'], 'L0_gnn_a_dst': _L0_gnn_in['a_dst'], 'L0_mix_Wqkv': _L0_mix_in['Wqkv'], 'L0_mix_Wout': _L0_mix_in['Wout'], 'L0_mix_gamma': _L0_mix_in['gamma'], 'L0_ffn_W_gat': _L0_ffn_in['W_gat'], 'L0_ffn_att_src': _L0_ffn_in['att_src'], 'L0_ffn_att_dst': _L0_ffn_in['att_dst'], 'L0_ffn_b_gat': _L0_ffn_in['b_gat'], 'L0_ffn_ln_gamma': _L0_ffn_in['ln_gamma'], 'L0_ffn_ln_beta': _L0_ffn_in['ln_beta'], 'L0_ffn_W1': _L0_ffn_in['W1'], 'L0_ffn_b1': _L0_ffn_in['b1'], 'L0_ffn_W2': _L0_ffn_in['W2'], 'L0_ffn_b2': _L0_ffn_in['b2'], 'L0_ffn_edge_index': _L0_ffn_in['edge_index']}

def reference(x, src, dst, L0_gnn_W, L0_gnn_a_src, L0_gnn_a_dst, L0_mix_Wqkv, L0_mix_Wout, L0_mix_gamma, L0_ffn_W_gat, L0_ffn_att_src, L0_ffn_att_dst, L0_ffn_b_gat, L0_ffn_ln_gamma, L0_ffn_ln_beta, L0_ffn_W1, L0_ffn_b1, L0_ffn_W2, L0_ffn_b2, L0_ffn_edge_index):
    import jax
    import jax.numpy as jnp

    def _L0_gnn_ref(h, W, a_src, a_dst, src, dst):
        import jax, jax.numpy as jnp
        import numpy as np
        N, DEG = (6250, 16)
        E = N * DEG
        IN_DIM, OUT_DIM, HEADS = (256, 64, 4)
        SLOPE = 0.01
        z = jnp.einsum('ni,hid->nhd', h, W)
        es = jnp.einsum('nhd,hd->nh', z, a_src)
        ed = jnp.einsum('nhd,hd->nh', z, a_dst)
        e = es[src] + ed[dst]
        e = jnp.where(e >= 0, e, SLOPE * e)
        m = jax.ops.segment_max(e, dst, num_segments=N)
        ex = jnp.exp(e - m[dst])
        denom = jax.ops.segment_sum(ex, dst, num_segments=N)
        alpha = ex / denom[dst]
        msg = alpha[:, :, None] * z[src]
        out = jax.ops.segment_sum(msg, dst, num_segments=N)
        return out.reshape(N, HEADS * OUT_DIM)

    def _L0_mix_ref(x, Wqkv, Wout, gamma):
        import jax, jax.numpy as jnp
        import numpy as np
        HEADS = 8
        DIM_HEAD = 32
        SCALE = DIM_HEAD ** (-0.5)
        EPS = 1e-05

        def _layernorm_gamma(x, gamma):
            mu = jnp.mean(x, axis=-1, keepdims=True)
            var = jnp.var(x, axis=-1, keepdims=True)
            return (x - mu) * jax.lax.rsqrt(var + EPS) * gamma
        B, N, D = x.shape
        qkv = x @ Wqkv
        q, k, v = jnp.split(qkv, 3, axis=-1)

        def to_heads(t):
            return t.reshape(B, N, HEADS, DIM_HEAD).transpose(0, 2, 1, 3)
        q, k, v = map(to_heads, (q, k, v))
        q = jax.nn.softmax(q, axis=-1) * SCALE
        k = jax.nn.softmax(k, axis=2)
        context = jnp.einsum('bhnd,bhne->bhde', k, v)
        out = jnp.einsum('bhde,bhnd->bhne', context, q)
        out = out.transpose(0, 2, 1, 3).reshape(B, N, HEADS * DIM_HEAD)
        out = out @ Wout
        return _layernorm_gamma(out, gamma)

    def _L0_ffn_ref(x, W_gat, att_src, att_dst, b_gat, ln_gamma, ln_beta, W1, b1, W2, b2, edge_index):
        import jax, jax.numpy as jnp
        import numpy as np
        B, N, D = (16, 512, 256)
        NUM_EXPERTS, TOP_K, HEADS = (4, 2, 4)
        N_EDGES = 131072
        LN_EPS = 1e-05

        def _layernorm(x, g, b):
            mu = x.mean(-1, keepdims=True)
            var = ((x - mu) ** 2).mean(-1, keepdims=True)
            return (x - mu) * jax.lax.rsqrt(var + LN_EPS) * g + b

        def _forward(x, edge_index, W_gat, att_src, att_dst, b_gat, ln_gamma, ln_beta, W1, b1, W2, b2):
            Bc, Nc, Dc = x.shape
            M = Bc * Nc
            x_flat = x.reshape(M, Dc)
            h = (x_flat @ W_gat).reshape(M, HEADS, NUM_EXPERTS)
            loops = jnp.arange(M, dtype=edge_index.dtype)
            src = jnp.concatenate([edge_index[0], loops])
            dst = jnp.concatenate([edge_index[1], loops])
            a_src = (h * att_src).sum(-1)
            a_dst = (h * att_dst).sum(-1)
            e = jax.nn.leaky_relu(a_src[src] + a_dst[dst], negative_slope=0.2)
            e_max = jax.ops.segment_max(e, dst, num_segments=M)
            ee = jnp.exp(e - e_max[dst])
            denom = jax.ops.segment_sum(ee, dst, num_segments=M)
            alpha = ee / (denom[dst] + 1e-16)
            msg = h[src] * alpha[:, :, None]
            agg = jax.ops.segment_sum(msg, dst, num_segments=M).reshape(M, HEADS * NUM_EXPERTS) + b_gat
            scores = _layernorm(agg, ln_gamma, ln_beta).reshape(M, HEADS, NUM_EXPERTS).mean(1)
            scores = scores.reshape(Bc, Nc, NUM_EXPERTS)
            topk_s, topk_i = jax.lax.top_k(scores, TOP_K)
            w = jax.nn.softmax(topk_s, axis=-1)
            out = jnp.zeros_like(x)
            for ei in range(NUM_EXPERTS):
                g = jnp.where(topk_i == ei, w, 0.0).sum(-1)
                hh = jax.nn.gelu(x @ W1[ei] + b1[ei], approximate=False)
                out = out + g[..., None] * (hh @ W2[ei] + b2[ei])
            return out
        return _forward(x, edge_index, W_gat, att_src, att_dst, b_gat, ln_gamma, ln_beta, W1, b1, W2, b2)
    xn = _layernorm(x, axis=-1)
    x = x + _L0_gnn_ref(xn, L0_gnn_W, L0_gnn_a_src, L0_gnn_a_dst, src, dst) + _L0_mix_ref(xn[None], L0_mix_Wqkv, L0_mix_Wout, L0_mix_gamma)[0]
    x = x + _L0_ffn_ref(_layernorm(x, axis=-1)[None], L0_ffn_W_gat, L0_ffn_att_src, L0_ffn_att_dst, L0_ffn_b_gat, L0_ffn_ln_gamma, L0_ffn_ln_beta, L0_ffn_W1, L0_ffn_b1, L0_ffn_W2, L0_ffn_b2, L0_ffn_edge_index)[0]
    return x

_drawn_inputs = setup_inputs


def setup_inputs(seed=0):
    import zlib

    import numpy as np

    out = dict(_drawn_inputs(seed))
    spreads = {'L0_mix_gamma': (1.0, 0.2),
     'L0_ffn_b_gat': (0.0, 0.1),
     'L0_ffn_ln_gamma': (1.0, 0.2),
     'L0_ffn_ln_beta': (0.0, 0.1),
     'L0_ffn_b1': (0.0, 0.1),
     'L0_ffn_b2': (0.0, 0.1)}
    factors = {}
    for name, (base, spread) in spreads.items():
        noise = np.random.default_rng([zlib.crc32(name.encode()), seed]).standard_normal(out[name].shape)
        drawn = base * np.exp(spread * noise) if base else spread * noise
        out[name] = jnp.asarray(drawn.astype(out[name].dtype))
    for name, factor in factors.items():
        out[name] = (out[name] * factor).astype(out[name].dtype)
    return out
```

```python
from contextlib import ExitStack, contextmanager

import concourse.bass as bass
from concourse import mybir

ALU = mybir.AluOpType
ACT = mybir.ActivationFunctionType
AX = mybir.AxisListType
F32 = mybir.dt.float32
I32 = mybir.dt.int32
BF16 = mybir.dt.bfloat16

P = 128
N = 6250
D = 256
H = 4
TILES = -(-N // P)
NPAD = TILES * P
LAST = N - (TILES - 1) * P
HIS = -(-NPAD // 256)
E1 = 200000
E2 = 131072
E2S = E2 + N
COLS2 = -(-E2S // P)
PADS2 = COLS2 * P - E2S
OFF_WINDOW = 16000.0
DROP_DST = 8191.0
BIG = 1.0e38
EPS = 1e-5
UNROLL = 16
RING = 8


def stand_apart(engine, sem):
    engine.sem_inc(sem, 1)


class Graph:

    def __init__(self, tag, chunks, slope, width):
        self.tag = tag
        self.chunks = chunks
        self.blocks = -(-(chunks + TILES - 1) // P)
        self.grid = self.blocks * P
        self.steps = -(-(chunks + TILES - 1) // UNROLL) * UNROLL
        self.batches = -(-chunks // 16) * 4
        self.slope = slope
        self.width = width // H
        self.row = width + H
        assert self.steps <= self.grid and self.batches * 4 <= self.grid


class Chain:

    def __init__(self, engine, sem, start=0):
        self.engine, self.sem, self.n = engine, sem, start

    def __call__(self, ins):
        self.n += 1
        ins.then_inc(self.sem, 1)
        self.engine.wait_ge(self.sem, self.n)


def bcast(ap, shape):
    return ap.to_broadcast(shape)


@contextmanager
def stage(nc):
    with ExitStack() as s:
        held = []

        def sem(name):
            held.append(s.enter_context(nc.semaphore(name)))
            return held[-1]

        yield sem
        with nc.Block() as block:
            @block.gpsimd
            def _(pool):
                for q in held:
                    pool.sem_clear(q)


def build_program(nc, x, src, dst, gw, gas, gad, wqkv, wout, gamma, wgat, fas, fad, bgat, lng, lnb,
                  w1, b1, w2, b2, edges, out):
    gnn = Graph("gnn", -(-E1 // P), 0.01, D)
    ffn = Graph("ffn", COLS2, 0.2, 16)
    with ExitStack() as ctx:
        ctx.enter_context(nc.allow_non_contiguous_dma(reason="small tables"))

        def dram(name, shape, dt=F32):
            return nc.dram_tensor(name, shape, dt).ap()

        c = Consts(nc, ctx)
        d = {
            "gnn_pairs": dram("gnn_pairs", [gnn.grid * P, 2]),
            "ffn_pairs": dram("ffn_pairs", [ffn.grid * P, 2]),
            "unsorted": dram("unsorted_pairs", [COLS2 * P, 2]),
            "halfsorted": dram("halfsorted_pairs", [COLS2 * P, 2]),
            "gnn_rows": dram("gnn_rows", [NPAD, gnn.row]),
            "ffn_rows": dram("ffn_rows", [NPAD, ffn.row]),
            "x1": dram("x_after_gnn", [NPAD, D]),
            "xt": dram("xn_transposed", [NPAD, D]),
            "xm": dram("x_plus_mix", [NPAD, D]),
        }
        for g in (gnn, ffn):
            d[g.tag + "_keys"] = dram(g.tag + "_keys", [g.grid, 2 * P], BF16)
            d[g.tag + "_edge_rows"] = dram(g.tag + "_edge_rows", [g.grid, 2 * P])
            d[g.tag + "_weight_rows"] = dram(g.tag + "_weight_rows", [g.grid, H * P])
            d[g.tag + "_ends"] = dram(g.tag + "_ends", [2, g.grid])
            d[g.tag + "_tails"] = dram(g.tag + "_tails", [2, H, g.grid])
            d[g.tag + "_carries"] = dram(g.tag + "_carries", [2, H, g.grid])
            d[g.tag + "_windows"] = dram(g.tag + "_windows", [g.grid], I32)
        with stage(nc) as sem:
            constants(nc, c, sem)
            list_edges(nc, sem, d, src, dst, edges, gnn, ffn)
            sort_pass(nc, c, sem, "lo", d["unsorted"], d["halfsorted"], COLS2 * P)
        with stage(nc) as sem:
            sort_pass(nc, c, sem, "hi", d["halfsorted"], d["ffn_pairs"], ffn.grid * P)
        with stage(nc) as sem:
            nodes_in(nc, c, sem, d, x, gw, gas, gad, wqkv, wout, gamma)
        with stage(nc) as sem, ExitStack() as kept:
            e = edge_tables(nc, kept, c, sem, d, gnn)
            edge_weights(nc, c, sem, d, gnn)
            acc = aggregate(nc, kept, c, sem, d, gnn, e)
            nodes_between(nc, c, sem, d, acc, wgat, fas, fad)
        gate = ctx.enter_context(nc.sbuf_tensor("gate_of_expert", [P, TILES, 4], F32))
        with stage(nc) as sem, ExitStack() as kept:
            e = edge_tables(nc, kept, c, sem, d, ffn)
            edge_weights(nc, c, sem, d, ffn)
            acc = aggregate(nc, kept, c, sem, d, ffn, e)
            gates(nc, c, sem, acc, gate, bgat, lng, lnb)
        with stage(nc) as sem:
            experts(nc, c, sem, d, out, gate, w1, b1, w2, b2)


class Consts:

    def __init__(self, nc, ctx):
        def sb(name, shape, dt=F32):
            return ctx.enter_context(nc.sbuf_tensor(name, shape, dt))

        self.row_i = sb("iota_row_i", [P, P], I32)
        self.col_i = sb("iota_col_i", [P, 1], I32)
        self.row = sb("iota_row", [P, P])
        self.lo = sb("iota_lo", [P, 2])
        self.ident = sb("identity", [P, P])
        self.ones = sb("ones", [P, P])
        self.before = sb("before", [P, P])
        self.blocks32 = sb("blocks32", [P, P])
        self.zeros = sb("zeros", [P, COLS2])
        self.eps = sb("eps", [P, 1])
        self.spread = sb("x1_mean_and_inverse_root_of_variance", [P, TILES, 2])
        self.pool_dma_before = 0
        self.pool_fetch_before = [0, 0, 0]
        self.pool_dma = [ctx.enter_context(nc.semaphore("pool_dma%d" % u)) for u in range(UNROLL)]
        self.pool_fetch = [ctx.enter_context(nc.semaphore("pool_fetch%d" % u)) for u in range(3)]
        self.scores = sb("scores_bf16", [P, 3, 2, 2, HIS, H], BF16)
        self.score = sb("scores_f32", [P, 2, HIS, 2, H])


def constants(nc, c, sem):
    made_iota, cs = sem("made_iota"), sem("const_step")
    with nc.sbuf_tensor("shifted_row", [P, P], I32) as shr, nc.sbuf_tensor("shifted_col", [P, 1], I32) as shc, \
            nc.sbuf_tensor("shifted_row_f", [P, P], F32) as shrf, nc.sbuf_tensor("shifted_col_f", [P, 1], F32) as shcf, \
            nc.Block() as block:
        @block.gpsimd
        def _(pool):
            pool.iota(c.row_i[:], [[1, P]], 0, 0).then_inc(made_iota, 1)
            pool.iota(c.col_i[:], [[0, 1]], 0, 1).then_inc(made_iota, 1)

        @block.vector
        def _(dve):
            link = Chain(dve, cs)
            link(dve.memset(c.ones[:], 1.0))
            link(dve.memset(c.zeros[:], 0.0))
            link(dve.memset(c.eps[:], EPS))
            dve.wait_ge(made_iota, 2)
            link(dve.tensor_copy(c.row[:], c.row_i[:]))
            link(dve.tensor_copy(c.lo[:, 0:1], c.col_i[:]))
            link(dve.tensor_scalar(c.lo[:, 1:2], c.lo[:, 0:1], 128.0, None, ALU.add))
            link(dve.tensor_scalar(c.ident[:], c.row[:], c.lo[:, 0:1], None, ALU.is_equal))
            link(dve.tensor_scalar(c.before[:], c.row[:], c.lo[:, 0:1], None, ALU.is_gt))
            link(dve.tensor_scalar(shr[:], c.row_i[:], 5, None, ALU.arith_shift_right))
            link(dve.tensor_scalar(shc[:], c.col_i[:], 5, None, ALU.arith_shift_right))
            link(dve.tensor_copy(shrf[:], shr[:]))
            link(dve.tensor_copy(shcf[:], shc[:]))
            link(dve.tensor_scalar(c.blocks32[:], shrf[:], shcf[:, 0:1], None, ALU.is_equal))
            link(dve.memset(c.score[:], 0.0))


def list_edges(nc, sem, d, src, dst, edges, gnn, ffn):
    loaded = [sem("edges_loaded%d" % i) for i in range(4)]
    paired, stored = sem("edges_paired"), sem("pairs_stored")
    R1 = 125
    T1 = E1 // R1
    T2 = E2 // P
    RS = 125
    TS = N // RS
    with ExitStack() as s:
        def sb(name, shape, dt=F32):
            return s.enter_context(nc.sbuf_tensor(name, shape, dt))

        i1 = sb("gnn_edges_i", [R1, 2, T1], I32)
        p1 = sb("gnn_edges_p", [R1, T1, 2])
        i2 = sb("ffn_edges_i", [P, 2, T2], I32)
        p2 = sb("ffn_edges_p", [P, T2, 2])
        si = sb("self_i", [RS, TS], I32)
        sp_ = sb("self_p", [RS, TS, 2])
        pad = sb("pad_pairs", [P, P, 2])
        drop = sb("drop_pairs", [P, 2])
        made = sem("self_iota")
        block = s.enter_context(nc.Block())

        @block.gpsimd
        def _(pool):
            pool.iota(si[:], [[1, TS]], 0, TS).then_inc(made, 1)

        @block.vector
        def _(dve):
            link = Chain(dve, paired)
            link(dve.memset(pad[:, :, 0], 0.0))
            link(dve.memset(pad[:, :, 1], OFF_WINDOW))
            link(dve.memset(drop[:, 0:1], 0.0))
            link(dve.memset(drop[:, 1:2], DROP_DST))
            dve.wait_ge(made, 1)
            link(dve.tensor_copy(sp_[:, :, 0], si[:]))
            link(dve.tensor_copy(sp_[:, :, 1], si[:]))
            for k in range(2):
                dve.wait_ge(loaded[2 + k], 16)
                link(dve.tensor_copy(p2[:, :, k], i2[:, k, :]))
            for k in range(2):
                dve.wait_ge(loaded[k], 16)
                link(dve.tensor_copy(p1[:, :, k], i1[:, k, :]))

        @block.sync
        def _(sp):
            for k in range(2):
                sp.dma_start(i2[:, k, :], edges[k].rearrange("(p t) -> p t", p=P)).then_inc(loaded[2 + k], 16)
            for k, a in enumerate((src, dst)):
                sp.dma_start(i1[:, k, :], a.rearrange("(p t) -> p t", p=R1)).then_inc(loaded[k], 16)
            sp.wait_ge(paired, 6)
            n = 0
            sp.dma_start(d["unsorted"][E2:E2 + N, :].rearrange("(p t) k -> p t k", p=RS), sp_[:]).then_inc(stored, 16)
            sp.dma_start(d["unsorted"][E2S:E2S + PADS2, :], drop[0:PADS2, :]).then_inc(stored, 16)
            rest = gnn.grid * P - E1
            rows = next(r for r in range(P, 0, -1) if rest % r == 0 and rest // r <= P)
            sp.dma_start(d["gnn_pairs"][E1:, :].rearrange("(p t) k -> p t k", p=rows),
                         pad[0:rows, 0:rest // rows, :]).then_inc(stored, 16)
            n += 3
            for b in range(ffn.blocks):
                sp.dma_start(d["ffn_pairs"][b * P * P:(b + 1) * P * P, :].rearrange("(p t) k -> p t k", p=P),
                             pad[:]).then_inc(stored, 16)
                n += 1
            sp.wait_ge(paired, 8)
            sp.dma_start(d["unsorted"][0:E2, :].rearrange("(p t) k -> p t k", p=P), p2[:]).then_inc(stored, 16)
            sp.wait_ge(paired, 10)
            sp.dma_start(d["gnn_pairs"][0:E1, :].rearrange("(p t) k -> p t k", p=R1), p1[:]).then_inc(stored, 16)
            sp.wait_ge(stored, 16 * (n + 2))


def sort_pass(nc, c, sem, digit, pairs_in, pairs_out, room):
    T = COLS2
    TP = -(-T // UNROLL) * UNROLL
    nb = P if digit == "lo" else TILES
    loaded, step = sem(digit + "_loaded"), sem(digit + "_step")
    summed = sem(digit + "_summed")
    places_ready = sem(digit + "_places_ready")
    staged, apart, pool_apart = (sem(digit + n) for n in ("_staged", "_wait_apart", "_pool_wait_apart"))
    scattered, before = c.pool_dma, c.pool_dma_before
    c.pool_dma_before += 16 * (-(-COLS2 // UNROLL))
    with ExitStack() as s:
        def sb(name, shape, dt=F32):
            return s.enter_context(nc.sbuf_tensor(digit + name, shape, dt))

        pr = sb("_pairs", [P, TP, 2])
        ki = sb("_key_i", [P, T], I32)
        key = sb("_key", [P, T])
        is_digit = sb("_is_digit", [P, 2, T])
        rank = sb("_rank", [P, 2, T])
        place = sb("_place", [P, TP])
        cnt = sb("_count", [P, P])
        tot = sb("_total", [P, P])
        base = sb("_base", [P, P])
        slot_i = sb("_slot_index", [P, UNROLL], I32)
        slot_p = sb("_slot_pair", [P, UNROLL, 2])
        ps = s.enter_context(nc.psum_tensor(digit + "_sums", [P, 2, 512], F32))
        block = s.enter_context(nc.Block())

        @block.sync
        def _(sp):
            sp.dma_start(pr[:, 0:T, :], pairs_in.rearrange("(p t) k -> p t k", p=P)).then_inc(loaded, 16)

        @block.vector
        def _(dve):
            link = Chain(dve, step)
            link(dve.memset(pr[:, T:TP, :], 0.0))
            link(dve.memset(place[:], 1.0e6))
            dve.wait_ge(loaded, 16)
            link(dve.tensor_copy(ki[:], pr[:, 0:T, 1]))
            if digit == "lo":
                link(dve.tensor_scalar(ki[:], ki[:], P - 1, None, ALU.bitwise_and))
            else:
                link(dve.tensor_scalar(ki[:], ki[:], 7, None, ALU.arith_shift_right))
            link(dve.tensor_copy(key[:], ki[:]))
            n = link.n
            with dve.Fori(0, nb) as b:
                dve.tensor_scalar(is_digit[:, 0, :], key[:], c.row[:, bass.ds(b, 1)], 0.0, ALU.is_equal,
                                  ALU.add, accum_out=cnt[:, bass.ds(b, 1)]).then_inc(step, 1)
                dve.wait_ge(step, b + (n + 1))
            link.n = n + nb
            dve.wait_ge(summed, 1)
            link(dve.tensor_copy(tot[:, 0:nb], ps[:, 0, 0:nb]))
            link(dve.tensor_tensor_scan(base[:, 0:nb], tot[:, 0:nb], c.zeros[:, 0:nb], -1.0, ALU.add, ALU.add))
            link(dve.tensor_tensor(base[:, 0:nb], base[:, 0:nb], tot[:, 0:nb], ALU.subtract))
            link(dve.tensor_tensor(base[:, 0:nb], base[:, 0:nb], ps[:, 1, 0:nb], ALU.add))
            n = link.n
            with dve.Fori(0, nb) as b:
                dve.tensor_scalar(is_digit[:, 1, :], key[:], c.row[:, bass.ds(b, 1)], None,
                                  ALU.is_equal).then_inc(step, 1)
                dve.wait_ge(step, b * 3 + (n + 1))
                dve.tensor_tensor_scan(rank[:, 0, :], is_digit[:, 1, :], c.zeros[:, 0:T], base[:, bass.ds(b, 1)],
                                       ALU.add, ALU.add).then_inc(step, 1)
                dve.wait_ge(step, b * 3 + (n + 2))
                stand_apart(dve, apart)
                dve.copy_predicated(place[:, 0:T], is_digit[:, 1, :].bitcast(I32), rank[:, 0, :]).then_inc(step, 1)
                dve.wait_ge(step, b * 3 + (n + 3))
            link.n = n + 3 * nb
            dve.sem_inc(places_ready, 1)

        @block.tensor
        def _(pe):
            pe.wait_ge(step, 5 + nb)
            pe.matmul(ps[:, 0, 0:nb], c.ones[:], cnt[:, 0:nb], start=True, stop=True)
            pe.matmul(ps[:, 1, 0:nb], c.before[:], cnt[:, 0:nb], start=True, stop=True).then_inc(summed, 1)

        @block.scalar
        def _(act):
            act.wait_ge(places_ready, 1)

            def stage(i, first):
                for half in range(2):
                    lo, hi = half * RING, (half + 1) * RING
                    if not first:
                        for u in range(lo, hi):
                            act.wait_ge(scattered[u], i * 16 + before)
                    act.copy(slot_i[:, lo:hi], place[:, bass.ds(i * UNROLL + lo, RING)]).then_inc(staged, 1)
                    act.copy(slot_p[:, lo:hi, :], pr[:, bass.ds(i * UNROLL + lo, RING), :]).then_inc(staged, 1)

            stage(0, True)
            with act.Fori(1, TP // UNROLL) as i:
                stage(i, False)

        @block.gpsimd
        def _(pool):
            def scatter(i, first):
                for u in range(UNROLL):
                    if u % RING == 0:
                        pool.wait_ge(staged, i * 4 + 2 * (u // RING) + 2)
                        stand_apart(pool, pool_apart)
                    pool.indirect_dma_start(
                        out=pairs_out, out_offset=bass.IndirectOffsetOnAxis(ap=slot_i[:, u:u + 1], axis=0),
                        in_=slot_p[:, u, :], in_offset=None, bounds_check=room - 1,
                        oob_is_err=False).then_inc(scattered[u], 16)

            scatter(0, True)
            with pool.Fori(1, TP // UNROLL) as i:
                scatter(i, False)
            for u in range(UNROLL):
                pool.wait_ge(scattered[u], 16 * (TP // UNROLL) + before)


def transposes(nc, pe, act, jobs, ps, given, taken, ident):
    banks = ps.shape[1]
    if pe is not None:
        for j, (ins, _, _) in enumerate(jobs):
            if j >= banks:
                pe.wait_ge(taken, j - banks + 1)
            for q, a in enumerate(ins):
                w = a.free_size()
                last = pe.transpose(ps[0:w, j % banks, q * P:(q + 1) * P], a, ident)
            last.then_inc(given, 1)
    if act is not None:
        for j, (_, o, view) in enumerate(jobs):
            act.wait_ge(given, j + 1)
            act.copy(o, view(ps[:, j % banks, :])).then_inc(taken, 1)


def measure(nc, link, stats, mv, rows, measured, apart, i):
    if not (isinstance(i, int) and i == 0):
        nc.vector.wait_ge(measured, i)
    link(nc.vector.bn_stats(stats, rows))
    stand_apart(nc.vector, apart)
    nc.vector.bn_aggr(mv, stats).then_inc(measured, 1)


def spreads(c, engine, measured, rooted, ring):
    def root(i, n):
        engine.wait_ge(measured, i + 1)
        v = ring[:, n, 1:2]
        engine.activation(v, v, ACT.Sqrt, bias=c.eps[:, 0:1]).then_inc(rooted, 1)
    return root


def tile_loop(engine, body):
    body(0)
    with engine.Fori(1, TILES - 1) as i:
        body(i)
    body(TILES - 1)


def nodes_in(nc, c, sem, d, x, gw, gas, gad, wqkv, wout, gamma):
    with ExitStack() as s:
        def sb(name, shape, dt=F32):
            return s.enter_context(nc.sbuf_tensor("in_" + name, shape, dt))

        X = sb("x", [P, TILES, D])
        XT = sb("xn_transposed", [P, 2, 2, P])
        WZ = sb("w_graph", [P, 2, D + 2 * H])
        WQ = sb("w_qkv", [P, 2, 3 * D])
        WO = sb("w_out", [P, 2, D])
        GA = sb("gamma", [P, D])
        AS = sb("att", [P, 2, D])
        PROD = sb("att_products", [P, D])
        KM = sb("k_max", [P, D])
        KMT = sb("k_max_column", [P, 2])
        KD = sb("k_max_diagonal", [P, 2, P])
        KB = sb("k_max_everywhere", [P, D])
        CT = sb("context_masked", [P, 2, P])
        CW = sb("context_out", [P, 2, D])
        SUMS = sb("k_sums", [P, 2])

        loaded = [sem("node_loaded%d" % i) for i in range(3)]
        cleared, step = sem("x_cleared"), sem("project_step")
        ahead, turned, copied = sem("xn_ready"), sem("xn_turned"), sem("xn_copied")
        measured, rooted, inverted, apart = (sem("x_" + n) for n in ("measured", "rooted", "inverted", "wait_apart"))
        projected, taken_z, taken_k = sem("projected"), sem("z_taken"), sem("k_taken")
        stored = [sem("z_stored0"), sem("z_stored1")]
        xt_stored = [sem("xt_stored0"), sem("xt_stored1")]

        def rows(ap, i):
            return ap.rearrange("(w i) d -> w i d", i=P)[bass.ds(i, 1)].rearrange("w i d -> (w i) d")

        def load_turned(sp, used, arrived):
            def load(i, n, first):
                if not first:
                    sp.wait_ge(used, i - 1)
                sp.dma_start(XT[:, n].rearrange("p k i -> p (k i)"), rows(d["xt"], i)).then_inc(arrived[n], 16)
            return load
        with ExitStack() as s2:
            XN = s2.enter_context(nc.sbuf_tensor("in_xn", [P, 2, D], F32))
            ST = s2.enter_context(nc.sbuf_tensor("in_stats", [P, 6], F32))
            MV = s2.enter_context(nc.sbuf_tensor("in_mean_var", [P, 2, 2], F32))
            ZO = s2.enter_context(nc.sbuf_tensor("in_z_out", [P, 2, H, D // H + 1], F32))
            PT = s2.enter_context(nc.psum_tensor("ps_in_turn", [P, 2, 512], F32))
            PZ = s2.enter_context(nc.psum_tensor("ps_in_z", [P, 2, 512], F32))
            PK = s2.enter_context(nc.psum_tensor("ps_in_k", [P, 2, 512], F32))
            block = s2.enter_context(nc.Block())

            @block.sync
            def _(sp):
                sp.wait_ge(cleared, 1)
                full = TILES - 1
                sp.dma_start(X[:, 0:full, :], x[0:full * P, :].rearrange("(w i) d -> i w d", i=P)).then_inc(loaded[0], 16)
                sp.dma_start(X[0:LAST, full, :], x[full * P:N, :]).then_inc(loaded[1], 16)
                for k in range(2):
                    sp.dma_start(WZ[:, k, 0:D].rearrange("i (h d) -> i h d", h=H),
                                 gw[:, k * P:(k + 1) * P, :].rearrange("h i d -> i h d")).then_inc(loaded[2], 16)
                sp.dma_start(WQ[:], wqkv.rearrange("(k i) d -> i k d", k=2)).then_inc(loaded[2], 16)
                sp.dma_start(WO[:], wout.rearrange("(k i) d -> i k d", k=2)).then_inc(loaded[2], 16)
                sp.dma_start(GA[:], gamma.partition_broadcast(P)).then_inc(loaded[2], 16)
                sp.dma_start(AS[:, 0, :], gas.rearrange("h d -> (h d)").partition_broadcast(P)).then_inc(loaded[2], 16)
                sp.dma_start(AS[:, 1, :], gad.rearrange("h d -> (h d)").partition_broadcast(P)).then_inc(loaded[2], 16)

                def store(i, n):
                    sp.wait_ge(copied, i + 1)
                    sp.dma_start(rows(d["xt"], i), XT[:, n].rearrange("p k i -> p (k i)")).then_inc(xt_stored[n], 16)
                    sp.wait_ge(taken_z, i + 1)
                    sp.dma_start(d["gnn_rows"].rearrange("(w i) d -> w i d", i=P)[bass.ds(i, 1)].rearrange("w i d -> (w i) d"),
                                 ZO[:, n, :, :].rearrange("p h f -> p (h f)")).then_inc(stored[n], 16)

                with sp.Fori(0, TILES // 2) as i:
                    store(i * 2, 0)
                    store(i * 2 + 1, 1)
                store(TILES - 1, 0)
                for q in (stored, xt_stored):
                    sp.wait_ge(q[0], 16 * (TILES // 2 + 1))
                    sp.wait_ge(q[1], 16 * (TILES // 2))

            @block.vector
            def _(dve):
                link = Chain(dve, step)
                dve.memset(X[:, TILES - 1, :], 0.0).then_inc(cleared, 1)
                link(dve.memset(KM[:], -3.0e38))
                link(dve.memset(ZO[:], 1.0))
                dve.wait_ge(loaded[2], 16 * 7)
                for k in range(2):
                    for a in range(2):
                        link(dve.tensor_tensor(PROD[:], WZ[:, k, 0:D], AS[:, a, :], ALU.mult))
                        link(dve.tensor_reduce(WZ[:, k, D + H * a:D + H * (a + 1)],
                                               PROD[:].rearrange("p (h d) -> p h d", h=H), AX.X, ALU.add))
                dve.wait_ge(loaded[0], 16)
                dve.wait_ge(loaded[1], 16)
                base = link.n

                def row_of(i):
                    return X[:, bass.ds(i, 1), :].rearrange("p w d -> p (w d)")

                def stats(i, n):
                    link.n = i + base
                    if not (isinstance(i, int) and i < 2):
                        dve.wait_ge(ahead, i - 1)
                    measure(nc, link, ST[:], MV[:, n, :], row_of(i), measured, apart, i)

                def norm(i, n):
                    if not (isinstance(i, int) and i == TILES - 1):
                        stats(i + 1, 1 - n)
                    mv = MV[:, n, :]
                    dve.wait_ge(rooted, i + 1)
                    dve.reciprocal(mv[:, 1:2], mv[:, 1:2]).then_inc(inverted, 1)
                    dve.wait_ge(inverted, i + 1)
                    if not (isinstance(i, int) and i < 2):
                        dve.wait_ge(turned, i - 1)
                    dve.tensor_scalar(XN[:, n, :], row_of(i), mv[:, 0:1], mv[:, 1:2], ALU.subtract, ALU.mult).then_inc(ahead, 1)

                def take(i, n):
                    dve.wait_ge(projected, i + 1)
                    w = bass.ds(i, 1)
                    rows = LAST if isinstance(i, int) and i == TILES - 1 else P
                    out_ = c.score[:].rearrange("p a hi par h -> p a (hi par) h")[:, :, w, :].rearrange("p a w h -> p a (w h)")
                    dve.tensor_copy(out_, PK[:, n, D:D + 2 * H].rearrange("p (a h) -> p a h", a=2)).then_inc(taken_k, 1)
                    dve.tensor_tensor(KM[0:rows, :], KM[0:rows, :], PK[0:rows, n, 0:D], ALU.max).then_inc(taken_k, 1)
                    dve.wait_ge(taken_k, i * 2 + 2)

                stats(0, 0)
                norm(0, 0)
                norm(1, 1)
                take(0, 0)
                with dve.Fori(1, TILES // 2) as j:
                    norm(j * 2, 0)
                    take(j * 2 - 1, 1)
                    norm(j * 2 + 1, 1)
                    take(j * 2, 0)
                norm(TILES - 1, 0)
                take(TILES - 2, 1)
                take(TILES - 1, 0)
                link.n = base + TILES
                for a in range(2):
                    rest = PROD[:, 0:HIS * H].rearrange("p (hi h) -> p hi h", h=H)
                    for par in range(2):
                        full = c.score[:, a, :, par, :]
                        link(dve.tensor_copy(rest, full))
                        for k in range(3):
                            link(dve.tensor_copy(c.scores[:, k, a, par, :, :], rest))
                            if k < 2:
                                link(dve.tensor_tensor(rest, rest, c.scores[:, k, a, par, :, :], ALU.subtract))

            @block.tensor
            def _(pe):
                pe.wait_ge(step, 10)

                def turn(i, n):
                    pe.wait_ge(ahead, i + 1)
                    if not (isinstance(i, int) and i < 2):
                        pe.wait_ge(copied, i - 1)
                    for k in range(2):
                        last = pe.transpose(PT[:, n, k * P:(k + 1) * P], XN[:, n, k * P:(k + 1) * P], c.ident[:])
                    last.then_inc(turned, 1)

                def project(i, n):
                    pe.wait_ge(copied, i + 1)
                    if not (isinstance(i, int) and i < 2):
                        pe.wait_ge(taken_z, i - 1)
                        pe.wait_ge(taken_k, i * 2 - 2)
                    for k in range(2):
                        cols = XT[:, n, k, :]
                        pe.matmul(PZ[:, n, 0:D], cols, WZ[:, k, 0:D], start=k == 0, stop=k == 1)
                    for k in range(2):
                        cols = XT[:, n, k, :]
                        pe.matmul(PK[:, n, 0:D], cols, WQ[:, k, D:2 * D], start=k == 0, stop=k == 1)
                    for k in range(2):
                        cols = XT[:, n, k, :]
                        last = pe.matmul(PK[:, n, D:D + 2 * H], cols, WZ[:, k, D:D + 2 * H], start=k == 0, stop=k == 1)
                    last.then_inc(projected, 1)

                turn(0, 0)
                turn(1, 1)
                project(0, 0)
                with pe.Fori(1, TILES // 2) as j:
                    turn(j * 2, 0)
                    project(j * 2 - 1, 1)
                    turn(j * 2 + 1, 1)
                    project(j * 2, 0)
                turn(TILES - 1, 0)
                project(TILES - 2, 1)
                project(TILES - 1, 0)

            @block.scalar
            def _(act):
                def copy(i, n):
                    act.wait_ge(turned, i + 1)
                    if not (isinstance(i, int) and i < 2):
                        act.wait_ge(projected, i - 1)
                        act.wait_ge(xt_stored[n], x_count(i, n))
                    act.copy(XT[:, n, :, :], PT[:, n, 0:D].rearrange("p (k i) -> p k i", k=2)).then_inc(copied, 1)

                def take(i, n):
                    act.wait_ge(projected, i + 1)
                    if not (isinstance(i, int) and i < 2):
                        act.wait_ge(stored[n], i // 2 * 16 if isinstance(i, int) else (i - n) * 8)
                    act.copy(ZO[:, n, :, 0:D // H], PZ[:, n, 0:D].rearrange("p (h f) -> p h f", h=H)).then_inc(taken_z, 1)

                root = spreads(c, act, measured, rooted, MV)
                for i in range(2):
                    root(i, i)
                copy(0, 0)
                root(2, 0)
                copy(1, 1)
                root(3, 1)
                take(0, 0)
                copy(2, 0)
                root(4, 0)
                take(1, 1)
                copy(3, 1)
                root(5, 1)
                take(2, 0)
                with act.Fori(2, TILES // 2 - 1) as j:
                    copy(j * 2, 0)
                    root(j * 2 + 2, 0)
                    act.wait_ge(projected, j * 2)
                    act.wait_ge(stored[1], j * 16 - 16)
                    act.copy(ZO[:, 1, :, 0:D // H], PZ[:, 1, 0:D].rearrange("p (h f) -> p h f", h=H)).then_inc(taken_z, 1)
                    copy(j * 2 + 1, 1)
                    root(j * 2 + 3, 1)
                    act.wait_ge(projected, j * 2 + 1)
                    act.wait_ge(stored[0], j * 16)
                    act.copy(ZO[:, 0, :, 0:D // H], PZ[:, 0, 0:D].rearrange("p (h f) -> p h f", h=H)).then_inc(taken_z, 1)
                copy(TILES - 3, 0)
                root(TILES - 1, 0)
                take(TILES - 4, 1)
                copy(TILES - 2, 1)
                take(TILES - 3, 0)
                copy(TILES - 1, 0)
                take(TILES - 2, 1)
                take(TILES - 1, 0)

        cs, spread = sem("context_step"), sem("k_max_spread")
        xt_in = [sem("ctx_xt_in0"), sem("ctx_xt_in1")]
        kv, shifted, expd, v_copied, summed = (sem("ctx_" + n) for n in ("kv", "shifted", "exp", "v", "summed"))
        with ExitStack() as s2:
            KS = s2.enter_context(nc.sbuf_tensor("in_k_shifted", [P, 2, D], F32))
            KE = s2.enter_context(nc.sbuf_tensor("in_k_exp", [P, 2, D], F32))
            V = s2.enter_context(nc.sbuf_tensor("in_v", [P, 2, D], F32))
            PX = s2.enter_context(nc.psum_tensor("ps_in_k2", [P, 2, 512], F32))
            PV = s2.enter_context(nc.psum_tensor("ps_in_v", [P, 2, 512], F32))
            PC = s2.enter_context(nc.psum_tensor("ps_in_context", [P, 2, 512], F32))
            PS = s2.enter_context(nc.psum_tensor("ps_in_k_sum", [P, 2, 512], F32))
            PM = PC[:, 0, :]
            block = s2.enter_context(nc.Block())

            @block.sync
            def _(sp):
                load = load_turned(sp, kv, xt_in)
                load(0, 0, True)
                load(1, 1, True)
                with sp.Fori(1, TILES // 2) as j:
                    load(j * 2, 0, False)
                    load(j * 2 + 1, 1, False)
                load(TILES - 1, 0, False)

            @block.tensor
            def _(pe):
                for k in range(2):
                    last = pe.transpose(PM[:, k * P:(k + 1) * P], KM[:, k * P:(k + 1) * P], c.ident[:])
                last.then_inc(spread, 1)
                pe.wait_ge(cs, 3)
                for k in range(2):
                    last = pe.matmul(PM[:, k * P:(k + 1) * P], c.ones[:], KD[:, k, :], start=True, stop=True)
                last.then_inc(spread, 1)

                def project(i, n):
                    if not (isinstance(i, int) and i < 2):
                        pe.wait_ge(shifted, i - 1)
                        pe.wait_ge(v_copied, i - 1)
                    pe.wait_ge(xt_in[n], x_count(i, n) + 16)
                    for k in range(2):
                        pe.matmul(PX[:, n, 0:D], XT[:, n, k, :], WQ[:, k, D:2 * D], start=k == 0, stop=k == 1)
                    for k in range(2):
                        last = pe.matmul(PV[:, n, 0:D], XT[:, n, k, :], WQ[:, k, 2 * D:3 * D], start=k == 0, stop=k == 1)
                    last.then_inc(kv, 1)

                def sum_up(i, n):
                    rows = LAST if isinstance(i, int) and i == TILES - 1 else P
                    pe.wait_ge(expd, i + 1)
                    pe.wait_ge(v_copied, i + 1)
                    first = isinstance(i, int) and i == 0
                    end = isinstance(i, int) and i == TILES - 1
                    for k in range(2):
                        cut = slice(k * P, (k + 1) * P)
                        pe.matmul(PC[:, k, 0:P], V[0:rows, n, cut], KE[0:rows, n, cut], start=first, stop=end,
                                  skip_group_check=True)
                        last = pe.matmul(PS[:, k, 0:1], KE[0:rows, n, cut], c.ones[0:rows, 0:1], start=first, stop=end,
                                         skip_group_check=True)
                    last.then_inc(summed, 1)

                project(0, 0)
                project(1, 1)
                sum_up(0, 0)
                with pe.Fori(1, TILES // 2) as j:
                    project(j * 2, 0)
                    sum_up(j * 2 - 1, 1)
                    project(j * 2 + 1, 1)
                    sum_up(j * 2, 0)
                project(TILES - 1, 0)
                sum_up(TILES - 2, 1)
                sum_up(TILES - 1, 0)
                pe.wait_ge(cs, 6)
                for k in range(2):
                    last = pe.matmul(PX[:, k, 0:D], CT[:, k, :], WO[:, k, :], start=True, stop=True)
                last.then_inc(spread, 1)

            @block.vector
            def _(dve):
                link = Chain(dve, cs)
                dve.wait_ge(spread, 1)
                link(dve.tensor_reduce(KMT[:], PM[:, 0:D].rearrange("p (k n) -> p k n", k=2), AX.X, ALU.max))
                for k in range(2):
                    link(dve.tensor_scalar(KD[:, k, :], c.ident[:], KMT[:, k:k + 1], None, ALU.mult))
                dve.wait_ge(spread, 2)
                link(dve.tensor_copy(KB[:], PM[:, 0:D]))

                def shift(i, n):
                    dve.wait_ge(kv, i + 1)
                    if not (isinstance(i, int) and i < 2):
                        dve.wait_ge(expd, i - 1)
                    dve.tensor_tensor(KS[:, n, :], PX[:, n, 0:D], KB[:], ALU.subtract).then_inc(shifted, 1)

                shift(0, 0)
                shift(1, 1)
                with dve.Fori(1, TILES // 2) as j:
                    shift(j * 2, 0)
                    shift(j * 2 + 1, 1)
                shift(TILES - 1, 0)
                dve.wait_ge(summed, TILES)
                for k in range(2):
                    link(dve.tensor_tensor(CT[:, k, :], PC[:, k, 0:P], c.blocks32[:], ALU.mult))
                for k in range(2):
                    link(dve.reciprocal(SUMS[:, k:k + 1], PS[:, k, 0:1]))
                dve.wait_ge(spread, 3)
                for k in range(2):
                    link(dve.tensor_scalar(CW[:, k, :], PX[:, k, 0:D], SUMS[:, k:k + 1], 32 ** -0.5, ALU.mult, ALU.mult))

            @block.scalar
            def _(act):
                def go(i, n):
                    act.wait_ge(kv, i + 1)
                    if not (isinstance(i, int) and i < 2):
                        act.wait_ge(summed, i - 1)
                    act.copy(V[:, n, :], PV[:, n, 0:D]).then_inc(v_copied, 1)
                    act.wait_ge(shifted, i + 1)
                    act.activation(KE[:, n, :], KS[:, n, :], ACT.Exp).then_inc(expd, 1)

                go(0, 0)
                go(1, 1)
                with act.Fori(1, TILES // 2) as j:
                    go(j * 2, 0)
                    go(j * 2 + 1, 1)
                go(TILES - 1, 0)

        ms = sem("mix_step")
        qt_in = [sem("mix_xt_in0"), sem("mix_xt_in1")]
        q_made, q_shift, q_exp, q_norm, q_turn, q_copied, mixed, mix_out = (
            sem("q_" + n) for n in ("made", "shift", "exp", "norm", "turn", "copied", "mixed", "out"))
        mix_stored = [sem("mix_stored0"), sem("mix_stored1")]
        mix_measured, logged, mix_rooted, mix_apart = (
            sem("mix_" + n) for n in ("measured", "logged", "rooted", "wait_apart"))
        with ExitStack() as s2:
            QM = s2.enter_context(nc.sbuf_tensor("in_q_max", [P, 8], F32))
            QE = s2.enter_context(nc.sbuf_tensor("in_q", [P, 2, D], F32))
            QT = s2.enter_context(nc.sbuf_tensor("in_q_turned", [P, 2, D], F32))
            ST = s2.enter_context(nc.sbuf_tensor("in_mstats", [P, 6], F32))
            MV = s2.enter_context(nc.sbuf_tensor("in_mmean_var", [P, 2], F32))
            MO = s2.enter_context(nc.sbuf_tensor("in_mix_out", [P, 2, D], F32))
            PQ = s2.enter_context(nc.psum_tensor("ps_in_q_ps", [P, 2, 512], F32))
            PT = s2.enter_context(nc.psum_tensor("ps_in_qt_ps", [P, 2, 512], F32))
            PM = s2.enter_context(nc.psum_tensor("ps_in_mix_ps", [P, 2, 512], F32))
            block = s2.enter_context(nc.Block())

            @block.tensor
            def _(pe):
                def query(i, n):
                    if not (isinstance(i, int) and i < 2):
                        pe.wait_ge(q_shift, i - 1)
                    pe.wait_ge(qt_in[n], x_count(i, n) + 16)
                    for k in range(2):
                        last = pe.matmul(PQ[:, n, 0:D], XT[:, n, k, :], WQ[:, k, 0:D], start=k == 0, stop=k == 1)
                    last.then_inc(q_made, 1)

                def mix(i, n):
                    pe.wait_ge(q_norm, i + 1)
                    if not (isinstance(i, int) and i < 2):
                        pe.wait_ge(q_copied, i - 1)
                        pe.wait_ge(mix_out, i - 1)
                    for k in range(2):
                        last = pe.transpose(PT[:, n, k * P:(k + 1) * P], QE[:, n, k * P:(k + 1) * P], c.ident[:])
                    last.then_inc(q_turn, 1)
                    pe.wait_ge(q_copied, i + 1)
                    for k in range(2):
                        last = pe.matmul(PM[:, n, 0:D], QT[:, n, k * P:(k + 1) * P], CW[:, k, :], start=k == 0, stop=k == 1)
                    last.then_inc(mixed, 1)

                query(0, 0)
                query(1, 1)
                mix(0, 0)
                with pe.Fori(1, TILES // 2) as j:
                    query(j * 2, 0)
                    mix(j * 2 - 1, 1)
                    query(j * 2 + 1, 1)
                    mix(j * 2, 0)
                query(TILES - 1, 0)
                mix(TILES - 2, 1)
                mix(TILES - 1, 0)

            @block.scalar
            def _(act):
                def exp(i, n):
                    act.wait_ge(q_shift, i + 1)
                    act.activation(QE[:, n, :], QE[:, n, :], ACT.Exp).then_inc(q_exp, 1)

                def copy(i, n):
                    act.wait_ge(q_turn, i + 1)
                    if not (isinstance(i, int) and i < 2):
                        act.wait_ge(mixed, i - 1)
                    act.copy(QT[:, n, :], PT[:, n, 0:D]).then_inc(q_copied, 1)

                def root(i):
                    act.wait_ge(mix_measured, i + 1)
                    act.activation(MV[:, 1:2], MV[:, 1:2], ACT.Ln, bias=c.eps[:, 0:1]).then_inc(logged, 1)
                    act.wait_ge(logged, i + 1)
                    act.activation(MV[:, 1:2], MV[:, 1:2], ACT.Exp, scale=-0.5).then_inc(mix_rooted, 1)

                exp(0, 0)
                exp(1, 1)
                copy(0, 0)
                root(0)
                with act.Fori(1, TILES // 2) as j:
                    exp(j * 2, 0)
                    copy(j * 2 - 1, 1)
                    root(j * 2 - 1)
                    exp(j * 2 + 1, 1)
                    copy(j * 2, 0)
                    root(j * 2)
                exp(TILES - 1, 0)
                copy(TILES - 2, 1)
                root(TILES - 2)
                copy(TILES - 1, 0)
                root(TILES - 1)

            @block.vector
            def _(dve):
                link = Chain(dve, ms)
                PER_SHIFT, PER_NORM, PER_OUT = 1, 2, 3

                def heads(ap):
                    return ap.rearrange("p (h d) -> p h d", h=8)

                def spread8(ap):
                    return bcast(ap.unsqueeze(2), [P, 8, 32])

                def shift(i, n, at):
                    link.n = at
                    dve.wait_ge(q_made, i + 1)
                    link(dve.tensor_reduce(QM[:], heads(PQ[:, n, 0:D]), AX.X, ALU.max))
                    if not (isinstance(i, int) and i < 2):
                        dve.wait_ge(q_turn, i - 1)
                    dve.tensor_tensor(heads(QE[:, n, :]), heads(PQ[:, n, 0:D]), spread8(QM[:]), ALU.subtract).then_inc(q_shift, 1)
                    dve.wait_ge(q_shift, i + 1)

                def norm(i, n, at):
                    link.n = at
                    dve.wait_ge(q_exp, i + 1)
                    link(dve.tensor_reduce(QM[:], heads(QE[:, n, :]), AX.X, ALU.add))
                    link(dve.reciprocal(QM[:], QM[:]))
                    dve.tensor_tensor(heads(QE[:, n, :]), heads(QE[:, n, :]), spread8(QM[:]), ALU.mult).then_inc(q_norm, 1)
                    dve.wait_ge(q_norm, i + 1)

                def finish(i, n, at, before):
                    link.n = at
                    dve.wait_ge(mixed, i + 1)
                    link(dve.bn_stats(ST[:], PM[:, n, 0:D]))
                    stand_apart(dve, mix_apart)
                    dve.bn_aggr(MV[:], ST[:]).then_inc(mix_measured, 1)
                    dve.wait_ge(mix_rooted, i + 1)
                    if before is not None:
                        dve.wait_ge(mix_stored[n], before)
                    link(dve.tensor_scalar(MO[:, n, :], PM[:, n, 0:D], MV[:, 0:1], MV[:, 1:2], ALU.subtract, ALU.mult))
                    link(dve.tensor_tensor(MO[:, n, :], MO[:, n, :], GA[:], ALU.mult))
                    dve.tensor_tensor(MO[:, n, :], MO[:, n, :], X[:, bass.ds(i, 1), :].rearrange("p w d -> p (w d)"),
                                      ALU.add).then_inc(mix_out, 1)
                    dve.wait_ge(mix_out, i + 1)

                per = PER_SHIFT + PER_NORM + PER_OUT
                shift(0, 0, 0)
                norm(0, 0, 1)
                shift(1, 1, 3)
                norm(1, 1, 4)
                finish(0, 0, 6, None)
                shift(2, 0, 9)
                norm(2, 0, 10)
                finish(1, 1, 12, None)
                base = 15
                with dve.Fori(1, TILES // 2) as j:
                    a = (j - 1) * (2 * per) + base
                    shift(j * 2 + 1, 1, a)
                    norm(j * 2 + 1, 1, a + 1)
                    finish(j * 2, 0, a + 3, j * 16)
                    shift(j * 2 + 2, 0, a + per)
                    norm(j * 2 + 2, 0, a + per + 1)
                    finish(j * 2 + 1, 1, a + per + 3, j * 16)
                finish(TILES - 1, 0, base + 2 * per * (TILES // 2 - 1), 16 * (TILES // 2))

            @block.sync
            def _(sp):
                load = load_turned(sp, q_made, qt_in)

                def store(i, n):
                    sp.wait_ge(mix_out, i + 1)
                    sp.dma_start(rows(d["xm"], i), MO[:, n, :]).then_inc(mix_stored[n], 16)

                load(0, 0, True)
                load(1, 1, True)
                load(2, 0, False)
                store(0, 0)
                load(3, 1, False)
                store(1, 1)
                with sp.Fori(1, TILES // 2 - 1) as j:
                    load(j * 2 + 2, 0, False)
                    store(j * 2, 0)
                    load(j * 2 + 3, 1, False)
                    store(j * 2 + 1, 1)
                load(TILES - 1, 0, False)
                store(TILES - 3, 0)
                store(TILES - 2, 1)
                store(TILES - 1, 0)
                sp.wait_ge(mix_stored[0], 16 * (TILES // 2 + 1))
                sp.wait_ge(mix_stored[1], 16 * (TILES // 2))


class EdgeTables:
    pass


def edge_tables(nc, ctx, c, sem, d, g):
    t = g.tag
    B = g.blocks
    e = EdgeTables()

    def keep(name, shape, dt=F32):
        return ctx.enter_context(nc.sbuf_tensor(t + name, shape, dt))

    e.dst = keep("_local_dst", [P, g.grid])
    e.src = keep("_src", [P, g.grid])
    e.chunk_i = keep("_chunk_of_step", [P, B], I32)
    e.window = keep("_window_of_step", [1, g.grid], I32)
    loaded, step, given = sem(t + "_rows_loaded"), sem(t + "_table_step"), sem(t + "_table_pe")
    stored = sem(t + "_tables_stored")
    fetched, fetched_before = c.pool_fetch[2], c.pool_fetch_before[2]
    c.pool_fetch_before[2] += 16 * B
    turned, taken = sem(t + "_cols_turned"), sem(t + "_cols_taken")
    with ExitStack() as s:
        def sb(name, shape, dt=F32):
            return s.enter_context(nc.sbuf_tensor(t + name, shape, dt))

        R = sb("_pair_rows", [P, B, P, 2])
        KI = sb("_keys_i", [P, B, P, 2], I32)
        KB = sb("_keys_b", [P, B, 2, P], BF16)
        ends = sb("_end_cols", [P, 2 * B])
        endT = sb("_end_rows", [2 * B, P])
        cmp1 = sb("_ended", [P, B, TILES + 1])
        sums = sb("_ended_sum", [P, 2, TILES + 1])
        win = sb("_window_edges", [P, TILES + 1])
        AB = sb("_chunks_at", [P, 2, TILES + 1])
        cnt = sb("_steps_of_window", [P, TILES])
        inc = sb("_steps_until", [P, TILES])
        off = sb("_step_offset", [P, TILES])
        doff = sb("_offset_change", [P, TILES])
        sid_i = sb("_step_id_i", [P, B], I32)
        sid = sb("_step_id", [P, B])
        past = sb("_past", [P, B, TILES])
        pastd = sb("_past_change", [P, B, TILES])
        wstep = sb("_window_f", [P, B])
        cstep = sb("_chunk_f", [P, B])
        wrow = sb("_window_rows", [B, P])
        wrow_i = sb("_window_rows_i", [B, P], I32)
        SR = sb("_step_rows", [P, B, P, 2])
        ps = s.enter_context(nc.psum_tensor(t + "_table_ps", [P, 2, 512], F32))
        pt = s.enter_context(nc.psum_tensor(t + "_cols_ps", [P, 2, 512], F32))
        made = sem(t + "_step_iota")
        block = s.enter_context(nc.Block())
        first, last = ends[:, 0:B], ends[:, B:2 * B]
        jobs = []
        for b in range(B):
            cols = slice(b * P, (b + 1) * P)
            jobs.append(([SR[:, b, :, 0]], e.src[:, cols], lambda a: a[:, 0:P]))
            jobs.append(([SR[:, b, :, 1]], e.dst[:, cols], lambda a: a[:, 0:P]))

        at = {}

        @block.vector
        def _(dve):
            link = Chain(dve, step)
            dve.wait_ge(loaded, 16)
            link(dve.tensor_scalar(R[:, :, :, 0], R[:, :, :, 0], float(N - 1), None, ALU.min))
            link(dve.tensor_copy(KI[:], R[:]))
            link(dve.tensor_scalar(KI[:], KI[:], 255, None, ALU.bitwise_and))
            link(dve.tensor_copy(KB[:].rearrange("p b k e -> p b e k"), KI[:]))
            link(dve.tensor_copy(first, R[:, :, 0, 1]))
            link(dve.tensor_copy(last, R[:, :, P - 1, 1]))
            dve.wait_ge(given, 1)
            link(dve.tensor_copy(endT[:], ps[0:2 * B, 0, 0:P]))
            link(dve.tensor_scalar(win[:], c.row[:, 0:TILES + 1], float(P), None, ALU.mult))
            for k, edge in enumerate((last, first)):
                link(dve.tensor_tensor(cmp1[:], bcast(edge.unsqueeze(2), [P, B, TILES + 1]),
                                       bcast(win[:].unsqueeze(1), [P, B, TILES + 1]), ALU.is_lt))
                link(dve.tensor_reduce(sums[:, k, :], cmp1[:].rearrange("p b w -> p w b"), AX.X, ALU.add))
            dve.wait_ge(given, 2)
            link(dve.tensor_copy(AB[:], ps[:, 1, 0:2 * (TILES + 1)].rearrange("p (k w) -> p k w", k=2)))
            link(dve.tensor_tensor(cnt[:], AB[:, 1, 1:TILES + 1], AB[:, 0, 0:TILES], ALU.subtract))
            link(dve.tensor_tensor_scan(inc[:], cnt[:], c.zeros[:, 0:TILES], 0.0, ALU.add, ALU.add))
            link(dve.tensor_tensor(off[:], AB[:, 0, 0:TILES], inc[:], ALU.subtract))
            link(dve.tensor_tensor(off[:], off[:], cnt[:], ALU.add))
            link(dve.memset(doff[:], 0.0))
            link(dve.tensor_tensor(doff[:, 0:TILES - 1], off[:, 1:TILES], off[:, 0:TILES - 1], ALU.subtract))
            dve.wait_ge(made, 1)
            link(dve.tensor_copy(sid[:], sid_i[:]))
            link(dve.tensor_tensor(past[:], bcast(sid[:].unsqueeze(2), [P, B, TILES]),
                                   bcast(inc[:].unsqueeze(1), [P, B, TILES]), ALU.is_ge))
            link(dve.tensor_reduce(wstep[:], past[:], AX.X, ALU.add))
            link(dve.tensor_tensor(pastd[:], past[:], bcast(doff[:].unsqueeze(1), [P, B, TILES]), ALU.mult))
            dve.wait_ge(given, 3)
            link(dve.tensor_copy(wrow_i[:], ps[0:B, 0, 0:P]))
            at["windows"] = link.n
            link(dve.tensor_reduce(cstep[:], pastd[:], AX.X, ALU.add))
            link(dve.tensor_tensor(cstep[:], cstep[:], sid[:], ALU.add))
            link(dve.tensor_scalar(cstep[:], cstep[:], off[:, 0:1], float(g.chunks - 1), ALU.add, ALU.min))
            link(dve.tensor_copy(e.chunk_i[:], cstep[:]))
            at["chunks"] = link.n
            link(dve.tensor_scalar(wstep[:], wstep[:], -float(P), None, ALU.mult))
            for b in range(B):
                if b == 0:
                    dve.wait_ge(fetched, 16 * B + fetched_before)
                link(dve.tensor_scalar(SR[:, b, :, 1], SR[:, b, :, 1], wstep[:, b:b + 1], None, ALU.add))
            at["step_rows"] = link.n

        @block.sync
        def _(sp):
            sp.dma_start(R[:].rearrange("p b e k -> p b (e k)"),
                         d[t + "_pairs"].rearrange("(b c e) k -> c b (e k)", c=P, e=P)).then_inc(loaded, 16)
            sp.wait_ge(step, 1)
            sp.dma_start(d[t + "_edge_rows"].rearrange("(b c) x -> c b x", c=P),
                         R[:].rearrange("p b e k -> p b (e k)")).then_inc(stored, 16)
            sp.wait_ge(step, 4)
            sp.dma_start(d[t + "_keys"].rearrange("(b c) x -> c b x", c=P),
                         KB[:].rearrange("p b k e -> p b (k e)")).then_inc(stored, 16)
            sp.wait_ge(step, 7)
            sp.dma_start(d[t + "_ends"].rearrange("k (b c) -> (k b) c", c=P), endT[:]).then_inc(stored, 16)
            sp.wait_ge(step, at["windows"])
            sp.dma_start(d[t + "_windows"].rearrange("(b c) -> b c", c=P), wrow_i[:]).then_inc(stored, 16)
            sp.wait_ge(stored, 64)
            sp.dma_start(e.window[:], d[t + "_windows"].rearrange("(o s) -> o s", o=1)).then_inc(loaded, 16)
            sp.wait_ge(loaded, 32)

        @block.gpsimd
        def _(pool):
            pool.iota(sid_i[:], [[P, B]], 0, 1).then_inc(made, 1)
            pool.wait_ge(stored, 64)
            pool.wait_ge(step, at["chunks"])
            for b in range(B):
                pool.indirect_dma_start(out=SR[:, b, :, :].rearrange("p e k -> p (e k)"), out_offset=None,
                                        in_=d[t + "_edge_rows"],
                                        in_offset=bass.IndirectOffsetOnAxis(ap=e.chunk_i[:, b:b + 1], axis=0)
                                        ).then_inc(fetched, 16)

        @block.tensor
        def _(pe):
            pe.wait_ge(step, 6)
            pe.transpose(ps[0:2 * B, 0, 0:P], ends[:], c.ident[:]).then_inc(given, 1)
            pe.wait_ge(step, 12)
            pe.matmul(ps[:, 1, 0:2 * (TILES + 1)], c.ones[:], sums[:].rearrange("p k w -> p (k w)"),
                      start=True, stop=True).then_inc(given, 1)
            pe.wait_ge(step, 22)
            pe.transpose(ps[0:B, 0, 0:P], wstep[:], c.ident[:]).then_inc(given, 1)
            pe.wait_ge(step, at["step_rows"])
            transposes(nc, pe, None, jobs, pt, turned, taken, c.ident[:])

        @block.scalar
        def _(act):
            transposes(nc, None, act, jobs, pt, turned, taken, c.ident[:])
    return e


def edge_weights(nc, c, sem, d, g):
    t = g.tag
    B, GR = g.blocks, g.grid
    with ExitStack() as s:
        ER = s.enter_context(nc.sbuf_tensor(t + "_scores_rows", [P, H, B, P], F32))
        look_up_scores(nc, c, sem, d, g, ER)
        subtract_maximum(nc, c, sem, d, g, ER)


def look_up_scores(nc, c, sem, d, g, ER):
    t = g.tag
    B, GR = g.blocks, g.grid
    nb = g.batches
    CH = 4
    keys_in = [sem(t + "_keys_in%d" % i) for i in range(4)]
    onehot, looked, summed, hi_made = (sem(t + n) for n in ("_onehot", "_looked_up", "_score_masked", "_hi_made"))
    hturned, htaken = sem(t + "_hi_turned"), sem(t + "_hi_taken")
    turned, taken = sem(t + "_sc_turned"), sem(t + "_sc_taken")
    rows_in, hstep, picked = sem(t + "_rows_in"), sem(t + "_hi_step"), sem(t + "_score_picked")
    with ExitStack() as s2:
        def sb(name, shape, dt=F32):
            return s2.enter_context(nc.sbuf_tensor(t + name, shape, dt))

        EC = sb("_scores_cols", [P, GR, H])
        R = sb("_rows2", [P, B, P, 2])
        HIr = sb("_hi_rows_i", [P, B, P, 2], I32)
        HC = sb("_hi_cols", [P, GR, 2])
        KB = sb("_keys_everywhere", [P, 4, CH * 2 * P], BF16)
        OH = sb("_lo_onehot", [P, 2, 2, CH * 2 * P], BF16)
        HH = sb("_hi_onehot", [P, CH, 2 * HIS])
        PR = sb("_masked", [P, CH, 2 * HIS, H])
        pt = s2.enter_context(nc.psum_tensor(t + "_hi_ps", [P, 2, 512], F32))
        ps = s2.enter_context(nc.psum_tensor(t + "_lookup_ps", [P, 2, CH, 256], F32))
        block = s2.enter_context(nc.Block())
        jobs = [([R[:, b, :, k]], HC[:, b * P:(b + 1) * P, k], lambda a: a[:, 0:P]) for b in range(B) for k in range(2)]
        jobs2 = []
        for h in range(H):
            for b0 in range(0, B, 4):
                bs = list(range(b0, min(B, b0 + 4)))
                jobs2.append(([EC[:, b * P:(b + 1) * P, h] for b in bs],
                              ER[:, h, bs[0]:bs[-1] + 1, :].rearrange("p b e -> p (b e)"),
                              lambda a, n=len(bs): a[:, 0:n * P]))
        at = {}

        @block.vector
        def _(dve):
            link = Chain(dve, hstep)
            link(dve.memset(EC[:], 0.0))
            dve.wait_ge(rows_in, 16)
            link(dve.tensor_copy(HIr[:], R[:]))
            link(dve.tensor_scalar(HIr[:], HIr[:], 8, None, ALU.arith_shift_right))
            link(dve.tensor_copy(R[:], HIr[:]))
            at["hi"] = link.n
            dve.wait_ge(htaken, len(jobs))

            def masks(i, n, m, j):
                dve.wait_ge(keys_in[n], j * 16 + 16)
                if not (isinstance(i, int) and i < 2):
                    dve.wait_ge(looked, i - 1)
                for par in range(2):
                    dve.tensor_scalar(OH[:, m, par, :], KB[:, n, :], c.lo[:, par:par + 1], None,
                                      ALU.is_equal).then_inc(onehot, 1)

            def pick(i, m):
                hc = HC[:, bass.ds(i * CH, CH), :]
                if not (isinstance(i, int) and i < 1):
                    dve.wait_ge(summed, i)
                dve.tensor_tensor(HH[:].rearrange("p u (k h) -> p (u k) h", k=2),
                                  bcast(hc.rearrange("p u k -> p (u k)").unsqueeze(2), [P, CH * 2, HIS]),
                                  bcast(c.row[:, 0:HIS].unsqueeze(1), [P, CH * 2, HIS]),
                                  ALU.is_equal).then_inc(hi_made, 1)
                dve.wait_ge(hi_made, i + 1)
                dve.wait_ge(looked, i + 1)
                if not (isinstance(i, int) and i < 1):
                    dve.wait_ge(picked, i)
                dve.tensor_tensor(PR[:], ps[:, m, :, 0:2 * HIS * H].rearrange("p u (x h) -> p u x h", h=H),
                                  bcast(HH[:].unsqueeze(3), [P, CH, 2 * HIS, H]), ALU.mult).then_inc(summed, 1)
                dve.wait_ge(summed, i + 1)
                dve.tensor_reduce(EC[:, bass.ds(i * CH, CH), :], PR[:].rearrange("p u x h -> p u h x"), AX.X,
                                  ALU.add).then_inc(picked, 1)

            for i in range(4):
                masks(i, i, i % 2, 0)
                if i:
                    pick(i - 1, (i - 1) % 2)
            with dve.Fori(1, nb // 4) as j:
                for n in range(4):
                    masks(j * 4 + n, n, n % 2, j)
                    pick(j * 4 + n - 1, (n - 1) % 2)
            pick(nb - 1, (nb - 1) % 2)
            dve.wait_ge(picked, nb)
            link(dve.scalar_tensor_tensor(EC[:], EC[:], g.slope, EC[:], ALU.mult, ALU.max))
            at["scores"] = link.n

        @block.sync
        def _(sp):
            sp.dma_start(R[:].rearrange("p b e k -> p b (e k)"),
                         d[t + "_edge_rows"].rearrange("(b c) x -> c b x", c=P)).then_inc(rows_in, 16)
            keys = d[t + "_keys"].rearrange("(n u) x -> n (u x)", u=CH)

            def load(i, n, first):
                if not first:
                    sp.wait_ge(onehot, i * 2 - 6)
                src_ = keys[bass.ds(i, 1), :].rearrange("n x -> (n x)").partition_broadcast(P)
                sp.dma_start(KB[:, n, :], src_).then_inc(keys_in[n], 16)

            for n in range(4):
                load(n, n, True)
            with sp.Fori(1, nb // 4) as j:
                for n in range(4):
                    load(j * 4 + n, n, False)

        @block.tensor
        def _(pe):
            pe.wait_ge(hstep, at["hi"])
            transposes(nc, pe, None, jobs, pt, hturned, htaken, c.ident[:])

            def look(i, m):
                pe.wait_ge(onehot, i * 2 + 2)
                if not (isinstance(i, int) and i < 2):
                    pe.wait_ge(summed, i - 1)
                for u in range(CH):
                    for k in range(2):
                        to = ps[:, m, u, k * HIS * H:(k + 1) * HIS * H]
                        for par in range(2):
                            for q in range(3):
                                last = pe.matmul(to, OH[:, m, par, (u * 2 + k) * P:(u * 2 + k + 1) * P],
                                                 c.scores[:, q, k, par, :, :].rearrange("p a h -> p (a h)"),
                                                 start=par == 0 and q == 0, stop=par == 1 and q == 2)
                last.then_inc(looked, 1)

            for i in range(4):
                look(i, i % 2)
            with pe.Fori(1, nb // 4) as j:
                for n in range(4):
                    look(j * 4 + n, n % 2)
            pe.wait_ge(hstep, at["scores"])
            pe.wait_ge(htaken, len(jobs))
            transposes(nc, pe, None, jobs2, pt, turned, taken, c.ident[:])

        @block.scalar
        def _(act):
            transposes(nc, None, act, jobs, pt, hturned, htaken, c.ident[:])
            transposes(nc, None, act, jobs2, pt, turned, taken, c.ident[:])


def subtract_maximum(nc, c, sem, d, g, ER):
    t = g.tag
    B, GR = g.blocks, g.grid
    step, given = sem(t + "_max_step"), sem(t + "_max_pe")
    loaded, stored, ends_in = sem(t + "_max_loaded"), sem(t + "_max_stored"), sem(t + "_ends_in")
    weights, saved = sem(t + "_weights"), sem(t + "_weights_saved")
    with ExitStack() as s2:
        def sb(name, shape, dt=F32):
            return s2.enter_context(nc.sbuf_tensor(t + name, shape, dt))

        X = [sb("_max_fwd", [P, H, B, P]), sb("_max_bwd", [P, H, B, P])]
        DR = sb("_dst_rows", [P, B, P])
        RS = [sb("_reset_fwd", [P, B, P]), sb("_reset_bwd", [P, B, P])]
        TC = sb("_tails_cols", [P, 2, H * B])
        TR = sb("_tails_rows", [H * B, 2, P])
        Q = 32 + H
        FL = sb("_ends_line", [Q, 2, GR])
        A = sb("_passes", [Q, GR])
        U = sb("_tails_line", [Q, GR])
        V = sb("_entering_line", [Q, GR])
        pm = s2.enter_context(nc.psum_tensor(t + "_max_ps", [P, 2, 512], F32))
        block = s2.enter_context(nc.Block())
        fwd, bwd = slice(0, H), slice(32, 32 + H)
        pairs = X[0][:, 0:2].rearrange("p h b e -> p (h b e)").rearrange("p (b e k) -> p b e k", b=B, k=2)
        at = {}

        def flat(ap):
            return ap.rearrange("p b e -> p (b e)")

        def scans(dve, link):
            for h in range(H):
                a = flat(X[0][:, h])
                link(dve.tensor_tensor_scan(a, flat(RS[0][:]), a, -BIG, ALU.add, ALU.max))
                a = flat(X[1][:, h])[:, ::-1]
                link(dve.tensor_tensor_scan(a, flat(RS[1][:])[:, ::-1], a, -BIG, ALU.add, ALU.max))

        @block.vector
        def _(dve):
            link = Chain(dve, step)
            dve.wait_ge(ends_in, 48)
            link(dve.tensor_copy(DR[:], pairs[:, :, :, 1]))
            for k, r in enumerate(RS):
                link(dve.memset(r[:], 1.0))
                link(dve.tensor_tensor(r[:, :, 1 - k:P - k], DR[:, :, 1:P], DR[:, :, 0:P - 1], ALU.not_equal))
                link(dve.tensor_scalar(r[:], r[:], -BIG, None, ALU.mult))
            for k in range(2):
                link(dve.tensor_copy(X[k][:], ER[:]))
            scans(dve, link)
            link(dve.tensor_copy(TC[:, 0, :].rearrange("p (h b) -> p h b", h=H), X[0][:, :, :, P - 1]))
            link(dve.tensor_copy(TC[:, 1, :].rearrange("p (h b) -> p h b", h=H), X[1][:, :, :, 0]))
            at["tail_cols"] = link.n
            for part in (fwd, bwd):
                link(dve.tensor_tensor(V[part], FL[part, 0, :], FL[part, 1, :], ALU.is_equal))
                link(dve.tensor_tensor(U[part, 1:GR], FL[part, 0, 1:GR], FL[part, 1, 0:GR - 1], ALU.is_equal))
                link(dve.memset(U[part, 0:1], 0.0))
                link(dve.tensor_scalar(FL[part, 0, :], U[part], 1.0, BIG, ALU.subtract, ALU.mult))
            link(dve.tensor_tensor(A[fwd], V[fwd], U[fwd], ALU.mult))
            link(dve.memset(A[bwd], 0.0))
            link(dve.tensor_tensor(A[bwd, 0:GR - 1], V[bwd, 0:GR - 1], U[bwd, 1:GR], ALU.mult))
            for part in (fwd, bwd):
                link(dve.tensor_scalar(A[part], A[part], 1.0, BIG, ALU.subtract, ALU.mult))
            at["line_free"] = link.n
            dve.wait_ge(given, 1)
            link(dve.tensor_copy(TR[:], pm[0:H * B, 0, 0:2 * P].rearrange("p (k c) -> p k c", k=2)))
            at["tails"] = link.n
            dve.wait_ge(loaded, 32)
            a = U[fwd]
            link(dve.tensor_tensor_scan(a, A[fwd], a, -BIG, ALU.add, ALU.max))
            a = U[bwd][:, ::-1]
            link(dve.tensor_tensor_scan(a, A[bwd][:, ::-1], a, -BIG, ALU.add, ALU.max))
            for part in (fwd, bwd):
                link(dve.memset(V[part], -BIG))
            link(dve.tensor_tensor(V[fwd, 1:GR], U[fwd, 0:GR - 1], FL[fwd, 0, 1:GR], ALU.add))
            link(dve.tensor_tensor(V[bwd, 0:GR - 1], U[bwd, 1:GR], FL[bwd, 0, 1:GR], ALU.add))
            at["carries"] = link.n
            for k in range(2):
                link(dve.tensor_copy(X[k][:], ER[:]))
            dve.wait_ge(given, 2)
            for k in range(2):
                edge = X[k][:, :, :, (P - 1) * k]
                link(dve.tensor_tensor(edge, edge, pm[:, 1, k * H * B:(k + 1) * H * B].rearrange("p (h b) -> p h b", h=H), ALU.max))
            scans(dve, link)
            link(dve.tensor_tensor(X[0][:], X[0][:], X[1][:], ALU.max))
            link(dve.tensor_tensor(X[0][:], ER[:], X[0][:], ALU.subtract))
            at["shifted"] = link.n

        @block.sync
        def _(sp):
            sp.dma_start(pairs.rearrange("p b e k -> p b (e k)"),
                         d[t + "_edge_rows"].rearrange("(b c) x -> c b x", c=P)).then_inc(ends_in, 16)
            for part in (fwd, bwd):
                sp.dma_start(FL[part], d[t + "_ends"].partition_broadcast(H)).then_inc(ends_in, 16)
            sp.wait_ge(step, at["tails"])
            sp.dma_start(d[t + "_tails"].rearrange("k h (b c) -> (h b) k c", c=P), TR[:]).then_inc(stored, 16)
            sp.wait_ge(stored, 16)
            for k, part in enumerate((fwd, bwd)):
                sp.dma_start(U[part], d[t + "_tails"][k]).then_inc(loaded, 16)
            sp.wait_ge(step, at["carries"])
            for k, part in enumerate((fwd, bwd)):
                sp.dma_start(d[t + "_carries"][k], V[part]).then_inc(stored, 16)
            sp.wait_ge(stored, 48)
            sp.dma_start(TR[:], d[t + "_carries"].rearrange("k h (b c) -> (h b) k c", c=P)).then_inc(loaded, 16)
            sp.wait_ge(weights, 1)
            rows = d[t + "_weight_rows"].rearrange("(b c) (h e) -> h c b e", c=P, h=H)
            for h in range(H):
                sp.dma_start(rows[h], X[0][:, h]).then_inc(saved, 16)
            sp.wait_ge(saved, 64)

        @block.tensor
        def _(pe):
            pe.wait_ge(step, at["tail_cols"])
            for k in range(2):
                last = pe.transpose(pm[0:H * B, 0, k * P:(k + 1) * P], TC[:, k, :], c.ident[:])
            last.then_inc(given, 1)
            pe.wait_ge(loaded, 48)
            for k in range(2):
                last = pe.transpose(pm[:, 1, k * H * B:(k + 1) * H * B], TR[:, k, :], c.ident[0:H * B, 0:H * B])
            last.then_inc(given, 1)

        @block.scalar
        def _(act):
            act.wait_ge(step, at["shifted"])
            act.activation(X[0][:], X[0][:], ACT.Exp).then_inc(weights, 1)


def fetch_weights(nc, s, c, sem, d, g, e):
    t = g.tag
    B = g.blocks
    W = s.enter_context(nc.sbuf_tensor(t + "_weights", [P, g.grid, H], F32))
    fetched, before = c.pool_fetch[0:2], c.pool_fetch_before[0:2]
    for n in range(2):
        c.pool_fetch_before[n] += 16 * ((B + 1 - n) // 2)
    turned, taken = sem(t + "_weights_turned"), sem(t + "_weights_taken")
    with ExitStack() as s2:
        WR = s2.enter_context(nc.sbuf_tensor(t + "_weight_rows_in", [P, 2, H * P], F32))
        pt = s2.enter_context(nc.psum_tensor(t + "_weights_ps", [P, 2, 512], F32))
        block = s2.enter_context(nc.Block())

        @block.gpsimd
        def _(pool):
            for b in range(B):
                if b >= 2:
                    pool.wait_ge(turned, b - 1)
                pool.indirect_dma_start(out=WR[:, b % 2, :], out_offset=None, in_=d[t + "_weight_rows"],
                                        in_offset=bass.IndirectOffsetOnAxis(ap=e.chunk_i[:, b:b + 1], axis=0)
                                        ).then_inc(fetched[b % 2], 16)

        @block.tensor
        def _(pe):
            for b in range(B):
                pe.wait_ge(fetched[b % 2], 16 * (b // 2 + 1) + before[b % 2])
                if b >= 2:
                    pe.wait_ge(taken, b - 1)
                for h in range(H):
                    last = pe.transpose(pt[:, b % 2, h * P:(h + 1) * P], WR[:, b % 2, h * P:(h + 1) * P], c.ident[:])
                last.then_inc(turned, 1)

        @block.scalar
        def _(act):
            for b in range(B):
                act.wait_ge(turned, b + 1)
                act.copy(W[:, b * P:(b + 1) * P, :].rearrange("p s h -> p h s"),
                         pt[:, b % 2, :].rearrange("p (h s) -> p h s", h=H)).then_inc(taken, 1)
    return W


def aggregate(nc, ctx, c, sem, d, g, e):
    t = g.tag
    F = g.width + 1
    ACC = ctx.enter_context(nc.sbuf_tensor(t + "_sums", [P, TILES + 1, g.row], F32))
    cleared, pool_apart, staged, scaled, multiplied, added = (
        sem(t + n) for n in ("_sums_cleared", "_pool_wait_apart", "_index_staged", "_rows_scaled", "_step_summed", "_step_added"))
    got, before = c.pool_dma, c.pool_dma_before
    c.pool_dma_before += 16 * (g.steps // UNROLL)
    loops = g.steps // UNROLL
    BUF = 4
    with ExitStack() as s2:
        W = fetch_weights(nc, s2, c, sem, d, g, e)
        slot = s2.enter_context(nc.sbuf_tensor(t + "_index_slots", [P, UNROLL], I32))
        G = s2.enter_context(nc.sbuf_tensor(t + "_gathered", [P, UNROLL, g.row], F32))
        ZW = s2.enter_context(nc.sbuf_tensor(t + "_scaled", [P, BUF, g.row], F32))
        OH = s2.enter_context(nc.sbuf_tensor(t + "_dst_onehot", [P, BUF, P], F32))
        ps = s2.enter_context(nc.psum_tensor(t + "_step_ps", [P, BUF, 512], F32))
        block = s2.enter_context(nc.Block())

        @block.scalar
        def _(act):
            def stage(i, first):
                for half in range(2):
                    lo = half * RING
                    if not first:
                        for u in range(lo, lo + RING):
                            act.wait_ge(got[u], i * 16 + before)
                    act.copy(slot[:, lo:lo + RING], e.src[:, bass.ds(i * UNROLL + lo, RING)]).then_inc(staged, 1)

            stage(0, True)
            with act.Fori(1, loops) as i:
                stage(i, False)

        @block.gpsimd
        def _(pool):
            def gather(i, first):
                for u in range(UNROLL):
                    if u % RING == 0:
                        pool.wait_ge(staged, i * 2 + u // RING + 1)
                        stand_apart(pool, pool_apart)
                        if not first:
                            pool.wait_ge(scaled, i * UNROLL + (u + RING - UNROLL))
                            stand_apart(pool, pool_apart)
                    pool.indirect_dma_start(out=G[:, u, :], out_offset=None, in_=d[t + "_rows"],
                                            in_offset=bass.IndirectOffsetOnAxis(ap=slot[:, u:u + 1], axis=0)
                                            ).then_inc(got[u], 16)

            gather(0, True)
            with pool.Fori(1, loops) as i:
                gather(i, False)

        @block.vector
        def _(dve):
            dve.memset(ACC[:], 0.0).then_inc(cleared, 1)
            dve.wait_ge(cleared, 1)

            def scale(i, u, first):
                st = i * UNROLL + u
                if not (first and u < BUF):
                    dve.wait_ge(multiplied, st - (BUF - 1))
                dve.tensor_scalar(OH[:, u % BUF, :], c.row[:], e.dst[:, bass.ds(st, 1)], None, ALU.is_equal)
                dve.wait_ge(got[u], i * 16 + (16 + before))
                dve.tensor_tensor(ZW[:, u % BUF, :].rearrange("p (h f) -> p h f", h=H),
                                  G[:, u, :].rearrange("p (h f) -> p h f", h=H),
                                  bcast(W[:, bass.ds(st, 1), :].rearrange("p s h -> p (s h)").unsqueeze(2), [P, H, F]),
                                  ALU.mult).then_inc(scaled, 1)

            def add(i, u, first):
                st = i * UNROLL + u
                w = dve.value_load(e.window[0:1, bass.ds(st, 1)], min_val=0, max_val=TILES)
                to = ACC[:, bass.ds(w, 1), :].rearrange("p w f -> p (w f)")
                dve.wait_ge(multiplied, st + 1)
                if not (first and u == 0):
                    dve.wait_ge(added, st)
                dve.tensor_tensor(to, to, ps[:, u % BUF, 0:g.row], ALU.add).then_inc(added, 1)

            def group(i, first):
                for u in range(UNROLL):
                    scale(i, u, first)
                    if u >= 2:
                        add(i, u - 2, first)
                add(i, UNROLL - 2, first)
                add(i, UNROLL - 1, first)

            group(0, True)
            with dve.Fori(1, loops) as i:
                group(i, False)
            dve.wait_ge(added, g.steps)

        @block.tensor
        def _(pe):
            def group(i, first):
                for u in range(UNROLL):
                    st = i * UNROLL + u
                    pe.wait_ge(scaled, st + 1)
                    if not (first and u < BUF):
                        pe.wait_ge(added, st - (BUF - 1))
                    pe.matmul(ps[:, u % BUF, 0:g.row], OH[:, u % BUF, :], ZW[:, u % BUF, :], start=True,
                              stop=True).then_inc(multiplied, 1)

            group(0, True)
            with pe.Fori(1, loops) as i:
                group(i, False)
    return ACC


def nodes_between(nc, c, sem, d, acc, wgat, fas, fad):
    W = D // H
    E = 4
    step, loaded, made, x_out, turned, copied, projected, taken = (
        sem("mid_" + n) for n in ("step", "loaded", "xn", "x1", "turned", "copied", "projected", "taken"))
    measured, rooted, apart = sem("mid_measured"), sem("mid_rooted"), sem("mid_wait_apart")
    xm_in = [sem("mid_xm_in0"), sem("mid_xm_in1")]
    x_stored = [sem("mid_x_stored0"), sem("mid_x_stored1")]
    h_stored = [sem("mid_h_stored0"), sem("mid_h_stored1")]
    with ExitStack() as s:
        def sb(name, shape, dt=F32):
            return s.enter_context(nc.sbuf_tensor("mid_" + name, shape, dt))

        WG = sb("w_gat", [P, 2, 24])
        AT = sb("att", [P, 2, 16])
        PR = sb("att_products", [P, 16])
        XM = sb("xm", [P, 2, D])
        X1 = sb("x1", [P, 2, D])
        XN = sb("xn", [P, 2, D])
        XT = sb("xn_turned", [P, 2, D])
        DEN = sb("den", [P, H])
        ST = sb("stats", [P, 6])
        MV = sb("mean_var", [P, 2, 2])
        HO = sb("h_out", [P, 2, H, E + 1])
        REST = sb("rest", [P, HIS, H])
        PT = s.enter_context(nc.psum_tensor("mid_turn_ps", [P, 2, 512], F32))
        PH = s.enter_context(nc.psum_tensor("mid_h_ps", [P, 2, 512], F32))
        block = s.enter_context(nc.Block())
        at = {}

        @block.vector
        def _(dve):
            link = Chain(dve, step)
            link(dve.memset(HO[:], 1.0))
            dve.wait_ge(loaded, 48)
            for k in range(2):
                for a in range(2):
                    link(dve.tensor_tensor(PR[:], WG[:, k, 0:16], AT[:, a, :], ALU.mult))
                    link(dve.tensor_reduce(WG[:, k, 16 + H * a:16 + H * (a + 1)],
                                           PR[:].rearrange("p (h e) -> p h e", h=H), AX.X, ALU.add))
            at["w"] = base = link.n

            def node(i, n, first):
                link.n = i * 6 + base
                cut = acc[:, bass.ds(i, 1), :].rearrange("p w (h f) -> p (w h) f", h=H)
                link(dve.tensor_scalar(DEN[:].unsqueeze(2), cut[:, :, W:W + 1], 1e-30, None, ALU.max))
                link(dve.reciprocal(DEN[:], DEN[:]))
                if not first:
                    dve.wait_ge(x_stored[n], x_count(i, n))
                x3 = X1[:, n, :].rearrange("p (h f) -> p h f", h=H)
                link(dve.tensor_tensor(x3, cut[:, :, 0:W], bcast(DEN[:].unsqueeze(2), [P, H, W]), ALU.mult))
                dve.wait_ge(xm_in[n], x_count(i, n) + 16)
                dve.tensor_tensor(X1[:, n, :], X1[:, n, :], XM[:, n, :], ALU.add).then_inc(x_out, 1)
                dve.wait_ge(x_out, i + 1)
                mv = MV[:, n, :]
                measure(nc, link, ST[:], mv, X1[:, n, :], measured, apart, i)
                if not first:
                    dve.wait_ge(turned, i - 1)
                dve.wait_ge(rooted, i + 1)
                link(dve.reciprocal(mv[:, 1:2], mv[:, 1:2]))
                link(dve.tensor_scalar(c.spread[:, bass.ds(i, 1), :].rearrange("p w s -> p (w s)"), mv, 1.0, None,
                                       ALU.mult))
                dve.tensor_scalar(XN[:, n, :], X1[:, n, :], mv[:, 0:1], mv[:, 1:2], ALU.subtract, ALU.mult).then_inc(made, 1)
                dve.wait_ge(made, i + 1)

            def take(i, n, first):
                dve.wait_ge(projected, i + 1)
                out_ = c.score[:].rearrange("p a hi par h -> p a (hi par) h")[:, :, bass.ds(i, 1), :].rearrange("p a w h -> p a (w h)")
                dve.tensor_copy(out_, PH[:, n, 16:24].rearrange("p (a h) -> p a h", a=2)).then_inc(taken, 1)
                if not first:
                    dve.wait_ge(h_stored[n], x_count(i, n))
                dve.tensor_copy(HO[:, n, :, 0:E], PH[:, n, 0:16].rearrange("p (h e) -> p h e", h=H)).then_inc(taken, 1)

            node(0, 0, True)
            node(1, 1, True)
            take(0, 0, True)
            node(2, 0, False)
            take(1, 1, True)
            with dve.Fori(1, TILES // 2) as j:
                node(j * 2 + 1, 1, False)
                take(j * 2, 0, False)
                node(j * 2 + 2, 0, False)
                take(j * 2 + 1, 1, False)
            take(TILES - 1, 0, False)
            dve.wait_ge(taken, 2 * TILES)
            link.n = base + 6 * TILES
            for a in range(2):
                for par in range(2):
                    link(dve.tensor_copy(REST[:], c.score[:, a, :, par, :]))
                    for k in range(3):
                        link(dve.tensor_copy(c.scores[:, k, a, par, :, :], REST[:]))
                        if k < 2:
                            link(dve.tensor_tensor(REST[:], REST[:], c.scores[:, k, a, par, :, :], ALU.subtract))

        @block.sync
        def _(sp):
            sp.dma_start(WG[:, :, 0:16], wgat.rearrange("(k i) e -> i k e", k=2)).then_inc(loaded, 16)
            sp.dma_start(AT[:, 0, :], fas.rearrange("h e -> (h e)").partition_broadcast(P)).then_inc(loaded, 16)
            sp.dma_start(AT[:, 1, :], fad.rearrange("h e -> (h e)").partition_broadcast(P)).then_inc(loaded, 16)

            def rows(ap, i):
                return ap.rearrange("(w i) d -> w i d", i=P)[bass.ds(i, 1)].rearrange("w i d -> (w i) d")

            def load(i, n, first):
                if not first:
                    sp.wait_ge(x_out, i - 1)
                sp.dma_start(XM[:, n, :], rows(d["xm"], i)).then_inc(xm_in[n], 16)

            def store(i, n):
                sp.wait_ge(x_out, i + 1)
                sp.dma_start(rows(d["x1"], i), X1[:, n, :]).then_inc(x_stored[n], 16)
                sp.wait_ge(taken, i * 2 + 2)
                sp.dma_start(rows(d["ffn_rows"], i), HO[:, n].rearrange("p h e -> p (h e)")).then_inc(h_stored[n], 16)

            load(0, 0, True)
            load(1, 1, True)
            load(2, 0, False)
            store(0, 0)
            load(3, 1, False)
            store(1, 1)
            with sp.Fori(1, TILES // 2 - 1) as j:
                load(j * 2 + 2, 0, False)
                store(j * 2, 0)
                load(j * 2 + 3, 1, False)
                store(j * 2 + 1, 1)
            load(TILES - 1, 0, False)
            store(TILES - 3, 0)
            store(TILES - 2, 1)
            store(TILES - 1, 0)
            for q in (x_stored, h_stored):
                sp.wait_ge(q[0], 16 * (TILES // 2 + 1))
                sp.wait_ge(q[1], 16 * (TILES // 2))

        @block.tensor
        def _(pe):
            pe.wait_ge(step, at["w"])

            def turn(i, n, first):
                pe.wait_ge(made, i + 1)
                if not first:
                    pe.wait_ge(copied, i - 1)
                for k in range(2):
                    last = pe.transpose(PT[:, n, k * P:(k + 1) * P], XN[:, n, k * P:(k + 1) * P], c.ident[:])
                last.then_inc(turned, 1)

            def project(i, n, first):
                pe.wait_ge(copied, i + 1)
                if not first:
                    pe.wait_ge(taken, i * 2 - 2)
                for k in range(2):
                    last = pe.matmul(PH[:, n, 0:24], XT[:, n, k * P:(k + 1) * P], WG[:, k, :], start=k == 0, stop=k == 1)
                last.then_inc(projected, 1)

            turn(0, 0, True)
            turn(1, 1, True)
            project(0, 0, True)
            turn(2, 0, False)
            project(1, 1, True)
            with pe.Fori(1, TILES // 2) as j:
                turn(j * 2 + 1, 1, False)
                project(j * 2, 0, False)
                turn(j * 2 + 2, 0, False)
                project(j * 2 + 1, 1, False)
            project(TILES - 1, 0, False)

        @block.scalar
        def _(act):
            def copy(i, n, first):
                act.wait_ge(turned, i + 1)
                if not first:
                    act.wait_ge(projected, i - 1)
                act.copy(XT[:, n, :], PT[:, n, 0:D]).then_inc(copied, 1)

            root = spreads(c, act, measured, rooted, MV)
            root(0, 0)
            root(1, 1)
            copy(0, 0, True)
            root(2, 0)
            copy(1, 1, True)
            with act.Fori(1, TILES // 2) as j:
                root(j * 2 + 1, 1)
                copy(j * 2, 0, False)
                root(j * 2 + 2, 0)
                copy(j * 2 + 1, 1, False)
            copy(TILES - 1, 0, False)


def x_count(i, n):
    return i // 2 * 16 if isinstance(i, int) else (i - n) * 8


def gates(nc, c, sem, acc, gate, bgat, lng, lnb):
    step, loaded, rooted, expd = sem("gate_step"), sem("gate_loaded"), sem("gate_rooted"), sem("gate_exp")
    E = 4
    with ExitStack() as s:
        def sb(name, shape):
            return s.enter_context(nc.sbuf_tensor("gate_" + name, shape, F32))

        BP = sb("b_gamma_beta", [P, 3, 16])
        A = sb("agg", [P, TILES, 16])
        SQ = sb("squares", [P, TILES, 16])
        DEN = sb("den", [P, TILES, H])
        M = sb("mean", [P, TILES])
        V = sb("var", [P, TILES])
        SC = sb("scores", [P, TILES, E])
        RK = sb("rank", [P, TILES, E])
        C1 = sb("cmp", [P, TILES])
        SUM = sb("sum", [P, TILES])
        block = s.enter_context(nc.Block())
        at = {}

        @block.vector
        def _(dve):
            link = Chain(dve, step)
            dve.wait_ge(loaded, 48)
            a4 = acc[:, 0:TILES, :].rearrange("p w (h f) -> p w h f", h=H)
            A4 = A[:].rearrange("p w (h e) -> p w h e", h=H)

            def row(k):
                return bcast(BP[:, k, :].unsqueeze(1), [P, TILES, 16])

            def tile(ap, n=16):
                return bcast(ap.unsqueeze(2), [P, TILES, n])

            link(dve.tensor_scalar(DEN[:].unsqueeze(3), a4[:, :, :, E:E + 1], 1e-16, None, ALU.add))
            link(dve.reciprocal(DEN[:], DEN[:]))
            link(dve.tensor_tensor(A4, a4[:, :, :, 0:E], bcast(DEN[:].unsqueeze(3), [P, TILES, H, E]), ALU.mult))
            link(dve.tensor_tensor(A[:], A[:], row(0), ALU.add))
            link(dve.tensor_reduce(M[:], A[:], AX.X, ALU.add))
            link(dve.tensor_scalar(M[:], M[:], 1.0 / 16, None, ALU.mult))
            link(dve.tensor_tensor(A[:], A[:], tile(M[:]), ALU.subtract))
            link(dve.tensor_tensor(SQ[:], A[:], A[:], ALU.mult))
            link(dve.tensor_reduce(V[:], SQ[:], AX.X, ALU.add))
            at["squared"] = link.n
            dve.wait_ge(rooted, 1)
            link(dve.reciprocal(V[:], V[:]))
            link(dve.tensor_tensor(A[:], A[:], tile(V[:]), ALU.mult))
            link(dve.tensor_tensor(A[:], A[:], row(1), ALU.mult))
            link(dve.tensor_tensor(A[:], A[:], row(2), ALU.add))
            link(dve.tensor_reduce(SC[:], A[:].rearrange("p w (h e) -> p w e h", h=H), AX.X, ALU.add))
            link(dve.tensor_scalar(SC[:], SC[:], 1.0 / H, None, ALU.mult))
            link(dve.memset(RK[:], 0.0))
            for a in range(E):
                for b in range(E):
                    if a != b:
                        op = ALU.is_ge if b < a else ALU.is_gt
                        link(dve.tensor_tensor(C1[:], SC[:, :, b], SC[:, :, a], op))
                        link(dve.tensor_tensor(RK[:, :, a], RK[:, :, a], C1[:], ALU.add))
            link(dve.tensor_scalar(RK[:], RK[:], 2.0, None, ALU.is_lt))
            link(dve.tensor_reduce(M[:], SC[:], AX.X, ALU.max))
            link(dve.tensor_tensor(SC[:], SC[:], tile(M[:], E), ALU.subtract))
            at["shifted"] = link.n
            dve.wait_ge(expd, 1)
            link(dve.tensor_tensor(SC[:], SC[:], RK[:], ALU.mult))
            link(dve.tensor_reduce(SUM[:], SC[:], AX.X, ALU.add))
            link(dve.reciprocal(SUM[:], SUM[:]))
            link(dve.tensor_tensor(gate[:], SC[:], tile(SUM[:], E), ALU.mult))

        @block.sync
        def _(sp):
            for k, a in enumerate((bgat, lng, lnb)):
                sp.dma_start(BP[:, k, :], a.partition_broadcast(P)).then_inc(loaded, 16)

        @block.scalar
        def _(act):
            act.wait_ge(step, at["squared"])
            act.activation(V[:], V[:], ACT.Sqrt, bias=c.eps[:, 0:1], scale=1.0 / 16).then_inc(rooted, 1)
            act.wait_ge(step, at["shifted"])
            act.activation(SC[:], SC[:], ACT.Exp).then_inc(expd, 1)


def experts(nc, c, sem, d, out, gate, w1, b1, w2, b2):
    E, HID, GT = 4, 512, 4
    HC = HID // P
    FULL = TILES // GT
    assert TILES == FULL * GT + 1 and FULL % 2 == 0
    PG = GT * E
    step, loaded, prepared, made, turned, copied, hidden, gelu, product, added = (
        sem("exp_" + n) for n in ("step", "loaded", "prepared", "xn", "turned", "copied", "hidden", "gelu", "product",
                                  "added"))
    x_in = [sem("exp_x_in0"), sem("exp_x_in1")]
    stored = [sem("exp_stored0"), sem("exp_stored1")]
    with ExitStack() as s:
        def sb(name, shape, dt=F32):
            return s.enter_context(nc.sbuf_tensor("exp_" + name, shape, dt))

        W1 = sb("w1", [P, E, 2, HID])
        W2 = sb("w2", [P, E, HC, D])
        B1 = sb("b1", [P, E, HC])
        B2 = sb("b2", [P, E, D])
        X = sb("x", [P, 2, GT, D])
        XN = sb("xn", [P, GT, D])
        XT = sb("xn_turned", [P, 2, 2, GT * P])
        HT = sb("hidden", [P, 2, HC, GT * P])
        O = sb("out", [P, 2, GT, D])
        PT = s.enter_context(nc.psum_tensor("exp_turn_ps", [P, 2, 512], F32))
        PH = s.enter_context(nc.psum_tensor("exp_hidden_ps", [P, 2, 512], F32))
        PO = s.enter_context(nc.psum_tensor("exp_out_ps", [P, 2, 512], F32))
        block = s.enter_context(nc.Block())

        def groups(engine, body):
            body(0, 0, GT, GT)
            with engine.Fori(0, FULL // 2 - 1) as j:
                body(j * 2 + 1, 1, GT, GT)
                body(j * 2 + 2, 0, GT, GT)
            body(FULL - 1, 1, GT, 1)
            body(FULL, 0, 1, 0)

        def static(i, n):
            return isinstance(i, int) and i < n

        @block.sync
        def _(sp):
            sp.dma_start(W1[:], w1.rearrange("e (k i) h -> i e k h", k=2)).then_inc(loaded, 16)
            sp.dma_start(W2[:], w2.rearrange("e (c i) o -> i e c o", c=HC)).then_inc(loaded, 16)
            sp.dma_start(B1[:], b1.rearrange("e (c i) -> i e c", c=HC)).then_inc(loaded, 16)
            sp.dma_start(B2[:], b2.partition_broadcast(P)).then_inc(loaded, 16)
            x4 = d["x1"][0:FULL * GT * P, :].rearrange("(g t i) d -> g i t d", t=GT, i=P)
            o4 = out[0:FULL * GT * P, :].rearrange("(g t i) d -> g i t d", t=GT, i=P)
            sp.dma_start(X[:, 0, :, :], x4[0]).then_inc(x_in[0], 16)

            def go(i, n, tiles, after):
                if after:
                    if not static(i, 1):
                        sp.wait_ge(prepared, i)
                    if after == GT:
                        sp.dma_start(X[:, 1 - n, :, :], x4[bass.ds(i + 1, 1)].rearrange("g i t d -> (g i) t d")
                                     ).then_inc(x_in[1 - n], 16)
                    else:
                        sp.dma_start(X[:, 1 - n, 0, :], d["x1"][FULL * GT * P:NPAD, :]).then_inc(x_in[1 - n], 16)
                sp.wait_ge(added, i * PG + tiles * E)
                if tiles == GT:
                    sp.dma_start(o4[bass.ds(i, 1)].rearrange("g i t d -> (g i) t d"), O[:, n, :, :]).then_inc(stored[n], 16)
                else:
                    sp.dma_start(out[FULL * GT * P:N, :], O[0:LAST, n, 0, :]).then_inc(stored[n], 16)

            groups(sp, go)
            sp.wait_ge(stored[0], 16 * (FULL // 2 + 1))
            sp.wait_ge(stored[1], 16 * (FULL // 2))

        @block.vector
        def _(dve):
            link = Chain(dve, step)
            LINKS = GT * E

            def gate_at(i, q, ei):
                return gate[:, bass.ds(i * GT + q, 1), ei]

            def prepare(i, n, tiles):
                link.n = i * LINKS
                dve.wait_ge(x_in[n], x_count(i, n) + 16)
                for q in range(tiles):
                    v = i * GT + q
                    mv = c.spread[:, bass.ds(v, 1), :].rearrange("p w s -> p (w s)")
                    if not static(i, 1):
                        dve.wait_ge(turned, v - GT + 1)
                    dve.tensor_scalar(XN[:, q, :], X[:, n, q, :], mv[:, 0:1], mv[:, 1:2], ALU.subtract,
                                      ALU.mult).then_inc(made, 1)
                    dve.wait_ge(made, v + 1)
                if not static(i, 2):
                    dve.wait_ge(stored[n], x_count(i, n))
                for q in range(tiles):
                    for ei in range(E):
                        of = X[:, n, q, :] if ei == 0 else O[:, n, q, :]
                        link(dve.scalar_tensor_tensor(O[:, n, q, :], B2[:, ei, :], gate_at(i, q, ei), of, ALU.mult, ALU.add))
                dve.sem_inc(prepared, 1)

            def go(i, n, tiles, after):
                if after:
                    prepare(i + 1, 1 - n, after)
                for ei in range(E):
                    for q in range(tiles):
                        v = i * PG + (ei * tiles + q)
                        dve.wait_ge(product, v + 1)
                        if ei:
                            dve.wait_ge(added, v - tiles + 1)
                        dve.scalar_tensor_tensor(O[:, n, q, :], PO[:, (ei * tiles + q) % 2, 0:D], gate_at(i, q, ei),
                                                 O[:, n, q, :], ALU.mult, ALU.add).then_inc(added, 1)

            dve.wait_ge(loaded, 64)
            prepare(0, 0, GT)
            groups(dve, go)

        @block.tensor
        def _(pe):
            def turn(i, n, tiles):
                for q in range(tiles):
                    v = i * GT + q
                    pe.wait_ge(made, v + 1)
                    if not (static(i, 1) and q < 2):
                        pe.wait_ge(copied, v - 1)
                    for k in range(2):
                        last = pe.transpose(PT[:, q % 2, k * P:(k + 1) * P], XN[:, q, k * P:(k + 1) * P], c.ident[:])
                    last.then_inc(turned, 1)

            def up(i, n, tiles, ei):
                for h in range(HC):
                    v = i * PG + (ei * HC + h)
                    if not (static(i, 1) and ei == 0 and h < 2):
                        pe.wait_ge(gelu, v - 1)
                    for k in range(2):
                        last = pe.matmul(PH[:, h % 2, 0:tiles * P], W1[:, ei, k, h * P:(h + 1) * P],
                                         XT[:, n, k, 0:tiles * P], start=k == 0, stop=k == 1)
                    last.then_inc(hidden, 1)

            def down(i, n, tiles, ei):
                pe.wait_ge(gelu, i * PG + (ei + 1) * HC)
                for q in range(tiles):
                    p = ei * tiles + q
                    if not (static(i, 1) and p < 2):
                        pe.wait_ge(added, i * PG + p - 1)
                    for h in range(HC):
                        last = pe.matmul(PO[:, p % 2, 0:D], HT[:, ei % 2, h, q * P:(q + 1) * P], W2[:, ei, h, :],
                                         start=h == 0, stop=h == HC - 1)
                    last.then_inc(product, 1)

            def go(i, n, tiles, after):
                pe.wait_ge(copied, i * GT + tiles)
                up(i, n, tiles, 0)
                if after:
                    turn(i + 1, 1 - n, after)
                for ei in range(1, E):
                    up(i, n, tiles, ei)
                    down(i, n, tiles, ei - 1)
                down(i, n, tiles, E - 1)

            pe.wait_ge(loaded, 64)
            turn(0, 0, GT)
            groups(pe, go)

        @block.scalar
        def _(act):
            def copy(i, n, tiles):
                for q in range(tiles):
                    act.wait_ge(turned, i * GT + q + 1)
                    act.copy(XT[:, n, :, q * P:(q + 1) * P], PT[:, q % 2, 0:D].rearrange("p (k i) -> p k i", k=2)
                             ).then_inc(copied, 1)

            def go(i, n, tiles, after):
                for ei in range(E):
                    done = (ei - 1) * tiles if ei >= 2 else (ei - 1) * GT
                    if not (static(i, 1) and ei < 2):
                        act.wait_ge(product, i * PG + done)
                    for h in range(HC):
                        act.wait_ge(hidden, i * PG + (ei * HC + h + 1))
                        act.activation(HT[:, ei % 2, h, 0:tiles * P], PH[:, h % 2, 0:tiles * P], ACT.Gelu,
                                       bias=B1[:, ei, h:h + 1]).then_inc(gelu, 1)
                    if ei == 0 and after:
                        copy(i + 1, 1 - n, after)

            act.wait_ge(loaded, 64)
            copy(0, 0, GT)
            groups(act, go)


_INS = ["x", "src", "dst", "L0_gnn_W", "L0_gnn_a_src", "L0_gnn_a_dst", "L0_mix_Wqkv", "L0_mix_Wout", "L0_mix_gamma",
        "L0_ffn_W_gat", "L0_ffn_att_src", "L0_ffn_att_dst", "L0_ffn_b_gat", "L0_ffn_ln_gamma", "L0_ffn_ln_beta",
        "L0_ffn_W1", "L0_ffn_b1", "L0_ffn_W2", "L0_ffn_b2", "L0_ffn_edge_index"]
_OUTS = [((N, D), "float32")]


def kernel(**inputs):
    import numpy as _np
    import concourse.bacc as _bacc
    from concourse import mybir as _mybir
    from concourse.bass_utils import run_bass_kernel_spmd as _run

    nc = _bacc.Bacc("TRN2", target_bir_lowering=False, num_devices=1)
    arrays, args = {}, []
    for name in _INS:
        a = _np.ascontiguousarray(inputs[name])
        arrays[f"in_{name}_dram"] = a
        args.append(nc.dram_tensor(f"in_{name}_dram", a.shape, _mybir.dt.from_np(a.dtype), kind="ExternalInput").ap())
    for i, (shape, dtype) in enumerate(_OUTS):
        dt = _mybir.dt.from_np(_np.dtype(dtype))
        args.append(nc.dram_tensor(f"out_{i}_dram", shape, dt, kind="ExternalOutput").ap())
    build_program(nc, *args)
    r = _run(nc, [arrays], core_ids=[0])
    got = tuple(r.results[0][f"out_{i}_dram"] for i in range(len(_OUTS)))
    return got[0]
```

```python
from contextlib import ExitStack, contextmanager

import concourse.bass as bass
from concourse import mybir

ALU = mybir.AluOpType
ACT = mybir.ActivationFunctionType
AX = mybir.AxisListType
F32 = mybir.dt.float32
I32 = mybir.dt.int32
BF16 = mybir.dt.bfloat16

P = 128
N = 6250
D = 256
H = 4
TILES = -(-N // P)
NPAD = TILES * P
LAST = N - (TILES - 1) * P
HIS = -(-NPAD // 256)
E1 = 200000
E2 = 131072
E2S = E2 + N
COLS2 = -(-E2S // P)
PADS2 = COLS2 * P - E2S
OFF_WINDOW = 16000.0
DROP_DST = 8191.0
BIG = 1.0e38
EPS = 1e-5
UNROLL = 16
RING = 8
REST = 1000


def stand_apart(engine, sem):
    engine.sem_inc(sem, 1)


class Graph:

    def __init__(self, tag, chunks, slope, width):
        self.tag = tag
        self.chunks = chunks
        self.blocks = -(-(chunks + TILES - 1) // P)
        self.grid = self.blocks * P
        self.steps = -(-(chunks + TILES - 1) // UNROLL) * UNROLL
        self.batches = -(-chunks // 16) * 4
        self.slope = slope
        self.width = width // H
        self.row = width + H
        self.in_psum = (TILES + 1) * self.row <= 1024
        self.beside_lookup = self.batches // 5 if self.in_psum else REST
        self.beside_maximum = 7 if self.in_psum else REST
        assert self.steps <= self.grid and self.batches * 4 <= self.grid


class Chain:

    def __init__(self, engine, sem, start=0):
        self.engine, self.sem, self.n = engine, sem, start

    def __call__(self, ins):
        self.n += 1
        ins.then_inc(self.sem, 1)
        self.engine.wait_ge(self.sem, self.n)


def bcast(ap, shape):
    return ap.to_broadcast(shape)


@contextmanager
def stage(nc):
    with ExitStack() as s:
        held = []

        def sem(name):
            held.append(s.enter_context(nc.semaphore(name)))
            return held[-1]

        yield sem
        with nc.Block() as block:
            @block.gpsimd
            def _(pool):
                for q in held:
                    pool.sem_clear(q)


def build_program(nc, x, src, dst, gw, gas, gad, wqkv, wout, gamma, wgat, fas, fad, bgat, lng, lnb,
                  w1, b1, w2, b2, edges, out):
    gnn = Graph("gnn", -(-E1 // P), 0.01, D)
    ffn = Graph("ffn", COLS2, 0.2, 16)
    with ExitStack() as ctx:
        ctx.enter_context(nc.allow_non_contiguous_dma(reason="small tables"))

        def dram(name, shape, dt=F32):
            return nc.dram_tensor(name, shape, dt).ap()

        c = Consts(nc, ctx)
        d = {
            "gnn_pairs": dram("gnn_pairs", [gnn.grid * P, 2]),
            "ffn_pairs": dram("ffn_pairs", [ffn.grid * P, 2]),
            "unsorted": dram("unsorted_pairs", [COLS2 * P, 2]),
            "halfsorted": dram("halfsorted_pairs", [COLS2 * P, 2]),
            "gnn_rows": dram("gnn_rows", [NPAD, gnn.row]),
            "ffn_rows": dram("ffn_rows", [NPAD, 16]),
            "x1": dram("x_after_gnn", [NPAD, D]),
            "xt": dram("xn_transposed", [NPAD, D]),
            "xm": dram("x_plus_mix", [NPAD, D]),
        }
        for g in (gnn, ffn):
            d[g.tag + "_keys"] = dram(g.tag + "_keys", [g.grid, 2 * P], BF16)
            d[g.tag + "_edge_rows"] = dram(g.tag + "_edge_rows", [g.grid, 2 * P])
            d[g.tag + "_weight_rows"] = dram(g.tag + "_weight_rows", [g.grid, H * P])
            d[g.tag + "_ends"] = dram(g.tag + "_ends", [2, g.grid])
            d[g.tag + "_tails"] = dram(g.tag + "_tails", [2, H, g.grid])
            d[g.tag + "_carries"] = dram(g.tag + "_carries", [2, H, g.grid])
            d[g.tag + "_windows"] = dram(g.tag + "_windows", [g.grid], I32)
        with stage(nc) as sem:
            constants(nc, c, sem)
            list_edges(nc, sem, d, src, dst, edges, gnn, ffn)
        kept = ctx.enter_context(ExitStack())
        tables = EdgeTables(nc, kept, gnn)
        with ExitStack() as sorting:
            with stage(nc) as sem:
                scatter = sort_pass(nc, sorting, c, sem, "lo", d["unsorted"], d["halfsorted"], COLS2 * P)
            with stage(nc) as sem:
                nodes_in(nc, c, sem, d, x, gw, gas, gad, wqkv, wout, gamma, scatter.share)
                edge_tables(nc, c, sem, d, gnn, tables, scatter.share)
        with ExitStack() as sorting:
            with stage(nc) as sem:
                scatter = sort_pass(nc, sorting, c, sem, "hi", d["halfsorted"], d["ffn_pairs"], ffn.grid * P)
            with stage(nc) as sem:
                edge_weights(nc, c, sem, d, gnn, scatter.share)
        with stage(nc) as sem:
            acc = aggregate(nc, kept, c, sem, d, gnn, tables)
            nodes_between(nc, c, sem, d, acc, wgat, fas, fad)
        kept.close()
        gate = ctx.enter_context(nc.sbuf_tensor("gate_of_expert", [P, TILES, 4], F32))
        with ExitStack() as kept:
            tables = EdgeTables(nc, kept, ffn)
            with stage(nc) as sem:
                edge_tables(nc, c, sem, d, ffn, tables, None)
                gather = Gather(nc, kept, c, d, ffn, tables)
                edge_weights(nc, c, sem, d, ffn, gather.share)
            with stage(nc) as sem:
                acc = add_up(nc, kept, c, sem, d, ffn, tables, gather)
                gates(nc, c, sem, acc, gate, bgat, lng, lnb)
        with stage(nc) as sem:
            experts(nc, c, sem, d, out, gate, w1, b1, w2, b2)


class Consts:

    def __init__(self, nc, ctx):
        def sb(name, shape, dt=F32):
            return ctx.enter_context(nc.sbuf_tensor(name, shape, dt))

        self.row_i = sb("iota_row_i", [P, P], I32)
        self.col_i = sb("iota_col_i", [P, 1], I32)
        self.row = sb("iota_row", [P, P])
        self.lo = sb("iota_lo", [P, 2])
        self.ident = sb("identity", [P, P])
        self.ones = sb("ones", [P, P])
        self.before = sb("before", [P, P])
        self.blocks32 = sb("blocks32", [P, P])
        self.zeros = sb("zeros", [P, COLS2])
        self.eps = sb("eps", [P, 1])
        self.spread = sb("x1_mean_and_inverse_root_of_variance", [P, TILES, 2])
        self.held = ctx
        self.ring_done = {use: [ctx.enter_context(nc.semaphore("%s_half%d_done" % (use, k))) for k in range(2)]
                          for use in ("lo_scatter", "hi_scatter", "ffn_gather")}
        self.ring_done["gnn_gather"] = [ctx.enter_context(nc.semaphore("gnn_gather_quarter%d_done" % k)) for k in range(4)]
        self.pool_fetch_before = [0, 0, 0]
        self.pool_fetch = [ctx.enter_context(nc.semaphore("pool_fetch%d" % u)) for u in range(3)]
        self.scores = sb("scores_bf16", [P, 3, 2, 2, HIS, H], BF16)
        self.score = sb("scores_f32", [P, 2, HIS, 2, H])


def constants(nc, c, sem):
    made_iota, cs = sem("made_iota"), sem("const_step")
    with nc.sbuf_tensor("shifted_row", [P, P], I32) as shr, nc.sbuf_tensor("shifted_col", [P, 1], I32) as shc, \
            nc.sbuf_tensor("shifted_row_f", [P, P], F32) as shrf, nc.sbuf_tensor("shifted_col_f", [P, 1], F32) as shcf, \
            nc.Block() as block:
        @block.gpsimd
        def _(pool):
            pool.iota(c.row_i[:], [[1, P]], 0, 0).then_inc(made_iota, 1)
            pool.iota(c.col_i[:], [[0, 1]], 0, 1).then_inc(made_iota, 1)

        @block.vector
        def _(dve):
            link = Chain(dve, cs)
            link(dve.memset(c.ones[:], 1.0))
            link(dve.memset(c.zeros[:], 0.0))
            link(dve.memset(c.eps[:], EPS))
            dve.wait_ge(made_iota, 2)
            link(dve.tensor_copy(c.row[:], c.row_i[:]))
            link(dve.tensor_copy(c.lo[:, 0:1], c.col_i[:]))
            link(dve.tensor_scalar(c.lo[:, 1:2], c.lo[:, 0:1], 128.0, None, ALU.add))
            link(dve.tensor_scalar(c.ident[:], c.row[:], c.lo[:, 0:1], None, ALU.is_equal))
            link(dve.tensor_scalar(c.before[:], c.row[:], c.lo[:, 0:1], None, ALU.is_gt))
            link(dve.tensor_scalar(shr[:], c.row_i[:], 5, None, ALU.arith_shift_right))
            link(dve.tensor_scalar(shc[:], c.col_i[:], 5, None, ALU.arith_shift_right))
            link(dve.tensor_copy(shrf[:], shr[:]))
            link(dve.tensor_copy(shcf[:], shc[:]))
            link(dve.tensor_scalar(c.blocks32[:], shrf[:], shcf[:, 0:1], None, ALU.is_equal))
            link(dve.memset(c.score[:], 0.0))


def list_edges(nc, sem, d, src, dst, edges, gnn, ffn):
    loaded = [sem("edges_loaded%d" % i) for i in range(4)]
    paired, stored = sem("edges_paired"), sem("pairs_stored")
    R1 = 125
    T1 = E1 // R1
    T2 = E2 // P
    RS = 125
    TS = N // RS
    with ExitStack() as s:
        def sb(name, shape, dt=F32):
            return s.enter_context(nc.sbuf_tensor(name, shape, dt))

        i1 = sb("gnn_edges_i", [R1, 2, T1], I32)
        p1 = sb("gnn_edges_p", [R1, T1, 2])
        i2 = sb("ffn_edges_i", [P, 2, T2], I32)
        p2 = sb("ffn_edges_p", [P, T2, 2])
        si = sb("self_i", [RS, TS], I32)
        sp_ = sb("self_p", [RS, TS, 2])
        pad = sb("pad_pairs", [P, P, 2])
        drop = sb("drop_pairs", [P, 2])
        made = sem("self_iota")
        block = s.enter_context(nc.Block())

        @block.gpsimd
        def _(pool):
            pool.iota(si[:], [[1, TS]], 0, TS).then_inc(made, 1)

        @block.vector
        def _(dve):
            link = Chain(dve, paired)
            link(dve.memset(pad[:, :, 0], 0.0))
            link(dve.memset(pad[:, :, 1], OFF_WINDOW))
            link(dve.memset(drop[:, 0:1], 0.0))
            link(dve.memset(drop[:, 1:2], DROP_DST))
            dve.wait_ge(made, 1)
            link(dve.tensor_copy(sp_[:, :, 0], si[:]))
            link(dve.tensor_copy(sp_[:, :, 1], si[:]))
            for k in range(2):
                dve.wait_ge(loaded[2 + k], 16)
                link(dve.tensor_copy(p2[:, :, k], i2[:, k, :]))
            for k in range(2):
                dve.wait_ge(loaded[k], 16)
                link(dve.tensor_copy(p1[:, :, k], i1[:, k, :]))

        @block.sync
        def _(sp):
            for k in range(2):
                sp.dma_start(i2[:, k, :], edges[k].rearrange("(p t) -> p t", p=P)).then_inc(loaded[2 + k], 16)
            for k, a in enumerate((src, dst)):
                sp.dma_start(i1[:, k, :], a.rearrange("(p t) -> p t", p=R1)).then_inc(loaded[k], 16)
            sp.wait_ge(paired, 6)
            n = 0
            sp.dma_start(d["unsorted"][E2:E2 + N, :].rearrange("(p t) k -> p t k", p=RS), sp_[:]).then_inc(stored, 16)
            sp.dma_start(d["unsorted"][E2S:E2S + PADS2, :], drop[0:PADS2, :]).then_inc(stored, 16)
            rest = gnn.grid * P - E1
            rows = next(r for r in range(P, 0, -1) if rest % r == 0 and rest // r <= P)
            sp.dma_start(d["gnn_pairs"][E1:, :].rearrange("(p t) k -> p t k", p=rows),
                         pad[0:rows, 0:rest // rows, :]).then_inc(stored, 16)
            n += 3
            for b in range(ffn.blocks):
                sp.dma_start(d["ffn_pairs"][b * P * P:(b + 1) * P * P, :].rearrange("(p t) k -> p t k", p=P),
                             pad[:]).then_inc(stored, 16)
                n += 1
            sp.wait_ge(paired, 8)
            sp.dma_start(d["unsorted"][0:E2, :].rearrange("(p t) k -> p t k", p=P), p2[:]).then_inc(stored, 16)
            sp.wait_ge(paired, 10)
            sp.dma_start(d["gnn_pairs"][0:E1, :].rearrange("(p t) k -> p t k", p=R1), p1[:]).then_inc(stored, 16)
            sp.wait_ge(stored, 16 * (n + 2))


def sort_pass(nc, kept, c, sem, digit, pairs_in, pairs_out, room):
    T = COLS2
    TP = -(-T // UNROLL) * UNROLL
    K = 4
    nb = P if digit == "lo" else -(-TILES // K) * K
    masked, ranked, placed = (sem(digit + n) for n in ("_masked", "_ranked", "_placed"))
    loaded, step = sem(digit + "_loaded"), sem(digit + "_step")
    summed = sem(digit + "_summed")
    apart = sem(digit + "_wait_apart")
    pr = kept.enter_context(nc.sbuf_tensor(digit + "_pairs", [P, TP, 2], F32))
    place = kept.enter_context(nc.sbuf_tensor(digit + "_place", [P, TP], F32))
    with ExitStack() as s:
        def sb(name, shape, dt=F32):
            return s.enter_context(nc.sbuf_tensor(digit + name, shape, dt))

        ki = sb("_key_i", [P, T], I32)
        key = sb("_key", [P, T])
        is_digit = sb("_is_digit", [P, K, T])
        rank = sb("_rank", [P, K, T])
        cnt = sb("_count", [P, P])
        tot = sb("_total", [P, P])
        base = sb("_base", [P, P])
        ps = s.enter_context(nc.psum_tensor(digit + "_sums", [P, 2, 512], F32))
        block = s.enter_context(nc.Block())

        @block.sync
        def _(sp):
            sp.dma_start(pr[:, 0:T, :], pairs_in.rearrange("(p t) k -> p t k", p=P)).then_inc(loaded, 16)

        @block.vector
        def _(dve):
            link = Chain(dve, step)
            link(dve.memset(pr[:, T:TP, :], 0.0))
            link(dve.memset(place[:], 1.0e6))
            dve.wait_ge(loaded, 16)
            link(dve.tensor_copy(ki[:], pr[:, 0:T, 1]))
            if digit == "lo":
                link(dve.tensor_scalar(ki[:], ki[:], P - 1, None, ALU.bitwise_and))
            else:
                link(dve.tensor_scalar(ki[:], ki[:], 7, None, ALU.arith_shift_right))
            link(dve.tensor_copy(key[:], ki[:]))
            n = link.n

            def count(j, first):
                for u in range(K):
                    b = bass.ds(j * K + u, 1)
                    if not first:
                        dve.wait_ge(step, j * K + (n + u + 1 - K))
                    dve.tensor_scalar(is_digit[:, u, :], key[:], c.row[:, b], 0.0, ALU.is_equal, ALU.add,
                                      accum_out=cnt[:, b]).then_inc(step, 1)

            count(0, True)
            with dve.Fori(1, nb // K) as j:
                count(j, False)
            link.n = n + nb
            dve.wait_ge(step, link.n)
            dve.wait_ge(summed, 1)
            link(dve.tensor_copy(tot[:, 0:nb], ps[:, 0, 0:nb]))
            link(dve.tensor_tensor_scan(base[:, 0:nb], tot[:, 0:nb], c.zeros[:, 0:nb], -1.0, ALU.add, ALU.add))
            link(dve.tensor_tensor(base[:, 0:nb], base[:, 0:nb], tot[:, 0:nb], ALU.subtract))
            link(dve.tensor_tensor(base[:, 0:nb], base[:, 0:nb], ps[:, 1, 0:nb], ALU.add))
            def mask(b, u, first):
                if not first:
                    dve.wait_ge(placed, b - (K - 1))
                dve.tensor_scalar(is_digit[:, u, :], key[:], c.row[:, bass.ds(b, 1)], None,
                                  ALU.is_equal).then_inc(masked, 1)

            def run(b, u):
                dve.wait_ge(masked, b + 1)
                dve.tensor_tensor_scan(rank[:, u, :], is_digit[:, u, :], c.zeros[:, 0:T], base[:, bass.ds(b, 1)],
                                       ALU.add, ALU.add).then_inc(ranked, 1)

            def put(b, u, first):
                dve.wait_ge(ranked, b + 1)
                stand_apart(dve, apart)
                if not first:
                    dve.wait_ge(placed, b)
                    stand_apart(dve, apart)
                dve.copy_predicated(place[:, 0:T], is_digit[:, u, :].bitcast(I32), rank[:, u, :]).then_inc(placed, 1)

            def group(j, first):
                for u in range(K):
                    b = j * K + u
                    mask(b, u, first)
                    if not (first and u < 1):
                        run(b - 1, (u - 1) % K)
                    if not (first and u < 2):
                        put(b - 2, (u - 2) % K, first and u == 2)

            group(0, True)
            with dve.Fori(1, nb // K) as j:
                group(j, False)
            run(nb - 1, K - 1)
            put(nb - 2, K - 2, False)
            put(nb - 1, K - 1, False)
            dve.wait_ge(placed, nb)

        @block.tensor
        def _(pe):
            pe.wait_ge(step, 5 + nb)
            pe.matmul(ps[:, 0, 0:nb], c.ones[:], cnt[:, 0:nb], start=True, stop=True)
            pe.matmul(ps[:, 1, 0:nb], c.before[:], cnt[:, 0:nb], start=True, stop=True).then_inc(summed, 1)

    return Scatter(nc, kept, c, digit, pr, place, pairs_out, room)


class Scatter:

    def __init__(self, nc, kept, c, digit, pr, place, pairs_out, room):
        self.pr, self.place, self.pairs_out, self.room = pr, place, pairs_out, room
        self.loops, self.done_loops = place.shape[1] // UNROLL, 0
        self.slot_i = kept.enter_context(nc.sbuf_tensor(digit + "_slot_index", [P, UNROLL], I32))
        self.slot_p = kept.enter_context(nc.sbuf_tensor(digit + "_slot_pair", [P, UNROLL, 2], F32))
        self.staged, self.apart = (c.held.enter_context(nc.semaphore(digit + n)) for n in ("_staged", "_pool_wait_apart"))
        self.scattered = c.ring_done[digit + "_scatter"]

    def half(self, pool, i, k, first):
        lo, hi = k * RING, (k + 1) * RING
        at = bass.ds(i * UNROLL + lo, RING)
        if not first:
            pool.wait_ge(self.scattered[k], i * (16 * RING))
            stand_apart(pool, self.apart)
        pool.tensor_copy(self.slot_i[:, lo:hi], self.place[:, at]).then_inc(self.staged, 1)
        pool.tensor_copy(self.slot_p[:, lo:hi, :], self.pr[:, at, :]).then_inc(self.staged, 1)
        pool.wait_ge(self.staged, i * 4 + 2 * k + 2)
        stand_apart(pool, self.apart)
        for u in range(lo, hi):
            pool.indirect_dma_start(
                out=self.pairs_out, out_offset=bass.IndirectOffsetOnAxis(ap=self.slot_i[:, u:u + 1], axis=0),
                in_=self.slot_p[:, u, :], in_offset=None, bounds_check=self.room - 1,
                oob_is_err=False).then_inc(self.scattered[k], 16)

    def share(self, pool, loops):
        i, end = self.done_loops, min(self.loops, self.done_loops + loops)
        if i == 0:
            for k in range(2):
                self.half(pool, 0, k, True)
            i = 1
        if i < end:
            with pool.Fori(i, end) as i:
                for k in range(2):
                    self.half(pool, i, k, False)
        if end == self.loops and self.done_loops < end:
            for k in range(2):
                pool.wait_ge(self.scattered[k], 16 * RING * self.loops)
        self.done_loops = end


def transposes(nc, pe, act, jobs, ps, given, taken, ident):
    banks = ps.shape[1]
    if pe is not None:
        for j, (ins, _, _) in enumerate(jobs):
            if j >= banks:
                pe.wait_ge(taken, j - banks + 1)
            for q, a in enumerate(ins):
                w = a.free_size()
                last = pe.transpose(ps[0:w, j % banks, q * P:(q + 1) * P], a, ident)
            last.then_inc(given, 1)
    if act is not None:
        for j, (_, o, view) in enumerate(jobs):
            act.wait_ge(given, j + 1)
            act.copy(o, view(ps[:, j % banks, :])).then_inc(taken, 1)


def measure(nc, link, stats, mv, rows, measured, apart, i):
    if not (isinstance(i, int) and i == 0):
        nc.vector.wait_ge(measured, i)
    link(nc.vector.bn_stats(stats, rows))
    stand_apart(nc.vector, apart)
    nc.vector.bn_aggr(mv, stats).then_inc(measured, 1)


def spreads(c, engine, measured, rooted, ring):
    def root(i, n):
        engine.wait_ge(measured, i + 1)
        v = ring[:, n, 1:2]
        engine.activation(v, v, ACT.Sqrt, bias=c.eps[:, 0:1]).then_inc(rooted, 1)
    return root


def tile_loop(engine, body):
    body(0)
    with engine.Fori(1, TILES - 1) as i:
        body(i)
    body(TILES - 1)


def nodes_in(nc, c, sem, d, x, gw, gas, gad, wqkv, wout, gamma, beside):
    with ExitStack() as s:
        def sb(name, shape, dt=F32):
            return s.enter_context(nc.sbuf_tensor("in_" + name, shape, dt))

        X = sb("x", [P, TILES, D])
        XT = sb("xn_transposed", [P, 2, 2, P])
        WZ = sb("w_graph", [P, 2, D + 2 * H])
        WQ = sb("w_qkv", [P, 2, 3 * D])
        WO = sb("w_out", [P, 2, D])
        GA = sb("gamma", [P, D])
        AS = sb("att", [P, 2, D])
        PROD = sb("att_products", [P, D])
        KM = sb("k_max", [P, D])
        KMT = sb("k_max_column", [P, 2])
        KD = sb("k_max_diagonal", [P, 2, P])
        KB = sb("k_max_everywhere", [P, D])
        CT = sb("context_masked", [P, 2, P])
        CW = sb("context_out", [P, 2, D])
        SUMS = sb("k_sums", [P, 2])

        loaded = [sem("node_loaded%d" % i) for i in range(3)]
        cleared, step = sem("x_cleared"), sem("project_step")
        ahead, turned, copied = sem("xn_ready"), sem("xn_turned"), sem("xn_copied")
        measured, rooted, inverted, apart = (sem("x_" + n) for n in ("measured", "rooted", "inverted", "wait_apart"))
        projected, taken_z, taken_k = sem("projected"), sem("z_taken"), sem("k_taken")
        stored = [sem("z_stored0"), sem("z_stored1")]
        xt_stored = [sem("xt_stored0"), sem("xt_stored1")]

        def rows(ap, i):
            return ap.rearrange("(w i) d -> w i d", i=P)[bass.ds(i, 1)].rearrange("w i d -> (w i) d")

        def load_turned(sp, used, arrived):
            def load(i, n, first):
                if not first:
                    sp.wait_ge(used, i - 1)
                sp.dma_start(XT[:, n].rearrange("p k i -> p (k i)"), rows(d["xt"], i)).then_inc(arrived[n], 16)
            return load
        with ExitStack() as s2:
            XN = s2.enter_context(nc.sbuf_tensor("in_xn", [P, 2, D], F32))
            ST = s2.enter_context(nc.sbuf_tensor("in_stats", [P, 6], F32))
            MV = s2.enter_context(nc.sbuf_tensor("in_mean_var", [P, 2, 2], F32))
            ZO = s2.enter_context(nc.sbuf_tensor("in_z_out", [P, 2, H, D // H + 1], F32))
            PT = s2.enter_context(nc.psum_tensor("ps_in_turn", [P, 2, 512], F32))
            PZ = s2.enter_context(nc.psum_tensor("ps_in_z", [P, 2, 512], F32))
            PK = s2.enter_context(nc.psum_tensor("ps_in_k", [P, 2, 512], F32))
            block = s2.enter_context(nc.Block())

            @block.gpsimd
            def _(pool):
                beside(pool, 21)

            @block.sync
            def _(sp):
                sp.wait_ge(cleared, 1)
                full = TILES - 1
                sp.dma_start(X[:, 0:full, :], x[0:full * P, :].rearrange("(w i) d -> i w d", i=P)).then_inc(loaded[0], 16)
                sp.dma_start(X[0:LAST, full, :], x[full * P:N, :]).then_inc(loaded[1], 16)
                for k in range(2):
                    sp.dma_start(WZ[:, k, 0:D].rearrange("i (h d) -> i h d", h=H),
                                 gw[:, k * P:(k + 1) * P, :].rearrange("h i d -> i h d")).then_inc(loaded[2], 16)
                sp.dma_start(WQ[:], wqkv.rearrange("(k i) d -> i k d", k=2)).then_inc(loaded[2], 16)
                sp.dma_start(WO[:], wout.rearrange("(k i) d -> i k d", k=2)).then_inc(loaded[2], 16)
                sp.dma_start(GA[:], gamma.partition_broadcast(P)).then_inc(loaded[2], 16)
                sp.dma_start(AS[:, 0, :], gas.rearrange("h d -> (h d)").partition_broadcast(P)).then_inc(loaded[2], 16)
                sp.dma_start(AS[:, 1, :], gad.rearrange("h d -> (h d)").partition_broadcast(P)).then_inc(loaded[2], 16)

                def store(i, n):
                    sp.wait_ge(copied, i + 1)
                    sp.dma_start(rows(d["xt"], i), XT[:, n].rearrange("p k i -> p (k i)")).then_inc(xt_stored[n], 16)
                    sp.wait_ge(taken_z, i + 1)
                    sp.dma_start(d["gnn_rows"].rearrange("(w i) d -> w i d", i=P)[bass.ds(i, 1)].rearrange("w i d -> (w i) d"),
                                 ZO[:, n, :, :].rearrange("p h f -> p (h f)")).then_inc(stored[n], 16)

                with sp.Fori(0, TILES // 2) as i:
                    store(i * 2, 0)
                    store(i * 2 + 1, 1)
                store(TILES - 1, 0)
                for q in (stored, xt_stored):
                    sp.wait_ge(q[0], 16 * (TILES // 2 + 1))
                    sp.wait_ge(q[1], 16 * (TILES // 2))

            @block.vector
            def _(dve):
                link = Chain(dve, step)
                dve.memset(X[:, TILES - 1, :], 0.0).then_inc(cleared, 1)
                link(dve.memset(KM[:], -3.0e38))
                link(dve.memset(ZO[:], 1.0))
                dve.wait_ge(loaded[2], 16 * 7)
                for k in range(2):
                    for a in range(2):
                        link(dve.tensor_tensor(PROD[:], WZ[:, k, 0:D], AS[:, a, :], ALU.mult))
                        link(dve.tensor_reduce(WZ[:, k, D + H * a:D + H * (a + 1)],
                                               PROD[:].rearrange("p (h d) -> p h d", h=H), AX.X, ALU.add))
                dve.wait_ge(loaded[0], 16)
                dve.wait_ge(loaded[1], 16)
                base = link.n

                def row_of(i):
                    return X[:, bass.ds(i, 1), :].rearrange("p w d -> p (w d)")

                def stats(i, n):
                    link.n = i + base
                    if not (isinstance(i, int) and i < 2):
                        dve.wait_ge(ahead, i - 1)
                    measure(nc, link, ST[:], MV[:, n, :], row_of(i), measured, apart, i)

                def norm(i, n):
                    if not (isinstance(i, int) and i == TILES - 1):
                        stats(i + 1, 1 - n)
                    mv = MV[:, n, :]
                    dve.wait_ge(rooted, i + 1)
                    dve.reciprocal(mv[:, 1:2], mv[:, 1:2]).then_inc(inverted, 1)
                    dve.wait_ge(inverted, i + 1)
                    if not (isinstance(i, int) and i < 2):
                        dve.wait_ge(turned, i - 1)
                    dve.tensor_scalar(XN[:, n, :], row_of(i), mv[:, 0:1], mv[:, 1:2], ALU.subtract, ALU.mult).then_inc(ahead, 1)

                def take(i, n):
                    dve.wait_ge(projected, i + 1)
                    w = bass.ds(i, 1)
                    rows = LAST if isinstance(i, int) and i == TILES - 1 else P
                    out_ = c.score[:].rearrange("p a hi par h -> p a (hi par) h")[:, :, w, :].rearrange("p a w h -> p a (w h)")
                    dve.tensor_copy(out_, PK[:, n, D:D + 2 * H].rearrange("p (a h) -> p a h", a=2)).then_inc(taken_k, 1)
                    dve.tensor_tensor(KM[0:rows, :], KM[0:rows, :], PK[0:rows, n, 0:D], ALU.max).then_inc(taken_k, 1)
                    dve.wait_ge(taken_k, i * 2 + 2)

                stats(0, 0)
                norm(0, 0)
                norm(1, 1)
                take(0, 0)
                with dve.Fori(1, TILES // 2) as j:
                    norm(j * 2, 0)
                    take(j * 2 - 1, 1)
                    norm(j * 2 + 1, 1)
                    take(j * 2, 0)
                norm(TILES - 1, 0)
                take(TILES - 2, 1)
                take(TILES - 1, 0)
                link.n = base + TILES
                for a in range(2):
                    rest = PROD[:, 0:HIS * H].rearrange("p (hi h) -> p hi h", h=H)
                    for par in range(2):
                        full = c.score[:, a, :, par, :]
                        link(dve.tensor_copy(rest, full))
                        for k in range(3):
                            link(dve.tensor_copy(c.scores[:, k, a, par, :, :], rest))
                            if k < 2:
                                link(dve.tensor_tensor(rest, rest, c.scores[:, k, a, par, :, :], ALU.subtract))

            @block.tensor
            def _(pe):
                pe.wait_ge(step, 10)

                def turn(i, n):
                    pe.wait_ge(ahead, i + 1)
                    if not (isinstance(i, int) and i < 2):
                        pe.wait_ge(copied, i - 1)
                    for k in range(2):
                        last = pe.transpose(PT[:, n, k * P:(k + 1) * P], XN[:, n, k * P:(k + 1) * P], c.ident[:])
                    last.then_inc(turned, 1)

                def project(i, n):
                    pe.wait_ge(copied, i + 1)
                    if not (isinstance(i, int) and i < 2):
                        pe.wait_ge(taken_z, i - 1)
                        pe.wait_ge(taken_k, i * 2 - 2)
                    for k in range(2):
                        cols = XT[:, n, k, :]
                        pe.matmul(PZ[:, n, 0:D], cols, WZ[:, k, 0:D], start=k == 0, stop=k == 1)
                    for k in range(2):
                        cols = XT[:, n, k, :]
                        pe.matmul(PK[:, n, 0:D], cols, WQ[:, k, D:2 * D], start=k == 0, stop=k == 1)
                    for k in range(2):
                        cols = XT[:, n, k, :]
                        last = pe.matmul(PK[:, n, D:D + 2 * H], cols, WZ[:, k, D:D + 2 * H], start=k == 0, stop=k == 1)
                    last.then_inc(projected, 1)

                turn(0, 0)
                turn(1, 1)
                project(0, 0)
                with pe.Fori(1, TILES // 2) as j:
                    turn(j * 2, 0)
                    project(j * 2 - 1, 1)
                    turn(j * 2 + 1, 1)
                    project(j * 2, 0)
                turn(TILES - 1, 0)
                project(TILES - 2, 1)
                project(TILES - 1, 0)

            @block.scalar
            def _(act):
                def copy(i, n):
                    act.wait_ge(turned, i + 1)
                    if not (isinstance(i, int) and i < 2):
                        act.wait_ge(projected, i - 1)
                        act.wait_ge(xt_stored[n], x_count(i, n))
                    act.copy(XT[:, n, :, :], PT[:, n, 0:D].rearrange("p (k i) -> p k i", k=2)).then_inc(copied, 1)

                def take(i, n):
                    act.wait_ge(projected, i + 1)
                    if not (isinstance(i, int) and i < 2):
                        act.wait_ge(stored[n], i // 2 * 16 if isinstance(i, int) else (i - n) * 8)
                    act.copy(ZO[:, n, :, 0:D // H], PZ[:, n, 0:D].rearrange("p (h f) -> p h f", h=H)).then_inc(taken_z, 1)

                root = spreads(c, act, measured, rooted, MV)
                for i in range(2):
                    root(i, i)
                copy(0, 0)
                root(2, 0)
                copy(1, 1)
                root(3, 1)
                take(0, 0)
                copy(2, 0)
                root(4, 0)
                take(1, 1)
                copy(3, 1)
                root(5, 1)
                take(2, 0)
                with act.Fori(2, TILES // 2 - 1) as j:
                    copy(j * 2, 0)
                    root(j * 2 + 2, 0)
                    act.wait_ge(projected, j * 2)
                    act.wait_ge(stored[1], j * 16 - 16)
                    act.copy(ZO[:, 1, :, 0:D // H], PZ[:, 1, 0:D].rearrange("p (h f) -> p h f", h=H)).then_inc(taken_z, 1)
                    copy(j * 2 + 1, 1)
                    root(j * 2 + 3, 1)
                    act.wait_ge(projected, j * 2 + 1)
                    act.wait_ge(stored[0], j * 16)
                    act.copy(ZO[:, 0, :, 0:D // H], PZ[:, 0, 0:D].rearrange("p (h f) -> p h f", h=H)).then_inc(taken_z, 1)
                copy(TILES - 3, 0)
                root(TILES - 1, 0)
                take(TILES - 4, 1)
                copy(TILES - 2, 1)
                take(TILES - 3, 0)
                copy(TILES - 1, 0)
                take(TILES - 2, 1)
                take(TILES - 1, 0)

        cs, spread = sem("context_step"), sem("k_max_spread")
        xt_in = [sem("ctx_xt_in0"), sem("ctx_xt_in1")]
        kv, shifted, expd, v_copied, summed = (sem("ctx_" + n) for n in ("kv", "shifted", "exp", "v", "summed"))
        with ExitStack() as s2:
            KS = s2.enter_context(nc.sbuf_tensor("in_k_shifted", [P, 2, D], F32))
            KE = s2.enter_context(nc.sbuf_tensor("in_k_exp", [P, 2, D], F32))
            V = s2.enter_context(nc.sbuf_tensor("in_v", [P, 2, D], F32))
            PX = s2.enter_context(nc.psum_tensor("ps_in_k2", [P, 2, 512], F32))
            PV = s2.enter_context(nc.psum_tensor("ps_in_v", [P, 2, 512], F32))
            PC = s2.enter_context(nc.psum_tensor("ps_in_context", [P, 2, 512], F32))
            PS = s2.enter_context(nc.psum_tensor("ps_in_k_sum", [P, 2, 512], F32))
            PM = PC[:, 0, :]
            block = s2.enter_context(nc.Block())

            @block.gpsimd
            def _(pool):
                beside(pool, 8)

            @block.sync
            def _(sp):
                load = load_turned(sp, kv, xt_in)
                load(0, 0, True)
                load(1, 1, True)
                with sp.Fori(1, TILES // 2) as j:
                    load(j * 2, 0, False)
                    load(j * 2 + 1, 1, False)
                load(TILES - 1, 0, False)

            @block.tensor
            def _(pe):
                for k in range(2):
                    last = pe.transpose(PM[:, k * P:(k + 1) * P], KM[:, k * P:(k + 1) * P], c.ident[:])
                last.then_inc(spread, 1)
                pe.wait_ge(cs, 3)
                for k in range(2):
                    last = pe.matmul(PM[:, k * P:(k + 1) * P], c.ones[:], KD[:, k, :], start=True, stop=True)
                last.then_inc(spread, 1)

                def project(i, n):
                    if not (isinstance(i, int) and i < 2):
                        pe.wait_ge(shifted, i - 1)
                        pe.wait_ge(v_copied, i - 1)
                    pe.wait_ge(xt_in[n], x_count(i, n) + 16)
                    for k in range(2):
                        pe.matmul(PX[:, n, 0:D], XT[:, n, k, :], WQ[:, k, D:2 * D], start=k == 0, stop=k == 1)
                    for k in range(2):
                        last = pe.matmul(PV[:, n, 0:D], XT[:, n, k, :], WQ[:, k, 2 * D:3 * D], start=k == 0, stop=k == 1)
                    last.then_inc(kv, 1)

                def sum_up(i, n):
                    rows = LAST if isinstance(i, int) and i == TILES - 1 else P
                    pe.wait_ge(expd, i + 1)
                    pe.wait_ge(v_copied, i + 1)
                    first = isinstance(i, int) and i == 0
                    end = isinstance(i, int) and i == TILES - 1
                    for k in range(2):
                        cut = slice(k * P, (k + 1) * P)
                        pe.matmul(PC[:, k, 0:P], V[0:rows, n, cut], KE[0:rows, n, cut], start=first, stop=end,
                                  skip_group_check=True)
                        last = pe.matmul(PS[:, k, 0:1], KE[0:rows, n, cut], c.ones[0:rows, 0:1], start=first, stop=end,
                                         skip_group_check=True)
                    last.then_inc(summed, 1)

                project(0, 0)
                project(1, 1)
                sum_up(0, 0)
                with pe.Fori(1, TILES // 2) as j:
                    project(j * 2, 0)
                    sum_up(j * 2 - 1, 1)
                    project(j * 2 + 1, 1)
                    sum_up(j * 2, 0)
                project(TILES - 1, 0)
                sum_up(TILES - 2, 1)
                sum_up(TILES - 1, 0)
                pe.wait_ge(cs, 6)
                for k in range(2):
                    last = pe.matmul(PX[:, k, 0:D], CT[:, k, :], WO[:, k, :], start=True, stop=True)
                last.then_inc(spread, 1)

            @block.vector
            def _(dve):
                link = Chain(dve, cs)
                dve.wait_ge(spread, 1)
                link(dve.tensor_reduce(KMT[:], PM[:, 0:D].rearrange("p (k n) -> p k n", k=2), AX.X, ALU.max))
                for k in range(2):
                    link(dve.tensor_scalar(KD[:, k, :], c.ident[:], KMT[:, k:k + 1], None, ALU.mult))
                dve.wait_ge(spread, 2)
                link(dve.tensor_copy(KB[:], PM[:, 0:D]))

                def shift(i, n):
                    dve.wait_ge(kv, i + 1)
                    if not (isinstance(i, int) and i < 2):
                        dve.wait_ge(expd, i - 1)
                    dve.tensor_tensor(KS[:, n, :], PX[:, n, 0:D], KB[:], ALU.subtract).then_inc(shifted, 1)

                shift(0, 0)
                shift(1, 1)
                with dve.Fori(1, TILES // 2) as j:
                    shift(j * 2, 0)
                    shift(j * 2 + 1, 1)
                shift(TILES - 1, 0)
                dve.wait_ge(summed, TILES)
                for k in range(2):
                    link(dve.tensor_tensor(CT[:, k, :], PC[:, k, 0:P], c.blocks32[:], ALU.mult))
                for k in range(2):
                    link(dve.reciprocal(SUMS[:, k:k + 1], PS[:, k, 0:1]))
                dve.wait_ge(spread, 3)
                for k in range(2):
                    link(dve.tensor_scalar(CW[:, k, :], PX[:, k, 0:D], SUMS[:, k:k + 1], 32 ** -0.5, ALU.mult, ALU.mult))

            @block.scalar
            def _(act):
                def go(i, n):
                    act.wait_ge(kv, i + 1)
                    if not (isinstance(i, int) and i < 2):
                        act.wait_ge(summed, i - 1)
                    act.copy(V[:, n, :], PV[:, n, 0:D]).then_inc(v_copied, 1)
                    act.wait_ge(shifted, i + 1)
                    act.activation(KE[:, n, :], KS[:, n, :], ACT.Exp).then_inc(expd, 1)

                go(0, 0)
                go(1, 1)
                with act.Fori(1, TILES // 2) as j:
                    go(j * 2, 0)
                    go(j * 2 + 1, 1)
                go(TILES - 1, 0)

        ms = sem("mix_step")
        qt_in = [sem("mix_xt_in0"), sem("mix_xt_in1")]
        q_made, q_shift, q_exp, q_norm, q_turn, q_copied, mixed, mix_out = (
            sem("q_" + n) for n in ("made", "shift", "exp", "norm", "turn", "copied", "mixed", "out"))
        mix_stored = [sem("mix_stored0"), sem("mix_stored1")]
        mix_measured, logged, mix_rooted, mix_apart = (
            sem("mix_" + n) for n in ("measured", "logged", "rooted", "wait_apart"))
        with ExitStack() as s2:
            QM = s2.enter_context(nc.sbuf_tensor("in_q_max", [P, 8], F32))
            QE = s2.enter_context(nc.sbuf_tensor("in_q", [P, 2, D], F32))
            QT = s2.enter_context(nc.sbuf_tensor("in_q_turned", [P, 2, D], F32))
            ST = s2.enter_context(nc.sbuf_tensor("in_mstats", [P, 6], F32))
            MV = s2.enter_context(nc.sbuf_tensor("in_mmean_var", [P, 2], F32))
            MO = s2.enter_context(nc.sbuf_tensor("in_mix_out", [P, 2, D], F32))
            PQ = s2.enter_context(nc.psum_tensor("ps_in_q_ps", [P, 2, 512], F32))
            PT = s2.enter_context(nc.psum_tensor("ps_in_qt_ps", [P, 2, 512], F32))
            PM = s2.enter_context(nc.psum_tensor("ps_in_mix_ps", [P, 2, 512], F32))
            block = s2.enter_context(nc.Block())

            @block.gpsimd
            def _(pool):
                beside(pool, 25)

            @block.tensor
            def _(pe):
                def query(i, n):
                    if not (isinstance(i, int) and i < 2):
                        pe.wait_ge(q_shift, i - 1)
                    pe.wait_ge(qt_in[n], x_count(i, n) + 16)
                    for k in range(2):
                        last = pe.matmul(PQ[:, n, 0:D], XT[:, n, k, :], WQ[:, k, 0:D], start=k == 0, stop=k == 1)
                    last.then_inc(q_made, 1)

                def mix(i, n):
                    pe.wait_ge(q_norm, i + 1)
                    if not (isinstance(i, int) and i < 2):
                        pe.wait_ge(q_copied, i - 1)
                        pe.wait_ge(mix_out, i - 1)
                    for k in range(2):
                        last = pe.transpose(PT[:, n, k * P:(k + 1) * P], QE[:, n, k * P:(k + 1) * P], c.ident[:])
                    last.then_inc(q_turn, 1)
                    pe.wait_ge(q_copied, i + 1)
                    for k in range(2):
                        last = pe.matmul(PM[:, n, 0:D], QT[:, n, k * P:(k + 1) * P], CW[:, k, :], start=k == 0, stop=k == 1)
                    last.then_inc(mixed, 1)

                query(0, 0)
                query(1, 1)
                mix(0, 0)
                with pe.Fori(1, TILES // 2) as j:
                    query(j * 2, 0)
                    mix(j * 2 - 1, 1)
                    query(j * 2 + 1, 1)
                    mix(j * 2, 0)
                query(TILES - 1, 0)
                mix(TILES - 2, 1)
                mix(TILES - 1, 0)

            @block.scalar
            def _(act):
                def exp(i, n):
                    act.wait_ge(q_shift, i + 1)
                    act.activation(QE[:, n, :], QE[:, n, :], ACT.Exp).then_inc(q_exp, 1)

                def copy(i, n):
                    act.wait_ge(q_turn, i + 1)
                    if not (isinstance(i, int) and i < 2):
                        act.wait_ge(mixed, i - 1)
                    act.copy(QT[:, n, :], PT[:, n, 0:D]).then_inc(q_copied, 1)

                def root(i):
                    act.wait_ge(mix_measured, i + 1)
                    act.activation(MV[:, 1:2], MV[:, 1:2], ACT.Ln, bias=c.eps[:, 0:1]).then_inc(logged, 1)
                    act.wait_ge(logged, i + 1)
                    act.activation(MV[:, 1:2], MV[:, 1:2], ACT.Exp, scale=-0.5).then_inc(mix_rooted, 1)

                exp(0, 0)
                exp(1, 1)
                copy(0, 0)
                root(0)
                with act.Fori(1, TILES // 2) as j:
                    exp(j * 2, 0)
                    copy(j * 2 - 1, 1)
                    root(j * 2 - 1)
                    exp(j * 2 + 1, 1)
                    copy(j * 2, 0)
                    root(j * 2)
                exp(TILES - 1, 0)
                copy(TILES - 2, 1)
                root(TILES - 2)
                copy(TILES - 1, 0)
                root(TILES - 1)

            @block.vector
            def _(dve):
                link = Chain(dve, ms)
                PER_SHIFT, PER_NORM, PER_OUT = 1, 2, 3

                def heads(ap):
                    return ap.rearrange("p (h d) -> p h d", h=8)

                def spread8(ap):
                    return bcast(ap.unsqueeze(2), [P, 8, 32])

                def shift(i, n, at):
                    link.n = at
                    dve.wait_ge(q_made, i + 1)
                    link(dve.tensor_reduce(QM[:], heads(PQ[:, n, 0:D]), AX.X, ALU.max))
                    if not (isinstance(i, int) and i < 2):
                        dve.wait_ge(q_turn, i - 1)
                    dve.tensor_tensor(heads(QE[:, n, :]), heads(PQ[:, n, 0:D]), spread8(QM[:]), ALU.subtract).then_inc(q_shift, 1)
                    dve.wait_ge(q_shift, i + 1)

                def norm(i, n, at):
                    link.n = at
                    dve.wait_ge(q_exp, i + 1)
                    link(dve.tensor_reduce(QM[:], heads(QE[:, n, :]), AX.X, ALU.add))
                    link(dve.reciprocal(QM[:], QM[:]))
                    dve.tensor_tensor(heads(QE[:, n, :]), heads(QE[:, n, :]), spread8(QM[:]), ALU.mult).then_inc(q_norm, 1)
                    dve.wait_ge(q_norm, i + 1)

                def finish(i, n, at, before):
                    link.n = at
                    dve.wait_ge(mixed, i + 1)
                    link(dve.bn_stats(ST[:], PM[:, n, 0:D]))
                    stand_apart(dve, mix_apart)
                    dve.bn_aggr(MV[:], ST[:]).then_inc(mix_measured, 1)
                    dve.wait_ge(mix_rooted, i + 1)
                    if before is not None:
                        dve.wait_ge(mix_stored[n], before)
                    link(dve.tensor_scalar(MO[:, n, :], PM[:, n, 0:D], MV[:, 0:1], MV[:, 1:2], ALU.subtract, ALU.mult))
                    link(dve.tensor_tensor(MO[:, n, :], MO[:, n, :], GA[:], ALU.mult))
                    dve.tensor_tensor(MO[:, n, :], MO[:, n, :], X[:, bass.ds(i, 1), :].rearrange("p w d -> p (w d)"),
                                      ALU.add).then_inc(mix_out, 1)
                    dve.wait_ge(mix_out, i + 1)

                per = PER_SHIFT + PER_NORM + PER_OUT
                shift(0, 0, 0)
                norm(0, 0, 1)
                shift(1, 1, 3)
                norm(1, 1, 4)
                finish(0, 0, 6, None)
                shift(2, 0, 9)
                norm(2, 0, 10)
                finish(1, 1, 12, None)
                base = 15
                with dve.Fori(1, TILES // 2) as j:
                    a = (j - 1) * (2 * per) + base
                    shift(j * 2 + 1, 1, a)
                    norm(j * 2 + 1, 1, a + 1)
                    finish(j * 2, 0, a + 3, j * 16)
                    shift(j * 2 + 2, 0, a + per)
                    norm(j * 2 + 2, 0, a + per + 1)
                    finish(j * 2 + 1, 1, a + per + 3, j * 16)
                finish(TILES - 1, 0, base + 2 * per * (TILES // 2 - 1), 16 * (TILES // 2))

            @block.sync
            def _(sp):
                load = load_turned(sp, q_made, qt_in)

                def store(i, n):
                    sp.wait_ge(mix_out, i + 1)
                    sp.dma_start(rows(d["xm"], i), MO[:, n, :]).then_inc(mix_stored[n], 16)

                load(0, 0, True)
                load(1, 1, True)
                load(2, 0, False)
                store(0, 0)
                load(3, 1, False)
                store(1, 1)
                with sp.Fori(1, TILES // 2 - 1) as j:
                    load(j * 2 + 2, 0, False)
                    store(j * 2, 0)
                    load(j * 2 + 3, 1, False)
                    store(j * 2 + 1, 1)
                load(TILES - 1, 0, False)
                store(TILES - 3, 0)
                store(TILES - 2, 1)
                store(TILES - 1, 0)
                sp.wait_ge(mix_stored[0], 16 * (TILES // 2 + 1))
                sp.wait_ge(mix_stored[1], 16 * (TILES // 2))


class EdgeTables:

    def __init__(self, nc, kept, g):
        def keep(name, shape, dt=F32):
            return kept.enter_context(nc.sbuf_tensor(g.tag + name, shape, dt))

        self.dst = keep("_local_dst", [P, g.grid])
        self.src = keep("_src", [P, g.grid])
        self.chunk_i = keep("_chunk_of_step", [P, g.blocks], I32)
        self.window = keep("_window_of_step", [1, g.grid], I32)


def edge_tables(nc, c, sem, d, g, e, beside):
    t = g.tag
    B = g.blocks
    loaded, step, given = sem(t + "_rows_loaded"), sem(t + "_table_step"), sem(t + "_table_pe")
    stored = sem(t + "_tables_stored")
    fetched, fetched_before = c.pool_fetch[2], c.pool_fetch_before[2]
    c.pool_fetch_before[2] += 16 * B
    turned, taken = sem(t + "_cols_turned"), sem(t + "_cols_taken")
    with ExitStack() as s:
        def sb(name, shape, dt=F32):
            return s.enter_context(nc.sbuf_tensor(t + name, shape, dt))

        R = sb("_pair_rows", [P, B, P, 2])
        KI = sb("_keys_i", [P, B, P, 2], I32)
        KB = sb("_keys_b", [P, B, 2, P], BF16)
        ends = sb("_end_cols", [P, 2 * B])
        endT = sb("_end_rows", [2 * B, P])
        cmp1 = sb("_ended", [P, B, TILES + 1])
        sums = sb("_ended_sum", [P, 2, TILES + 1])
        win = sb("_window_edges", [P, TILES + 1])
        AB = sb("_chunks_at", [P, 2, TILES + 1])
        cnt = sb("_steps_of_window", [P, TILES])
        inc = sb("_steps_until", [P, TILES])
        off = sb("_step_offset", [P, TILES])
        doff = sb("_offset_change", [P, TILES])
        sid_i = sb("_step_id_i", [P, B], I32)
        sid = sb("_step_id", [P, B])
        past = sb("_past", [P, B, TILES])
        pastd = sb("_past_change", [P, B, TILES])
        wstep = sb("_window_f", [P, B])
        cstep = sb("_chunk_f", [P, B])
        wrow = sb("_window_rows", [B, P])
        wrow_i = sb("_window_rows_i", [B, P], I32)
        SR = sb("_step_rows", [P, B, P, 2])
        ps = s.enter_context(nc.psum_tensor(t + "_table_ps", [P, 2, 512], F32))
        pt = s.enter_context(nc.psum_tensor(t + "_cols_ps", [P, 2, 512], F32))
        made = sem(t + "_step_iota")
        block = s.enter_context(nc.Block())
        first, last = ends[:, 0:B], ends[:, B:2 * B]
        jobs = []
        for b in range(B):
            cols = slice(b * P, (b + 1) * P)
            jobs.append(([SR[:, b, :, 0]], e.src[:, cols], lambda a: a[:, 0:P]))
            jobs.append(([SR[:, b, :, 1]], e.dst[:, cols], lambda a: a[:, 0:P]))

        at = {}

        @block.vector
        def _(dve):
            link = Chain(dve, step)
            dve.wait_ge(loaded, 16)
            link(dve.tensor_scalar(R[:, :, :, 0], R[:, :, :, 0], float(N - 1), None, ALU.min))
            link(dve.tensor_copy(KI[:], R[:]))
            link(dve.tensor_scalar(KI[:], KI[:], 255, None, ALU.bitwise_and))
            link(dve.tensor_copy(KB[:].rearrange("p b k e -> p b e k"), KI[:]))
            link(dve.tensor_copy(first, R[:, :, 0, 1]))
            link(dve.tensor_copy(last, R[:, :, P - 1, 1]))
            dve.wait_ge(given, 1)
            link(dve.tensor_copy(endT[:], ps[0:2 * B, 0, 0:P]))
            link(dve.tensor_scalar(win[:], c.row[:, 0:TILES + 1], float(P), None, ALU.mult))
            for k, edge in enumerate((last, first)):
                link(dve.tensor_tensor(cmp1[:], bcast(edge.unsqueeze(2), [P, B, TILES + 1]),
                                       bcast(win[:].unsqueeze(1), [P, B, TILES + 1]), ALU.is_lt))
                link(dve.tensor_reduce(sums[:, k, :], cmp1[:].rearrange("p b w -> p w b"), AX.X, ALU.add))
            dve.wait_ge(given, 2)
            link(dve.tensor_copy(AB[:], ps[:, 1, 0:2 * (TILES + 1)].rearrange("p (k w) -> p k w", k=2)))
            link(dve.tensor_tensor(cnt[:], AB[:, 1, 1:TILES + 1], AB[:, 0, 0:TILES], ALU.subtract))
            link(dve.tensor_tensor_scan(inc[:], cnt[:], c.zeros[:, 0:TILES], 0.0, ALU.add, ALU.add))
            link(dve.tensor_tensor(off[:], AB[:, 0, 0:TILES], inc[:], ALU.subtract))
            link(dve.tensor_tensor(off[:], off[:], cnt[:], ALU.add))
            link(dve.memset(doff[:], 0.0))
            link(dve.tensor_tensor(doff[:, 0:TILES - 1], off[:, 1:TILES], off[:, 0:TILES - 1], ALU.subtract))
            dve.wait_ge(made, 1)
            link(dve.tensor_copy(sid[:], sid_i[:]))
            link(dve.tensor_tensor(past[:], bcast(sid[:].unsqueeze(2), [P, B, TILES]),
                                   bcast(inc[:].unsqueeze(1), [P, B, TILES]), ALU.is_ge))
            link(dve.tensor_reduce(wstep[:], past[:], AX.X, ALU.add))
            link(dve.tensor_tensor(pastd[:], past[:], bcast(doff[:].unsqueeze(1), [P, B, TILES]), ALU.mult))
            dve.wait_ge(given, 3)
            if g.in_psum:
                link(dve.tensor_scalar(wrow[:], ps[0:B, 0, 0:P], float(HIS), float(512 - HIS * g.row), ALU.is_ge, ALU.mult))
                link(dve.scalar_tensor_tensor(wrow_i[:], ps[0:B, 0, 0:P], float(g.row), wrow[:], ALU.mult, ALU.add))
            else:
                link(dve.tensor_copy(wrow_i[:], ps[0:B, 0, 0:P]))
            at["windows"] = link.n
            link(dve.tensor_reduce(cstep[:], pastd[:], AX.X, ALU.add))
            link(dve.tensor_tensor(cstep[:], cstep[:], sid[:], ALU.add))
            link(dve.tensor_scalar(cstep[:], cstep[:], off[:, 0:1], float(g.chunks - 1), ALU.add, ALU.min))
            link(dve.tensor_copy(e.chunk_i[:], cstep[:]))
            at["chunks"] = link.n
            link(dve.tensor_scalar(wstep[:], wstep[:], -float(P), None, ALU.mult))
            for b in range(B):
                if b == 0:
                    dve.wait_ge(fetched, 16 * B + fetched_before)
                link(dve.tensor_scalar(SR[:, b, :, 1], SR[:, b, :, 1], wstep[:, b:b + 1], None, ALU.add))
            at["step_rows"] = link.n

        @block.sync
        def _(sp):
            sp.dma_start(R[:].rearrange("p b e k -> p b (e k)"),
                         d[t + "_pairs"].rearrange("(b c e) k -> c b (e k)", c=P, e=P)).then_inc(loaded, 16)
            sp.wait_ge(step, 1)
            sp.dma_start(d[t + "_edge_rows"].rearrange("(b c) x -> c b x", c=P),
                         R[:].rearrange("p b e k -> p b (e k)")).then_inc(stored, 16)
            sp.wait_ge(step, 4)
            sp.dma_start(d[t + "_keys"].rearrange("(b c) x -> c b x", c=P),
                         KB[:].rearrange("p b k e -> p b (k e)")).then_inc(stored, 16)
            sp.wait_ge(step, 7)
            sp.dma_start(d[t + "_ends"].rearrange("k (b c) -> (k b) c", c=P), endT[:]).then_inc(stored, 16)
            sp.wait_ge(step, at["windows"])
            sp.dma_start(d[t + "_windows"].rearrange("(b c) -> b c", c=P), wrow_i[:]).then_inc(stored, 16)
            sp.wait_ge(stored, 64)
            sp.dma_start(e.window[:], d[t + "_windows"].rearrange("(o s) -> o s", o=1)).then_inc(loaded, 16)
            sp.wait_ge(loaded, 32)

        @block.gpsimd
        def _(pool):
            pool.iota(sid_i[:], [[P, B]], 0, 1).then_inc(made, 1)
            if beside:
                beside(pool, REST)
            pool.wait_ge(stored, 64)
            pool.wait_ge(step, at["chunks"])
            for b in range(B):
                pool.indirect_dma_start(out=SR[:, b, :, :].rearrange("p e k -> p (e k)"), out_offset=None,
                                        in_=d[t + "_edge_rows"],
                                        in_offset=bass.IndirectOffsetOnAxis(ap=e.chunk_i[:, b:b + 1], axis=0)
                                        ).then_inc(fetched, 16)

        @block.tensor
        def _(pe):
            pe.wait_ge(step, 6)
            pe.transpose(ps[0:2 * B, 0, 0:P], ends[:], c.ident[:]).then_inc(given, 1)
            pe.wait_ge(step, 12)
            pe.matmul(ps[:, 1, 0:2 * (TILES + 1)], c.ones[:], sums[:].rearrange("p k w -> p (k w)"),
                      start=True, stop=True).then_inc(given, 1)
            pe.wait_ge(step, 22)
            pe.transpose(ps[0:B, 0, 0:P], wstep[:], c.ident[:]).then_inc(given, 1)
            pe.wait_ge(step, at["step_rows"])
            transposes(nc, pe, None, jobs, pt, turned, taken, c.ident[:])

        @block.scalar
        def _(act):
            transposes(nc, None, act, jobs, pt, turned, taken, c.ident[:])


def edge_weights(nc, c, sem, d, g, beside):
    t = g.tag
    B, GR = g.blocks, g.grid
    with ExitStack() as s:
        ER = s.enter_context(nc.sbuf_tensor(t + "_scores_rows", [P, H, B, P], F32))
        look_up_scores(nc, c, sem, d, g, ER, beside)
        subtract_maximum(nc, c, sem, d, g, ER, beside)


def look_up_scores(nc, c, sem, d, g, ER, beside):
    t = g.tag
    B, GR = g.blocks, g.grid
    nb = g.batches
    CH = 4
    keys_in = [sem(t + "_keys_in%d" % i) for i in range(4)]
    onehot, looked, summed, hi_made = (sem(t + n) for n in ("_onehot", "_looked_up", "_score_masked", "_hi_made"))
    hturned, htaken = sem(t + "_hi_turned"), sem(t + "_hi_taken")
    turned, taken = sem(t + "_sc_turned"), sem(t + "_sc_taken")
    rows_in, hstep, picked = sem(t + "_rows_in"), sem(t + "_hi_step"), sem(t + "_score_picked")
    with ExitStack() as s2:
        def sb(name, shape, dt=F32):
            return s2.enter_context(nc.sbuf_tensor(t + name, shape, dt))

        EC = sb("_scores_cols", [P, GR, H])
        R = sb("_rows2", [P, B, P, 2])
        HIr = EC[:].rearrange("p s h -> p (s h)")[:, 0:GR * 2].bitcast(I32).rearrange("p (b e k) -> p b e k", b=B, k=2)
        HC = sb("_hi_cols", [P, GR, 2])
        KB = sb("_keys_everywhere", [P, 4, CH * 2 * P], BF16)
        OH = sb("_lo_onehot", [P, 2, 2, CH * 2 * P], BF16)
        HH = sb("_hi_onehot", [P, CH, 2 * HIS])
        PR = sb("_masked", [P, CH, 2 * HIS, H])
        pt = s2.enter_context(nc.psum_tensor(t + "_hi_ps", [P, 2, 512], F32))
        ps = s2.enter_context(nc.psum_tensor(t + "_lookup_ps", [P, 2, CH, 256], F32))
        block = s2.enter_context(nc.Block())
        jobs = [([R[:, b, :, k]], HC[:, b * P:(b + 1) * P, k], lambda a: a[:, 0:P]) for b in range(B) for k in range(2)]
        jobs2 = []
        for h in range(H):
            for b0 in range(0, B, 4):
                bs = list(range(b0, min(B, b0 + 4)))
                jobs2.append(([EC[:, b * P:(b + 1) * P, h] for b in bs],
                              ER[:, h, bs[0]:bs[-1] + 1, :].rearrange("p b e -> p (b e)"),
                              lambda a, n=len(bs): a[:, 0:n * P]))
        at = {}

        @block.vector
        def _(dve):
            link = Chain(dve, hstep)
            dve.wait_ge(rows_in, 16)
            link(dve.tensor_copy(HIr, R[:]))
            link(dve.tensor_scalar(HIr, HIr, 8, None, ALU.arith_shift_right))
            link(dve.tensor_copy(R[:], HIr))
            at["hi"] = link.n
            link(dve.memset(EC[:], 0.0))
            dve.wait_ge(htaken, len(jobs))

            def masks(i, n, m, j):
                dve.wait_ge(keys_in[n], j * 16 + 16)
                if not (isinstance(i, int) and i < 2):
                    dve.wait_ge(looked, i - 1)
                for par in range(2):
                    dve.tensor_scalar(OH[:, m, par, :], KB[:, n, :], c.lo[:, par:par + 1], None,
                                      ALU.is_equal).then_inc(onehot, 1)

            def pick(i, m):
                hc = HC[:, bass.ds(i * CH, CH), :]
                if not (isinstance(i, int) and i < 1):
                    dve.wait_ge(summed, i)
                dve.tensor_tensor(HH[:].rearrange("p u (k h) -> p (u k) h", k=2),
                                  bcast(hc.rearrange("p u k -> p (u k)").unsqueeze(2), [P, CH * 2, HIS]),
                                  bcast(c.row[:, 0:HIS].unsqueeze(1), [P, CH * 2, HIS]),
                                  ALU.is_equal).then_inc(hi_made, 1)
                dve.wait_ge(hi_made, i + 1)
                dve.wait_ge(looked, i + 1)
                if not (isinstance(i, int) and i < 1):
                    dve.wait_ge(picked, i)
                dve.tensor_tensor(PR[:], ps[:, m, :, 0:2 * HIS * H].rearrange("p u (x h) -> p u x h", h=H),
                                  bcast(HH[:].unsqueeze(3), [P, CH, 2 * HIS, H]), ALU.mult).then_inc(summed, 1)
                dve.wait_ge(summed, i + 1)
                dve.tensor_reduce(EC[:, bass.ds(i * CH, CH), :], PR[:].rearrange("p u x h -> p u h x"), AX.X,
                                  ALU.add).then_inc(picked, 1)

            for i in range(4):
                masks(i, i, i % 2, 0)
                if i:
                    pick(i - 1, (i - 1) % 2)
            with dve.Fori(1, nb // 4) as j:
                for n in range(4):
                    masks(j * 4 + n, n, n % 2, j)
                    pick(j * 4 + n - 1, (n - 1) % 2)
            pick(nb - 1, (nb - 1) % 2)
            dve.wait_ge(picked, nb)
            link(dve.scalar_tensor_tensor(EC[:], EC[:], g.slope, EC[:], ALU.mult, ALU.max))
            at["scores"] = link.n

        @block.sync
        def _(sp):
            sp.dma_start(R[:].rearrange("p b e k -> p b (e k)"),
                         d[t + "_edge_rows"].rearrange("(b c) x -> c b x", c=P)).then_inc(rows_in, 16)
            keys = d[t + "_keys"].rearrange("(n u) x -> n (u x)", u=CH)

            def load(i, n, first):
                if not first:
                    sp.wait_ge(onehot, i * 2 - 6)
                src_ = keys[bass.ds(i, 1), :].rearrange("n x -> (n x)").partition_broadcast(P)
                sp.dma_start(KB[:, n, :], src_).then_inc(keys_in[n], 16)

            for n in range(4):
                load(n, n, True)
            with sp.Fori(1, nb // 4) as j:
                for n in range(4):
                    load(j * 4 + n, n, False)

        @block.tensor
        def _(pe):
            pe.wait_ge(hstep, at["hi"])
            transposes(nc, pe, None, jobs, pt, hturned, htaken, c.ident[:])

            def look(i, m):
                pe.wait_ge(onehot, i * 2 + 2)
                if not (isinstance(i, int) and i < 2):
                    pe.wait_ge(summed, i - 1)
                for u in range(CH):
                    for k in range(2):
                        to = ps[:, m, u, k * HIS * H:(k + 1) * HIS * H]
                        for par in range(2):
                            for q in range(3):
                                last = pe.matmul(to, OH[:, m, par, (u * 2 + k) * P:(u * 2 + k + 1) * P],
                                                 c.scores[:, q, k, par, :, :].rearrange("p a h -> p (a h)"),
                                                 start=par == 0 and q == 0, stop=par == 1 and q == 2)
                last.then_inc(looked, 1)

            for i in range(4):
                look(i, i % 2)
            with pe.Fori(1, nb // 4) as j:
                for n in range(4):
                    look(j * 4 + n, n % 2)
            pe.wait_ge(hstep, at["scores"])
            pe.wait_ge(htaken, len(jobs))
            transposes(nc, pe, None, jobs2, pt, turned, taken, c.ident[:])

        @block.scalar
        def _(act):
            transposes(nc, None, act, jobs, pt, hturned, htaken, c.ident[:])
            transposes(nc, None, act, jobs2, pt, turned, taken, c.ident[:])

        @block.gpsimd
        def _(pool):
            beside(pool, g.beside_lookup)


def subtract_maximum(nc, c, sem, d, g, ER, beside):
    t = g.tag
    B, GR = g.blocks, g.grid
    step, given = sem(t + "_max_step"), sem(t + "_max_pe")
    loaded, stored, ends_in = sem(t + "_max_loaded"), sem(t + "_max_stored"), sem(t + "_ends_in")
    weights, saved = sem(t + "_weights"), sem(t + "_weights_saved")
    with ExitStack() as s2:
        def sb(name, shape, dt=F32):
            return s2.enter_context(nc.sbuf_tensor(t + name, shape, dt))

        X = [sb("_max_fwd", [P, H, B, P]), sb("_max_bwd", [P, H, B, P])]
        DR = sb("_dst_rows", [P, B, P])
        RS = [sb("_reset_fwd", [P, B, P]), sb("_reset_bwd", [P, B, P])]
        TC = sb("_tails_cols", [P, 2, H * B])
        TR = sb("_tails_rows", [H * B, 2, P])
        Q = 32 + H
        FL = sb("_ends_line", [Q, 2, GR])
        A, U, V = (X[1][0:Q, h].rearrange("p b c -> p (b c)") for h in range(3))
        pm = s2.enter_context(nc.psum_tensor(t + "_max_ps", [P, 2, 512], F32))
        block = s2.enter_context(nc.Block())
        fwd, bwd = slice(0, H), slice(32, 32 + H)
        pairs = X[0][:, 0:2].rearrange("p h b e -> p (h b e)").rearrange("p (b e k) -> p b e k", b=B, k=2)
        at = {}

        def flat(ap):
            return ap.rearrange("p b e -> p (b e)")

        def scans(dve, link):
            for h in range(H):
                a = flat(X[0][:, h])
                link(dve.tensor_tensor_scan(a, flat(RS[0][:]), a, -BIG, ALU.add, ALU.max))
                a = flat(X[1][:, h])[:, ::-1]
                link(dve.tensor_tensor_scan(a, flat(RS[1][:])[:, ::-1], a, -BIG, ALU.add, ALU.max))

        @block.vector
        def _(dve):
            link = Chain(dve, step)
            dve.wait_ge(ends_in, 48)
            link(dve.tensor_copy(DR[:], pairs[:, :, :, 1]))
            for k, r in enumerate(RS):
                link(dve.memset(r[:], 1.0))
                link(dve.tensor_tensor(r[:, :, 1 - k:P - k], DR[:, :, 1:P], DR[:, :, 0:P - 1], ALU.not_equal))
                link(dve.tensor_scalar(r[:], r[:], -BIG, None, ALU.mult))
            for k in range(2):
                link(dve.tensor_copy(X[k][:], ER[:]))
            scans(dve, link)
            link(dve.tensor_copy(TC[:, 0, :].rearrange("p (h b) -> p h b", h=H), X[0][:, :, :, P - 1]))
            link(dve.tensor_copy(TC[:, 1, :].rearrange("p (h b) -> p h b", h=H), X[1][:, :, :, 0]))
            at["tail_cols"] = link.n
            for part in (fwd, bwd):
                link(dve.tensor_tensor(V[part], FL[part, 0, :], FL[part, 1, :], ALU.is_equal))
                link(dve.tensor_tensor(U[part, 1:GR], FL[part, 0, 1:GR], FL[part, 1, 0:GR - 1], ALU.is_equal))
                link(dve.memset(U[part, 0:1], 0.0))
                link(dve.tensor_scalar(FL[part, 0, :], U[part], 1.0, BIG, ALU.subtract, ALU.mult))
            link(dve.tensor_tensor(A[fwd], V[fwd], U[fwd], ALU.mult))
            link(dve.memset(A[bwd], 0.0))
            link(dve.tensor_tensor(A[bwd, 0:GR - 1], V[bwd, 0:GR - 1], U[bwd, 1:GR], ALU.mult))
            for part in (fwd, bwd):
                link(dve.tensor_scalar(A[part], A[part], 1.0, BIG, ALU.subtract, ALU.mult))
            at["line_free"] = link.n
            dve.wait_ge(given, 1)
            link(dve.tensor_copy(TR[:], pm[0:H * B, 0, 0:2 * P].rearrange("p (k c) -> p k c", k=2)))
            at["tails"] = link.n
            dve.wait_ge(loaded, 32)
            a = U[fwd]
            link(dve.tensor_tensor_scan(a, A[fwd], a, -BIG, ALU.add, ALU.max))
            a = U[bwd][:, ::-1]
            link(dve.tensor_tensor_scan(a, A[bwd][:, ::-1], a, -BIG, ALU.add, ALU.max))
            for part in (fwd, bwd):
                link(dve.memset(V[part], -BIG))
            link(dve.tensor_tensor(V[fwd, 1:GR], U[fwd, 0:GR - 1], FL[fwd, 0, 1:GR], ALU.add))
            link(dve.tensor_tensor(V[bwd, 0:GR - 1], U[bwd, 1:GR], FL[bwd, 0, 1:GR], ALU.add))
            at["carries"] = link.n
            dve.wait_ge(given, 2)
            for k in range(2):
                link(dve.tensor_copy(X[k][:], ER[:]))
            for k in range(2):
                edge = X[k][:, :, :, (P - 1) * k]
                link(dve.tensor_tensor(edge, edge, pm[:, 1, k * H * B:(k + 1) * H * B].rearrange("p (h b) -> p h b", h=H), ALU.max))
            scans(dve, link)
            link(dve.tensor_tensor(X[0][:], X[0][:], X[1][:], ALU.max))
            link(dve.tensor_tensor(X[0][:], ER[:], X[0][:], ALU.subtract))
            at["shifted"] = link.n

        @block.sync
        def _(sp):
            sp.dma_start(pairs.rearrange("p b e k -> p b (e k)"),
                         d[t + "_edge_rows"].rearrange("(b c) x -> c b x", c=P)).then_inc(ends_in, 16)
            for part in (fwd, bwd):
                sp.dma_start(FL[part], d[t + "_ends"].partition_broadcast(H)).then_inc(ends_in, 16)
            sp.wait_ge(step, at["tails"])
            sp.dma_start(d[t + "_tails"].rearrange("k h (b c) -> (h b) k c", c=P), TR[:]).then_inc(stored, 16)
            sp.wait_ge(stored, 16)
            for k, part in enumerate((fwd, bwd)):
                sp.dma_start(U[part], d[t + "_tails"][k]).then_inc(loaded, 16)
            sp.wait_ge(step, at["carries"])
            for k, part in enumerate((fwd, bwd)):
                sp.dma_start(d[t + "_carries"][k], V[part]).then_inc(stored, 16)
            sp.wait_ge(stored, 48)
            sp.dma_start(TR[:], d[t + "_carries"].rearrange("k h (b c) -> (h b) k c", c=P)).then_inc(loaded, 16)
            sp.wait_ge(weights, 1)
            rows = d[t + "_weight_rows"].rearrange("(b c) (h e) -> h c b e", c=P, h=H)
            for h in range(H):
                sp.dma_start(rows[h], X[0][:, h]).then_inc(saved, 16)
            sp.wait_ge(saved, 64)

        @block.tensor
        def _(pe):
            pe.wait_ge(step, at["tail_cols"])
            for k in range(2):
                last = pe.transpose(pm[0:H * B, 0, k * P:(k + 1) * P], TC[:, k, :], c.ident[:])
            last.then_inc(given, 1)
            pe.wait_ge(loaded, 48)
            for k in range(2):
                last = pe.transpose(pm[:, 1, k * H * B:(k + 1) * H * B], TR[:, k, :], c.ident[0:H * B, 0:H * B])
            last.then_inc(given, 1)

        @block.scalar
        def _(act):
            act.wait_ge(step, at["shifted"])
            act.activation(X[0][:], X[0][:], ACT.Exp).then_inc(weights, 1)

        @block.gpsimd
        def _(pool):
            beside(pool, g.beside_maximum)


def fetch_weights(nc, s, c, sem, d, g, e):
    t = g.tag
    B = g.blocks
    W = s.enter_context(nc.sbuf_tensor(t + "_weights", [P, g.grid, H], F32))
    fetched, before = c.pool_fetch[0:2], c.pool_fetch_before[0:2]
    for n in range(2):
        c.pool_fetch_before[n] += 16 * ((B + 1 - n) // 2)
    turned, taken = sem(t + "_weights_turned"), sem(t + "_weights_taken")
    with ExitStack() as s2:
        WR = s2.enter_context(nc.sbuf_tensor(t + "_weight_rows_in", [P, 2, H * P], F32))
        pt = s2.enter_context(nc.psum_tensor(t + "_weights_ps", [P, 2, 512], F32))
        block = s2.enter_context(nc.Block())

        @block.gpsimd
        def _(pool):
            for b in range(B):
                if b >= 2:
                    pool.wait_ge(turned, b - 1)
                pool.indirect_dma_start(out=WR[:, b % 2, :], out_offset=None, in_=d[t + "_weight_rows"],
                                        in_offset=bass.IndirectOffsetOnAxis(ap=e.chunk_i[:, b:b + 1], axis=0)
                                        ).then_inc(fetched[b % 2], 16)

        @block.tensor
        def _(pe):
            for b in range(B):
                pe.wait_ge(fetched[b % 2], 16 * (b // 2 + 1) + before[b % 2])
                if b >= 2:
                    pe.wait_ge(taken, b - 1)
                for h in range(H):
                    last = pe.transpose(pt[:, b % 2, h * P:(h + 1) * P], WR[:, b % 2, h * P:(h + 1) * P], c.ident[:])
                last.then_inc(turned, 1)

        @block.scalar
        def _(act):
            for b in range(B):
                act.wait_ge(turned, b + 1)
                act.copy(W[:, b * P:(b + 1) * P, :].rearrange("p s h -> p h s"),
                         pt[:, b % 2, :].rearrange("p (h s) -> p h s", h=H)).then_inc(taken, 1)
    return W


def aggregate(nc, ctx, c, sem, d, g, e):
    t = g.tag
    F = g.width + 1
    ACC = ctx.enter_context(nc.sbuf_tensor(t + "_sums", [P, TILES + 1, g.row], F32))
    AH = 3
    act_apart, scaled_too = sem(t + "_act_wait_apart"), sem(t + "_rows_scaled_too")
    cleared, pool_apart, staged, scaled, multiplied, added = (
        sem(t + n) for n in ("_sums_cleared", "_pool_wait_apart", "_index_staged", "_rows_scaled", "_step_summed", "_step_added"))
    got = c.ring_done[t + "_gather"]
    loops = g.steps // UNROLL
    Q = UNROLL // len(got)
    BUF = 4
    with ExitStack() as s2:
        W = fetch_weights(nc, s2, c, sem, d, g, e)
        slot = s2.enter_context(nc.sbuf_tensor(t + "_index_slots", [P, UNROLL], I32))
        G = s2.enter_context(nc.sbuf_tensor(t + "_gathered", [P, UNROLL, g.row], F32))
        ZW = s2.enter_context(nc.sbuf_tensor(t + "_scaled", [P, BUF, g.row], F32))
        OH = s2.enter_context(nc.sbuf_tensor(t + "_dst_onehot", [P, BUF, P], F32))
        ps = s2.enter_context(nc.psum_tensor(t + "_step_ps", [P, BUF, 512], F32))
        block = s2.enter_context(nc.Block())

        @block.scalar
        def _(act):
            def scale(i, u, first):
                st = i * UNROLL + u
                if not (first and u < BUF):
                    act.wait_ge(multiplied, st - (BUF - 1))
                    stand_apart(act, act_apart)
                if u % Q == 0:
                    act.wait_ge(got[u // Q], i * (16 * Q) + 16 * Q)
                    stand_apart(act, act_apart)
                for h in range(AH):
                    last = act.activation(ZW[:, u % BUF, h * F:(h + 1) * F], G[:, u, h * F:(h + 1) * F], ACT.Copy,
                                          scale=W[:, bass.ds(st, 1), h])
                last.then_inc(scaled_too, 1)

            for u in range(UNROLL):
                scale(0, u, True)
            with act.Fori(1, loops) as i:
                for u in range(UNROLL):
                    scale(i, u, False)

        @block.gpsimd
        def _(pool):
            def gather(i, k, first):
                lo = k * Q
                if not first:
                    for q in (scaled, scaled_too):
                        pool.wait_ge(q, i * UNROLL + (lo + Q - UNROLL))
                        stand_apart(pool, pool_apart)
                pool.tensor_copy(slot[:, lo:lo + Q], e.src[:, bass.ds(i * UNROLL + lo, Q)]).then_inc(staged, 1)
                pool.wait_ge(staged, i * (UNROLL // Q) + (k + 1))
                stand_apart(pool, pool_apart)
                for u in range(lo, lo + Q):
                    pool.indirect_dma_start(out=G[:, u, :], out_offset=None, in_=d[t + "_rows"],
                                            in_offset=bass.IndirectOffsetOnAxis(ap=slot[:, u:u + 1], axis=0)
                                            ).then_inc(got[k], 16)

            for k in range(UNROLL // Q):
                gather(0, k, True)
            with pool.Fori(1, loops) as i:
                for k in range(UNROLL // Q):
                    gather(i, k, False)

        @block.vector
        def _(dve):
            dve.memset(ACC[:], 0.0).then_inc(cleared, 1)
            dve.wait_ge(cleared, 1)

            def scale(i, u, first):
                st = i * UNROLL + u
                if not (first and u < BUF):
                    dve.wait_ge(multiplied, st - (BUF - 1))
                dve.tensor_scalar(OH[:, u % BUF, :], c.row[:], e.dst[:, bass.ds(st, 1)], None, ALU.is_equal)
                if u % Q == 0:
                    dve.wait_ge(got[u // Q], i * (16 * Q) + 16 * Q)
                dve.tensor_scalar(ZW[:, u % BUF, AH * F:H * F], G[:, u, AH * F:H * F], W[:, bass.ds(st, 1), AH], None,
                                  ALU.mult).then_inc(scaled, 1)

            def add(i, u, first, w):
                st = i * UNROLL + u
                to = ACC[:, bass.ds(w, 1), :].rearrange("p w f -> p (w f)")
                dve.wait_ge(multiplied, st + 1)
                if not (first and u == 0):
                    dve.wait_ge(added, st)
                dve.tensor_tensor(to, to, ps[:, u % BUF, 0:g.row], ALU.add).then_inc(added, 1)

            def group(i, first):
                _, windows = nc.values_load_multi_w_load_instructions(e.window[0:1, bass.ds(i * UNROLL, UNROLL)],
                                               engines=[mybir.EngineType.DVE], min_val=0, max_val=TILES,
                                               skip_runtime_bounds_check_because="counts of windows passed")
                for u in range(UNROLL):
                    scale(i, u, first)
                    if u >= 2:
                        add(i, u - 2, first, windows[u - 2])
                for u in range(UNROLL - 2, UNROLL):
                    add(i, u, first, windows[u])

            group(0, True)
            with dve.Fori(1, loops) as i:
                group(i, False)
            dve.wait_ge(added, g.steps)

        @block.tensor
        def _(pe):
            def group(i, first):
                for u in range(UNROLL):
                    st = i * UNROLL + u
                    pe.wait_ge(scaled, st + 1)
                    pe.wait_ge(scaled_too, st + 1)
                    if not (first and u < BUF):
                        pe.wait_ge(added, st - (BUF - 1))
                    pe.matmul(ps[:, u % BUF, 0:g.row], OH[:, u % BUF, :], ZW[:, u % BUF, :], start=True,
                              stop=True).then_inc(multiplied, 1)

            group(0, True)
            with pe.Fori(1, loops) as i:
                group(i, False)
    return ACC


class Gather:

    def __init__(self, nc, kept, c, d, g, e):
        t = g.tag
        self.rows, self.src, self.loops, self.done_loops = d[t + "_rows"], e.src, g.steps // UNROLL, 0
        self.out = kept.enter_context(nc.sbuf_tensor(t + "_gathered", [P, g.steps, g.width * H], F32))
        self.slot = kept.enter_context(nc.sbuf_tensor(t + "_slot_index", [P, UNROLL], I32))
        self.room = kept.enter_context(nc.sbuf_tensor(t + "_slot_rows", [P, UNROLL, g.width * H], F32))
        self.staged, self.moved, self.apart = (c.held.enter_context(nc.semaphore(t + n)) for n in (
            "_slots_staged", "_rows_moved", "_gather_wait_apart"))
        self.got = c.ring_done[t + "_gather"]

    def issue(self, pool, i, k):
        lo = k * RING
        pool.tensor_copy(self.slot[:, lo:lo + RING], self.src[:, bass.ds(i * UNROLL + lo, RING)]
                         ).then_inc(self.staged, 1)
        pool.wait_ge(self.staged, i * 2 + (k + 1))
        stand_apart(pool, self.apart)
        for u in range(lo, lo + RING):
            pool.indirect_dma_start(out=self.room[:, u, :], out_offset=None, in_=self.rows,
                                    in_offset=bass.IndirectOffsetOnAxis(ap=self.slot[:, u:u + 1], axis=0)
                                    ).then_inc(self.got[k], 16)

    def move(self, pool, i, k):
        lo = k * RING
        pool.wait_ge(self.got[k], i * (16 * RING) + 16 * RING)
        stand_apart(pool, self.apart)
        pool.tensor_copy(self.out[:, bass.ds(i * UNROLL + lo, RING), :], self.room[:, lo:lo + RING, :]
                         ).then_inc(self.moved, 1)
        pool.wait_ge(self.moved, i * 2 + (k + 1))
        stand_apart(pool, self.apart)

    def share(self, pool, loops):
        i, end = self.done_loops, min(self.loops, self.done_loops + loops)
        if i == 0:
            for k in range(2):
                self.issue(pool, 0, k)
            i = 1
        if i < end:
            with pool.Fori(i, end) as i:
                for k in range(2):
                    self.move(pool, i - 1, k)
                    self.issue(pool, i, k)
        if end == self.loops and self.done_loops < end:
            for k in range(2):
                self.move(pool, end - 1, k)
        self.done_loops = end


def add_up(nc, kept, c, sem, d, g, e, gather):
    t = g.tag
    F = g.width
    S = 8
    ACC = kept.enter_context(nc.sbuf_tensor(t + "_sums", [P, 2 * HIS, g.row], F32))
    act_apart = sem(t + "_act_wait_apart")
    masked, scaled, weighed, zeroed, multiplied, whole = (
        sem(t + n) for n in ("_masked", "_scaled", "_weighed", "_zeroed", "_multiplied", "_whole"))
    loops = g.steps // UNROLL
    with ExitStack() as s2:
        W = fetch_weights(nc, s2, c, sem, d, g, e)
        ZW = s2.enter_context(nc.sbuf_tensor(t + "_scaled_rows", [P, 2, S, H, F + 1], F32))
        OH = s2.enter_context(nc.sbuf_tensor(t + "_dst_onehot", [P, 2, S, P], F32))
        ps = s2.enter_context(nc.psum_tensor(t + "_sums_ps", [P, 2 * 512], F32))
        block = s2.enter_context(nc.Block())

        def rounds(engine, batch):
            for k in range(2):
                batch(0, k, True)
            with engine.Fori(1, loops) as i:
                for k in range(2):
                    batch(i, k, False)

        @block.vector
        def _(dve):
            def batch(i, k, first):
                at = bass.ds(i * UNROLL + k * S, S)
                if not first:
                    dve.wait_ge(multiplied, i * 2 + (k - 1))
                dve.tensor_tensor(OH[:, k], bcast(e.dst[:, at].unsqueeze(2), [P, S, P]),
                                  bcast(c.row[:].unsqueeze(1), [P, S, P]), ALU.is_equal).then_inc(masked, 1)
                dve.wait_ge(gather.moved, i * 2 + (k + 1))
                dve.tensor_tensor(ZW[:, k, :, :, 0:F], gather.out[:, at, :].rearrange("p s (h f) -> p s h f", h=H),
                                  bcast(W[:, at, :].unsqueeze(3), [P, S, H, F]), ALU.mult).then_inc(scaled, 1)

            rounds(dve, batch)
            dve.wait_ge(whole, 1)
            for k in range(2):
                dve.tensor_copy(ACC[:, k * HIS:(k + 1) * HIS, :],
                                ps[:, k * 512:k * 512 + HIS * g.row].rearrange("p (w f) -> p w f", f=g.row))

        @block.scalar
        def _(act):
            def batch(i, k, first):
                if not first:
                    act.wait_ge(multiplied, i * 2 + (k - 1))
                    stand_apart(act, act_apart)
                act.copy(ZW[:, k, :, :, F], W[:, bass.ds(i * UNROLL + k * S, S), :]).then_inc(weighed, 1)

            rounds(act, batch)

        @block.gpsimd
        def _(pool):
            gather.share(pool, REST)

        @block.tensor
        def _(pe):
            for k in range(2):
                last = pe.matmul(ps[:, k * 512:(k + 1) * 512], c.zeros[:, 0:P], c.zeros[:, 0:512], start=True, stop=False,
                                 skip_group_check=True)
            last.then_inc(zeroed, 1)
            pe.wait_ge(zeroed, 1)

            def batch(i, k, first):
                _, at = nc.values_load_multi_w_load_instructions(e.window[0:1, bass.ds(i * UNROLL + k * S, S)],
                                          engines=[mybir.EngineType.PE], min_val=0, max_val=1024 - g.row,
                                          skip_runtime_bounds_check_because="places of the windows passed")
                for q in (masked, scaled, weighed):
                    pe.wait_ge(q, i * 2 + (k + 1))
                for u in range(S):
                    last = pe.matmul(ps[:, bass.ds(at[u], g.row)], OH[:, k, u, :],
                                     ZW[:, k, u].rearrange("p h f -> p (h f)"), start=False, stop=False,
                                     skip_group_check=True)
                last.then_inc(multiplied, 1)

            rounds(pe, batch)
            pe.wait_ge(multiplied, 2 * loops)
            pe.sem_inc(whole, 1)
    return ACC


def nodes_between(nc, c, sem, d, acc, wgat, fas, fad):
    W = D // H
    E = 4
    step, loaded, made, x_out, turned, copied, projected, taken = (
        sem("mid_" + n) for n in ("step", "loaded", "xn", "x1", "turned", "copied", "projected", "taken"))
    measured, rooted, apart = sem("mid_measured"), sem("mid_rooted"), sem("mid_wait_apart")
    xm_in = [sem("mid_xm_in0"), sem("mid_xm_in1")]
    x_stored = [sem("mid_x_stored0"), sem("mid_x_stored1")]
    h_stored = [sem("mid_h_stored0"), sem("mid_h_stored1")]
    with ExitStack() as s:
        def sb(name, shape, dt=F32):
            return s.enter_context(nc.sbuf_tensor("mid_" + name, shape, dt))

        WG = sb("w_gat", [P, 2, 24])
        AT = sb("att", [P, 2, 16])
        PR = sb("att_products", [P, 16])
        XM = sb("xm", [P, 2, D])
        X1 = sb("x1", [P, 2, D])
        XN = sb("xn", [P, 2, D])
        XT = sb("xn_turned", [P, 2, D])
        DEN = sb("den", [P, H])
        ST = sb("stats", [P, 6])
        MV = sb("mean_var", [P, 2, 2])
        HO = sb("h_out", [P, 2, H * E])
        REST = sb("rest", [P, HIS, H])
        PT = s.enter_context(nc.psum_tensor("mid_turn_ps", [P, 2, 512], F32))
        PH = s.enter_context(nc.psum_tensor("mid_h_ps", [P, 2, 512], F32))
        block = s.enter_context(nc.Block())
        at = {}

        @block.vector
        def _(dve):
            link = Chain(dve, step)
            dve.wait_ge(loaded, 48)
            for k in range(2):
                for a in range(2):
                    link(dve.tensor_tensor(PR[:], WG[:, k, 0:16], AT[:, a, :], ALU.mult))
                    link(dve.tensor_reduce(WG[:, k, 16 + H * a:16 + H * (a + 1)],
                                           PR[:].rearrange("p (h e) -> p h e", h=H), AX.X, ALU.add))
            at["w"] = base = link.n

            def node(i, n, first):
                link.n = i * 6 + base
                cut = acc[:, bass.ds(i, 1), :].rearrange("p w (h f) -> p (w h) f", h=H)
                link(dve.tensor_scalar(DEN[:].unsqueeze(2), cut[:, :, W:W + 1], 1e-30, None, ALU.max))
                link(dve.reciprocal(DEN[:], DEN[:]))
                if not first:
                    dve.wait_ge(x_stored[n], x_count(i, n))
                x3 = X1[:, n, :].rearrange("p (h f) -> p h f", h=H)
                link(dve.tensor_tensor(x3, cut[:, :, 0:W], bcast(DEN[:].unsqueeze(2), [P, H, W]), ALU.mult))
                dve.wait_ge(xm_in[n], x_count(i, n) + 16)
                dve.tensor_tensor(X1[:, n, :], X1[:, n, :], XM[:, n, :], ALU.add).then_inc(x_out, 1)
                dve.wait_ge(x_out, i + 1)
                mv = MV[:, n, :]
                measure(nc, link, ST[:], mv, X1[:, n, :], measured, apart, i)
                if not first:
                    dve.wait_ge(turned, i - 1)
                dve.wait_ge(rooted, i + 1)
                link(dve.reciprocal(mv[:, 1:2], mv[:, 1:2]))
                link(dve.tensor_scalar(c.spread[:, bass.ds(i, 1), :].rearrange("p w s -> p (w s)"), mv, 1.0, None,
                                       ALU.mult))
                dve.tensor_scalar(XN[:, n, :], X1[:, n, :], mv[:, 0:1], mv[:, 1:2], ALU.subtract, ALU.mult).then_inc(made, 1)
                dve.wait_ge(made, i + 1)

            def take(i, n, first):
                dve.wait_ge(projected, i + 1)
                out_ = c.score[:].rearrange("p a hi par h -> p a (hi par) h")[:, :, bass.ds(i, 1), :].rearrange("p a w h -> p a (w h)")
                dve.tensor_copy(out_, PH[:, n, 16:24].rearrange("p (a h) -> p a h", a=2)).then_inc(taken, 1)
                if not first:
                    dve.wait_ge(h_stored[n], x_count(i, n))
                dve.tensor_copy(HO[:, n, :], PH[:, n, 0:16]).then_inc(taken, 1)

            node(0, 0, True)
            node(1, 1, True)
            take(0, 0, True)
            node(2, 0, False)
            take(1, 1, True)
            with dve.Fori(1, TILES // 2) as j:
                node(j * 2 + 1, 1, False)
                take(j * 2, 0, False)
                node(j * 2 + 2, 0, False)
                take(j * 2 + 1, 1, False)
            take(TILES - 1, 0, False)
            dve.wait_ge(taken, 2 * TILES)
            link.n = base + 6 * TILES
            for a in range(2):
                for par in range(2):
                    link(dve.tensor_copy(REST[:], c.score[:, a, :, par, :]))
                    for k in range(3):
                        link(dve.tensor_copy(c.scores[:, k, a, par, :, :], REST[:]))
                        if k < 2:
                            link(dve.tensor_tensor(REST[:], REST[:], c.scores[:, k, a, par, :, :], ALU.subtract))

        @block.sync
        def _(sp):
            sp.dma_start(WG[:, :, 0:16], wgat.rearrange("(k i) e -> i k e", k=2)).then_inc(loaded, 16)
            sp.dma_start(AT[:, 0, :], fas.rearrange("h e -> (h e)").partition_broadcast(P)).then_inc(loaded, 16)
            sp.dma_start(AT[:, 1, :], fad.rearrange("h e -> (h e)").partition_broadcast(P)).then_inc(loaded, 16)

            def rows(ap, i):
                return ap.rearrange("(w i) d -> w i d", i=P)[bass.ds(i, 1)].rearrange("w i d -> (w i) d")

            def load(i, n, first):
                if not first:
                    sp.wait_ge(x_out, i - 1)
                sp.dma_start(XM[:, n, :], rows(d["xm"], i)).then_inc(xm_in[n], 16)

            def store(i, n):
                sp.wait_ge(x_out, i + 1)
                sp.dma_start(rows(d["x1"], i), X1[:, n, :]).then_inc(x_stored[n], 16)
                sp.wait_ge(taken, i * 2 + 2)
                sp.dma_start(rows(d["ffn_rows"], i), HO[:, n, :]).then_inc(h_stored[n], 16)

            load(0, 0, True)
            load(1, 1, True)
            load(2, 0, False)
            store(0, 0)
            load(3, 1, False)
            store(1, 1)
            with sp.Fori(1, TILES // 2 - 1) as j:
                load(j * 2 + 2, 0, False)
                store(j * 2, 0)
                load(j * 2 + 3, 1, False)
                store(j * 2 + 1, 1)
            load(TILES - 1, 0, False)
            store(TILES - 3, 0)
            store(TILES - 2, 1)
            store(TILES - 1, 0)
            for q in (x_stored, h_stored):
                sp.wait_ge(q[0], 16 * (TILES // 2 + 1))
                sp.wait_ge(q[1], 16 * (TILES // 2))

        @block.tensor
        def _(pe):
            pe.wait_ge(step, at["w"])

            def turn(i, n, first):
                pe.wait_ge(made, i + 1)
                if not first:
                    pe.wait_ge(copied, i - 1)
                for k in range(2):
                    last = pe.transpose(PT[:, n, k * P:(k + 1) * P], XN[:, n, k * P:(k + 1) * P], c.ident[:])
                last.then_inc(turned, 1)

            def project(i, n, first):
                pe.wait_ge(copied, i + 1)
                if not first:
                    pe.wait_ge(taken, i * 2 - 2)
                for k in range(2):
                    last = pe.matmul(PH[:, n, 0:24], XT[:, n, k * P:(k + 1) * P], WG[:, k, :], start=k == 0, stop=k == 1)
                last.then_inc(projected, 1)

            turn(0, 0, True)
            turn(1, 1, True)
            project(0, 0, True)
            turn(2, 0, False)
            project(1, 1, True)
            with pe.Fori(1, TILES // 2) as j:
                turn(j * 2 + 1, 1, False)
                project(j * 2, 0, False)
                turn(j * 2 + 2, 0, False)
                project(j * 2 + 1, 1, False)
            project(TILES - 1, 0, False)

        @block.scalar
        def _(act):
            def copy(i, n, first):
                act.wait_ge(turned, i + 1)
                if not first:
                    act.wait_ge(projected, i - 1)
                act.copy(XT[:, n, :], PT[:, n, 0:D]).then_inc(copied, 1)

            root = spreads(c, act, measured, rooted, MV)
            root(0, 0)
            root(1, 1)
            copy(0, 0, True)
            root(2, 0)
            copy(1, 1, True)
            with act.Fori(1, TILES // 2) as j:
                root(j * 2 + 1, 1)
                copy(j * 2, 0, False)
                root(j * 2 + 2, 0)
                copy(j * 2 + 1, 1, False)
            copy(TILES - 1, 0, False)


def x_count(i, n):
    return i // 2 * 16 if isinstance(i, int) else (i - n) * 8


def gates(nc, c, sem, acc, gate, bgat, lng, lnb):
    step, loaded, rooted, expd = sem("gate_step"), sem("gate_loaded"), sem("gate_rooted"), sem("gate_exp")
    E = 4
    with ExitStack() as s:
        def sb(name, shape):
            return s.enter_context(nc.sbuf_tensor("gate_" + name, shape, F32))

        BP = sb("b_gamma_beta", [P, 3, 16])
        A = sb("agg", [P, TILES, 16])
        SQ = sb("squares", [P, TILES, 16])
        DEN = sb("den", [P, TILES, H])
        M = sb("mean", [P, TILES])
        V = sb("var", [P, TILES])
        SC = sb("scores", [P, TILES, E])
        RK = sb("rank", [P, TILES, E])
        C1 = sb("cmp", [P, TILES])
        SUM = sb("sum", [P, TILES])
        block = s.enter_context(nc.Block())
        at = {}

        @block.vector
        def _(dve):
            link = Chain(dve, step)
            dve.wait_ge(loaded, 48)
            a4 = acc[:, 0:TILES, :].rearrange("p w (h f) -> p w h f", h=H)
            A4 = A[:].rearrange("p w (h e) -> p w h e", h=H)

            def row(k):
                return bcast(BP[:, k, :].unsqueeze(1), [P, TILES, 16])

            def tile(ap, n=16):
                return bcast(ap.unsqueeze(2), [P, TILES, n])

            link(dve.tensor_scalar(DEN[:].unsqueeze(3), a4[:, :, :, E:E + 1], 1e-16, None, ALU.add))
            link(dve.reciprocal(DEN[:], DEN[:]))
            link(dve.tensor_tensor(A4, a4[:, :, :, 0:E], bcast(DEN[:].unsqueeze(3), [P, TILES, H, E]), ALU.mult))
            link(dve.tensor_tensor(A[:], A[:], row(0), ALU.add))
            link(dve.tensor_reduce(M[:], A[:], AX.X, ALU.add))
            link(dve.tensor_scalar(M[:], M[:], 1.0 / 16, None, ALU.mult))
            link(dve.tensor_tensor(A[:], A[:], tile(M[:]), ALU.subtract))
            link(dve.tensor_tensor(SQ[:], A[:], A[:], ALU.mult))
            link(dve.tensor_reduce(V[:], SQ[:], AX.X, ALU.add))
            at["squared"] = link.n
            dve.wait_ge(rooted, 1)
            link(dve.reciprocal(V[:], V[:]))
            link(dve.tensor_tensor(A[:], A[:], tile(V[:]), ALU.mult))
            link(dve.tensor_tensor(A[:], A[:], row(1), ALU.mult))
            link(dve.tensor_tensor(A[:], A[:], row(2), ALU.add))
            link(dve.tensor_reduce(SC[:], A[:].rearrange("p w (h e) -> p w e h", h=H), AX.X, ALU.add))
            link(dve.tensor_scalar(SC[:], SC[:], 1.0 / H, None, ALU.mult))
            link(dve.memset(RK[:], 0.0))
            for a in range(E):
                for b in range(E):
                    if a != b:
                        op = ALU.is_ge if b < a else ALU.is_gt
                        link(dve.tensor_tensor(C1[:], SC[:, :, b], SC[:, :, a], op))
                        link(dve.tensor_tensor(RK[:, :, a], RK[:, :, a], C1[:], ALU.add))
            link(dve.tensor_scalar(RK[:], RK[:], 2.0, None, ALU.is_lt))
            link(dve.tensor_reduce(M[:], SC[:], AX.X, ALU.max))
            link(dve.tensor_tensor(SC[:], SC[:], tile(M[:], E), ALU.subtract))
            at["shifted"] = link.n
            dve.wait_ge(expd, 1)
            link(dve.tensor_tensor(SC[:], SC[:], RK[:], ALU.mult))
            link(dve.tensor_reduce(SUM[:], SC[:], AX.X, ALU.add))
            link(dve.reciprocal(SUM[:], SUM[:]))
            link(dve.tensor_tensor(gate[:], SC[:], tile(SUM[:], E), ALU.mult))

        @block.sync
        def _(sp):
            for k, a in enumerate((bgat, lng, lnb)):
                sp.dma_start(BP[:, k, :], a.partition_broadcast(P)).then_inc(loaded, 16)

        @block.scalar
        def _(act):
            act.wait_ge(step, at["squared"])
            act.activation(V[:], V[:], ACT.Sqrt, bias=c.eps[:, 0:1], scale=1.0 / 16).then_inc(rooted, 1)
            act.wait_ge(step, at["shifted"])
            act.activation(SC[:], SC[:], ACT.Exp).then_inc(expd, 1)


def experts(nc, c, sem, d, out, gate, w1, b1, w2, b2):
    E, HID, GT = 4, 512, 4
    HC = HID // P
    FULL = TILES // GT
    assert TILES == FULL * GT + 1 and FULL % 2 == 0
    PG = GT * E
    step, loaded, prepared, made, turned, copied, hidden, gelu, product, added = (
        sem("exp_" + n) for n in ("step", "loaded", "prepared", "xn", "turned", "copied", "hidden", "gelu", "product",
                                  "added"))
    x_in = [sem("exp_x_in0"), sem("exp_x_in1")]
    stored = [sem("exp_stored0"), sem("exp_stored1")]
    with ExitStack() as s:
        def sb(name, shape, dt=F32):
            return s.enter_context(nc.sbuf_tensor("exp_" + name, shape, dt))

        W1 = sb("w1", [P, E, 2, HID])
        W2 = sb("w2", [P, E, HC, D])
        B1 = sb("b1", [P, E, HC])
        B2 = sb("b2", [P, E, D])
        X = sb("x", [P, 2, GT, D])
        XN = sb("xn", [P, GT, D])
        XT = sb("xn_turned", [P, 2, 2, GT * P])
        HT = sb("hidden", [P, 2, HC, GT * P])
        O = sb("out", [P, 2, GT, D])
        PT = s.enter_context(nc.psum_tensor("exp_turn_ps", [P, 2, 512], F32))
        PH = s.enter_context(nc.psum_tensor("exp_hidden_ps", [P, 2, 512], F32))
        PO = s.enter_context(nc.psum_tensor("exp_out_ps", [P, 2, 512], F32))
        block = s.enter_context(nc.Block())

        def groups(engine, body):
            body(0, 0, GT, GT)
            with engine.Fori(0, FULL // 2 - 1) as j:
                body(j * 2 + 1, 1, GT, GT)
                body(j * 2 + 2, 0, GT, GT)
            body(FULL - 1, 1, GT, 1)
            body(FULL, 0, 1, 0)

        def static(i, n):
            return isinstance(i, int) and i < n

        @block.sync
        def _(sp):
            sp.dma_start(W1[:], w1.rearrange("e (k i) h -> i e k h", k=2)).then_inc(loaded, 16)
            sp.dma_start(W2[:], w2.rearrange("e (c i) o -> i e c o", c=HC)).then_inc(loaded, 16)
            sp.dma_start(B1[:], b1.rearrange("e (c i) -> i e c", c=HC)).then_inc(loaded, 16)
            sp.dma_start(B2[:], b2.partition_broadcast(P)).then_inc(loaded, 16)
            x4 = d["x1"][0:FULL * GT * P, :].rearrange("(g t i) d -> g i t d", t=GT, i=P)
            o4 = out[0:FULL * GT * P, :].rearrange("(g t i) d -> g i t d", t=GT, i=P)
            sp.dma_start(X[:, 0, :, :], x4[0]).then_inc(x_in[0], 16)

            def go(i, n, tiles, after):
                if after:
                    if not static(i, 1):
                        sp.wait_ge(prepared, i)
                    if after == GT:
                        sp.dma_start(X[:, 1 - n, :, :], x4[bass.ds(i + 1, 1)].rearrange("g i t d -> (g i) t d")
                                     ).then_inc(x_in[1 - n], 16)
                    else:
                        sp.dma_start(X[:, 1 - n, 0, :], d["x1"][FULL * GT * P:NPAD, :]).then_inc(x_in[1 - n], 16)
                sp.wait_ge(added, i * PG + tiles * E)
                if tiles == GT:
                    sp.dma_start(o4[bass.ds(i, 1)].rearrange("g i t d -> (g i) t d"), O[:, n, :, :]).then_inc(stored[n], 16)
                else:
                    sp.dma_start(out[FULL * GT * P:N, :], O[0:LAST, n, 0, :]).then_inc(stored[n], 16)

            groups(sp, go)
            sp.wait_ge(stored[0], 16 * (FULL // 2 + 1))
            sp.wait_ge(stored[1], 16 * (FULL // 2))

        @block.vector
        def _(dve):
            link = Chain(dve, step)
            LINKS = GT * E

            def gate_at(i, q, ei):
                return gate[:, bass.ds(i * GT + q, 1), ei]

            def prepare(i, n, tiles):
                link.n = i * LINKS
                dve.wait_ge(x_in[n], x_count(i, n) + 16)
                for q in range(tiles):
                    v = i * GT + q
                    mv = c.spread[:, bass.ds(v, 1), :].rearrange("p w s -> p (w s)")
                    if not static(i, 1):
                        dve.wait_ge(turned, v - GT + 1)
                    dve.tensor_scalar(XN[:, q, :], X[:, n, q, :], mv[:, 0:1], mv[:, 1:2], ALU.subtract,
                                      ALU.mult).then_inc(made, 1)
                    dve.wait_ge(made, v + 1)
                if not static(i, 2):
                    dve.wait_ge(stored[n], x_count(i, n))
                for q in range(tiles):
                    for ei in range(E):
                        of = X[:, n, q, :] if ei == 0 else O[:, n, q, :]
                        link(dve.scalar_tensor_tensor(O[:, n, q, :], B2[:, ei, :], gate_at(i, q, ei), of, ALU.mult, ALU.add))
                dve.sem_inc(prepared, 1)

            def go(i, n, tiles, after):
                if after:
                    prepare(i + 1, 1 - n, after)
                for ei in range(E):
                    for q in range(tiles):
                        v = i * PG + (ei * tiles + q)
                        dve.wait_ge(product, v + 1)
                        if ei:
                            dve.wait_ge(added, v - tiles + 1)
                        dve.scalar_tensor_tensor(O[:, n, q, :], PO[:, (ei * tiles + q) % 2, 0:D], gate_at(i, q, ei),
                                                 O[:, n, q, :], ALU.mult, ALU.add).then_inc(added, 1)

            dve.wait_ge(loaded, 64)
            prepare(0, 0, GT)
            groups(dve, go)

        @block.tensor
        def _(pe):
            def turn(i, n, tiles):
                for q in range(tiles):
                    v = i * GT + q
                    pe.wait_ge(made, v + 1)
                    if not (static(i, 1) and q < 2):
                        pe.wait_ge(copied, v - 1)
                    for k in range(2):
                        last = pe.transpose(PT[:, q % 2, k * P:(k + 1) * P], XN[:, q, k * P:(k + 1) * P], c.ident[:])
                    last.then_inc(turned, 1)

            def up(i, n, tiles, ei):
                for h in range(HC):
                    v = i * PG + (ei * HC + h)
                    if not (static(i, 1) and ei == 0 and h < 2):
                        pe.wait_ge(gelu, v - 1)
                    for k in range(2):
                        last = pe.matmul(PH[:, h % 2, 0:tiles * P], W1[:, ei, k, h * P:(h + 1) * P],
                                         XT[:, n, k, 0:tiles * P], start=k == 0, stop=k == 1)
                    last.then_inc(hidden, 1)

            def down(i, n, tiles, ei):
                pe.wait_ge(gelu, i * PG + (ei + 1) * HC)
                for q in range(tiles):
                    p = ei * tiles + q
                    if not (static(i, 1) and p < 2):
                        pe.wait_ge(added, i * PG + p - 1)
                    for h in range(HC):
                        last = pe.matmul(PO[:, p % 2, 0:D], HT[:, ei % 2, h, q * P:(q + 1) * P], W2[:, ei, h, :],
                                         start=h == 0, stop=h == HC - 1)
                    last.then_inc(product, 1)

            def go(i, n, tiles, after):
                pe.wait_ge(copied, i * GT + tiles)
                up(i, n, tiles, 0)
                if after:
                    turn(i + 1, 1 - n, after)
                for ei in range(1, E):
                    up(i, n, tiles, ei)
                    down(i, n, tiles, ei - 1)
                down(i, n, tiles, E - 1)

            pe.wait_ge(loaded, 64)
            turn(0, 0, GT)
            groups(pe, go)

        @block.scalar
        def _(act):
            def copy(i, n, tiles):
                for q in range(tiles):
                    act.wait_ge(turned, i * GT + q + 1)
                    act.copy(XT[:, n, :, q * P:(q + 1) * P], PT[:, q % 2, 0:D].rearrange("p (k i) -> p k i", k=2)
                             ).then_inc(copied, 1)

            def go(i, n, tiles, after):
                for ei in range(E):
                    done = (ei - 1) * tiles if ei >= 2 else (ei - 1) * GT
                    if not (static(i, 1) and ei < 2):
                        act.wait_ge(product, i * PG + done)
                    for h in range(HC):
                        act.wait_ge(hidden, i * PG + (ei * HC + h + 1))
                        act.activation(HT[:, ei % 2, h, 0:tiles * P], PH[:, h % 2, 0:tiles * P], ACT.Gelu,
                                       bias=B1[:, ei, h:h + 1]).then_inc(gelu, 1)
                    if ei == 0 and after:
                        copy(i + 1, 1 - n, after)

            act.wait_ge(loaded, 64)
            copy(0, 0, GT)
            groups(act, go)


_INS = ["x", "src", "dst", "L0_gnn_W", "L0_gnn_a_src", "L0_gnn_a_dst", "L0_mix_Wqkv", "L0_mix_Wout", "L0_mix_gamma",
        "L0_ffn_W_gat", "L0_ffn_att_src", "L0_ffn_att_dst", "L0_ffn_b_gat", "L0_ffn_ln_gamma", "L0_ffn_ln_beta",
        "L0_ffn_W1", "L0_ffn_b1", "L0_ffn_W2", "L0_ffn_b2", "L0_ffn_edge_index"]
_OUTS = [((N, D), "float32")]


def kernel(**inputs):
    import numpy as _np
    import concourse.bacc as _bacc
    from concourse import mybir as _mybir
    from concourse.bass_utils import run_bass_kernel_spmd as _run

    nc = _bacc.Bacc("TRN2", target_bir_lowering=False, num_devices=1)
    arrays, args = {}, []
    for name in _INS:
        a = _np.ascontiguousarray(inputs[name])
        arrays[f"in_{name}_dram"] = a
        args.append(nc.dram_tensor(f"in_{name}_dram", a.shape, _mybir.dt.from_np(a.dtype), kind="ExternalInput").ap())
    for i, (shape, dtype) in enumerate(_OUTS):
        dt = _mybir.dt.from_np(_np.dtype(dtype))
        args.append(nc.dram_tensor(f"out_{i}_dram", shape, dt, kind="ExternalOutput").ap())
    build_program(nc, *args)
    r = _run(nc, [arrays], core_ids=[0])
    got = tuple(r.results[0][f"out_{i}_dram"] for i in range(len(_OUTS)))
    return got[0]
```

```python
from contextlib import ExitStack, contextmanager

import concourse.bass as bass
from concourse import mybir

ALU = mybir.AluOpType
ACT = mybir.ActivationFunctionType
AX = mybir.AxisListType
F32 = mybir.dt.float32
I32 = mybir.dt.int32
BF16 = mybir.dt.bfloat16

P = 128
N = 6250
D = 256
H = 4
TILES = -(-N // P)
NPAD = TILES * P
LAST = N - (TILES - 1) * P
HIS = -(-NPAD // 256)
E1 = 200000
E2 = 131072
E2S = E2 + N
COLS2 = -(-E2S // P)
PADS2 = COLS2 * P - E2S
OFF_WINDOW = 16000.0
DROP_DST = 8191.0
BIG = 1.0e38
EPS = 1e-5
UNROLL = 16
RING = 8
REST = 1000


def stand_apart(engine, sem):
    engine.sem_inc(sem, 1)


class Graph:

    def __init__(self, tag, chunks, slope, width):
        self.tag = tag
        self.chunks = chunks
        self.blocks = -(-(chunks + TILES - 1) // P)
        self.grid = self.blocks * P
        self.steps = -(-(chunks + TILES - 1) // UNROLL) * UNROLL
        self.batches = -(-chunks // 16) * 4
        self.slope = slope
        self.width = width // H
        self.row = width + H
        self.in_psum = (TILES + 1) * self.row <= 1024
        assert self.steps <= self.grid and self.batches * 4 <= self.grid


class Chain:

    def __init__(self, engine, sem, start=0):
        self.engine, self.sem, self.n = engine, sem, start

    def __call__(self, ins):
        self.n += 1
        ins.then_inc(self.sem, 1)
        self.engine.wait_ge(self.sem, self.n)


def bcast(ap, shape):
    return ap.to_broadcast(shape)


@contextmanager
def stage(nc):
    with ExitStack() as s:
        held = []

        def sem(name):
            held.append(s.enter_context(nc.semaphore(name)))
            return held[-1]

        yield sem
        with nc.Block() as block:
            @block.gpsimd
            def _(pool):
                for q in held:
                    pool.sem_clear(q)


def build_program(nc, x, src, dst, gw, gas, gad, wqkv, wout, gamma, wgat, fas, fad, bgat, lng, lnb,
                  w1, b1, w2, b2, edges, out):
    gnn = Graph("gnn", -(-E1 // P), 0.01, D)
    ffn = Graph("ffn", COLS2, 0.2, 16)
    with ExitStack() as ctx:
        ctx.enter_context(nc.allow_non_contiguous_dma(reason="small tables"))

        def dram(name, shape, dt=F32):
            return nc.dram_tensor(name, shape, dt).ap()

        c = Consts(nc, ctx)
        d = {
            "gnn_pairs": dram("gnn_pairs", [gnn.grid * P, 2]),
            "ffn_pairs": dram("ffn_pairs", [ffn.grid * P, 2]),
            "unsorted": dram("unsorted_pairs", [COLS2 * P, 2]),
            "halfsorted": dram("halfsorted_pairs", [COLS2 * P, 2]),
            "gnn_rows": dram("gnn_rows", [NPAD, gnn.row]),
            "ffn_rows": dram("ffn_rows", [NPAD, 16]),
            "x1": dram("x_after_gnn", [NPAD, D]),
            "xt": dram("xn_transposed", [NPAD, D]),
            "xm": dram("x_plus_mix", [NPAD, D]),
        }
        for g in (gnn, ffn):
            d[g.tag + "_keys"] = dram(g.tag + "_keys", [g.grid, 2 * P], BF16)
            d[g.tag + "_edge_rows"] = dram(g.tag + "_edge_rows", [g.grid, 2 * P])
            d[g.tag + "_weight_rows"] = dram(g.tag + "_weight_rows", [g.grid, H * P])
            d[g.tag + "_ends"] = dram(g.tag + "_ends", [2, g.grid])
            d[g.tag + "_tails"] = dram(g.tag + "_tails", [2, H, g.grid])
            d[g.tag + "_carries"] = dram(g.tag + "_carries", [2, H, g.grid])
            d[g.tag + "_windows"] = dram(g.tag + "_windows", [g.grid], I32)
        with stage(nc) as sem:
            constants(nc, c, sem)
            list_edges(nc, sem, d, src, dst, edges, gnn, ffn)
        kept = ctx.enter_context(ExitStack())
        tables = EdgeTables(nc, kept, gnn)
        with ExitStack() as shared:
            ER = shared.enter_context(nc.sbuf_tensor("gnn_scores_rows", [P, H, gnn.blocks, P], F32))
            places = Places(nc, shared)
            with stage(nc) as sem:
                scatter = sort_pass(nc, c, sem, places, "lo", d["unsorted"], d["halfsorted"], COLS2 * P)
            early = gnn.batches // 28 * 4
            with ExitStack() as scored:
                with stage(nc) as sem:
                    nodes_in(nc, c, sem, d, x, gw, gas, gad, wqkv, wout, gamma, scatter.share)
                    edge_tables(nc, c, sem, d, gnn, tables, scatter.share)
                    scores = Scores(nc, scored, gnn)
                    hi_columns(nc, c, sem, d, gnn, scores, scatter.share)
                    look_up_scores(nc, c, sem, d, gnn, scores, 0, early, scatter.share, REST)
                with stage(nc) as sem:
                    scatter = sort_pass(nc, c, sem, places, "hi", d["halfsorted"], d["ffn_pairs"], ffn.grid * P)
                with stage(nc) as sem:
                    look_up_scores(nc, c, sem, d, gnn, scores, early, gnn.batches - early, scatter.share, 51)
                    score_rows(nc, c, sem, gnn, scores, ER)
            with stage(nc) as sem:
                subtract_maximum(nc, c, sem, d, gnn, ER, scatter.share, REST)
            assert scatter.done_loops == scatter.loops
        with stage(nc) as sem:
            acc = aggregate(nc, kept, c, sem, d, gnn, tables)
            nodes_between(nc, c, sem, d, acc, wgat, fas, fad)
        kept.close()
        gate = ctx.enter_context(nc.sbuf_tensor("gate_of_expert", [P, TILES, 4], F32))
        with ExitStack() as kept:
            tables = EdgeTables(nc, kept, ffn)
            with stage(nc) as sem:
                edge_tables(nc, c, sem, d, ffn, tables, None)
                gather = Gather(nc, kept, c, d, ffn, tables)
                ER = kept.enter_context(nc.sbuf_tensor("ffn_scores_rows", [P, H, ffn.blocks, P], F32))
                with ExitStack() as scored:
                    scores = Scores(nc, scored, ffn)
                    hi_columns(nc, c, sem, d, ffn, scores, gather.share)
                    look_up_scores(nc, c, sem, d, ffn, scores, 0, ffn.batches, gather.share, 37)
                    score_rows(nc, c, sem, ffn, scores, ER)
                subtract_maximum(nc, c, sem, d, ffn, ER, gather.share, 5)
            with stage(nc) as sem:
                acc = add_up(nc, kept, c, sem, d, ffn, tables, gather)
                gates(nc, c, sem, acc, gate, bgat, lng, lnb)
        with stage(nc) as sem:
            experts(nc, c, sem, d, out, gate, w1, b1, w2, b2)


class Consts:

    def __init__(self, nc, ctx):
        def sb(name, shape, dt=F32):
            return ctx.enter_context(nc.sbuf_tensor(name, shape, dt))

        self.row_i = sb("iota_row_i", [P, P], I32)
        self.col_i = sb("iota_col_i", [P, 1], I32)
        self.row = sb("iota_row", [P, P])
        self.lo = sb("iota_lo", [P, 2])
        self.ident = sb("identity", [P, P])
        self.ones = sb("ones", [P, P])
        self.before = sb("before", [P, P])
        self.blocks32 = sb("blocks32", [P, P])
        self.zeros = sb("zeros", [P, COLS2])
        self.eps = sb("eps", [P, 1])
        self.spread = sb("x1_mean_and_inverse_root_of_variance", [P, TILES, 2])
        self.nc = nc
        self.held = ctx
        self.ring_done = {use: [ctx.enter_context(nc.semaphore("%s_half%d_done" % (use, k))) for k in range(2)]
                          for use in ("lo_scatter", "hi_scatter", "ffn_gather")}
        self.ring_done["gnn_gather"] = [ctx.enter_context(nc.semaphore("gnn_gather_quarter%d_done" % k)) for k in range(4)]
        self.pool_fetch_before = [0, 0, 0]
        self.pool_fetch = [ctx.enter_context(nc.semaphore("pool_fetch%d" % u)) for u in range(3)]
        self.scores = sb("scores_bf16", [P, 3, 2, 2, HIS, H], BF16)
        self.score = sb("scores_f32", [P, 2, HIS, 2, H])


def constants(nc, c, sem):
    made_iota, cs = sem("made_iota"), sem("const_step")
    with nc.sbuf_tensor("shifted_row", [P, P], I32) as shr, nc.sbuf_tensor("shifted_col", [P, 1], I32) as shc, \
            nc.sbuf_tensor("shifted_row_f", [P, P], F32) as shrf, nc.sbuf_tensor("shifted_col_f", [P, 1], F32) as shcf, \
            nc.Block() as block:
        @block.gpsimd
        def _(pool):
            pool.iota(c.row_i[:], [[1, P]], 0, 0).then_inc(made_iota, 1)
            pool.iota(c.col_i[:], [[0, 1]], 0, 1).then_inc(made_iota, 1)

        @block.vector
        def _(dve):
            link = Chain(dve, cs)
            link(dve.memset(c.ones[:], 1.0))
            link(dve.memset(c.zeros[:], 0.0))
            link(dve.memset(c.eps[:], EPS))
            dve.wait_ge(made_iota, 2)
            link(dve.tensor_copy(c.row[:], c.row_i[:]))
            link(dve.tensor_copy(c.lo[:, 0:1], c.col_i[:]))
            link(dve.tensor_scalar(c.lo[:, 1:2], c.lo[:, 0:1], 128.0, None, ALU.add))
            link(dve.tensor_scalar(c.ident[:], c.row[:], c.lo[:, 0:1], None, ALU.is_equal))
            link(dve.tensor_scalar(c.before[:], c.row[:], c.lo[:, 0:1], None, ALU.is_gt))
            link(dve.tensor_scalar(shr[:], c.row_i[:], 5, None, ALU.arith_shift_right))
            link(dve.tensor_scalar(shc[:], c.col_i[:], 5, None, ALU.arith_shift_right))
            link(dve.tensor_copy(shrf[:], shr[:]))
            link(dve.tensor_copy(shcf[:], shc[:]))
            link(dve.tensor_scalar(c.blocks32[:], shrf[:], shcf[:, 0:1], None, ALU.is_equal))
            link(dve.memset(c.score[:], 0.0))


def list_edges(nc, sem, d, src, dst, edges, gnn, ffn):
    loaded = [sem("edges_loaded%d" % i) for i in range(4)]
    paired, stored = sem("edges_paired"), sem("pairs_stored")
    R1 = 125
    T1 = E1 // R1
    T2 = E2 // P
    RS = 125
    TS = N // RS
    with ExitStack() as s:
        def sb(name, shape, dt=F32):
            return s.enter_context(nc.sbuf_tensor(name, shape, dt))

        i1 = sb("gnn_edges_i", [R1, 2, T1], I32)
        p1 = sb("gnn_edges_p", [R1, T1, 2])
        i2 = sb("ffn_edges_i", [P, 2, T2], I32)
        p2 = sb("ffn_edges_p", [P, T2, 2])
        si = sb("self_i", [RS, TS], I32)
        sp_ = sb("self_p", [RS, TS, 2])
        pad = sb("pad_pairs", [P, P, 2])
        drop = sb("drop_pairs", [P, 2])
        made = sem("self_iota")
        block = s.enter_context(nc.Block())

        @block.gpsimd
        def _(pool):
            pool.iota(si[:], [[1, TS]], 0, TS).then_inc(made, 1)

        @block.vector
        def _(dve):
            link = Chain(dve, paired)
            link(dve.memset(pad[:, :, 0], 0.0))
            link(dve.memset(pad[:, :, 1], OFF_WINDOW))
            link(dve.memset(drop[:, 0:1], 0.0))
            link(dve.memset(drop[:, 1:2], DROP_DST))
            dve.wait_ge(made, 1)
            link(dve.tensor_copy(sp_[:, :, 0], si[:]))
            link(dve.tensor_copy(sp_[:, :, 1], si[:]))
            for k in range(2):
                dve.wait_ge(loaded[2 + k], 16)
                link(dve.tensor_copy(p2[:, :, k], i2[:, k, :]))
            for k in range(2):
                dve.wait_ge(loaded[k], 16)
                link(dve.tensor_copy(p1[:, :, k], i1[:, k, :]))

        @block.sync
        def _(sp):
            for k in range(2):
                sp.dma_start(i2[:, k, :], edges[k].rearrange("(p t) -> p t", p=P)).then_inc(loaded[2 + k], 16)
            for k, a in enumerate((src, dst)):
                sp.dma_start(i1[:, k, :], a.rearrange("(p t) -> p t", p=R1)).then_inc(loaded[k], 16)
            sp.wait_ge(paired, 6)
            n = 0
            sp.dma_start(d["unsorted"][E2:E2 + N, :].rearrange("(p t) k -> p t k", p=RS), sp_[:]).then_inc(stored, 16)
            sp.dma_start(d["unsorted"][E2S:E2S + PADS2, :], drop[0:PADS2, :]).then_inc(stored, 16)
            rest = gnn.grid * P - E1
            rows = next(r for r in range(P, 0, -1) if rest % r == 0 and rest // r <= P)
            sp.dma_start(d["gnn_pairs"][E1:, :].rearrange("(p t) k -> p t k", p=rows),
                         pad[0:rows, 0:rest // rows, :]).then_inc(stored, 16)
            n += 3
            for b in range(ffn.blocks):
                sp.dma_start(d["ffn_pairs"][b * P * P:(b + 1) * P * P, :].rearrange("(p t) k -> p t k", p=P),
                             pad[:]).then_inc(stored, 16)
                n += 1
            sp.wait_ge(paired, 8)
            sp.dma_start(d["unsorted"][0:E2, :].rearrange("(p t) k -> p t k", p=P), p2[:]).then_inc(stored, 16)
            sp.wait_ge(paired, 10)
            sp.dma_start(d["gnn_pairs"][0:E1, :].rearrange("(p t) k -> p t k", p=R1), p1[:]).then_inc(stored, 16)
            sp.wait_ge(stored, 16 * (n + 2))


def sort_pass(nc, c, sem, places, digit, pairs_in, pairs_out, room):
    T = COLS2
    TP = -(-T // UNROLL) * UNROLL
    K = 4
    nb = P if digit == "lo" else -(-TILES // K) * K
    NA = nb * 3 // 8 // K * K
    masked, ranked, placed, apart_act, distant, counted, distant2 = (sem(digit + n) for n in (
        "_masked", "_ranked", "_placed", "_act_wait_apart", "_distance", "_counted", "_distance_again"))
    loaded, step = sem(digit + "_loaded"), sem(digit + "_step")
    summed = sem(digit + "_summed")
    apart = sem(digit + "_wait_apart")
    pr, place = places.pairs, places.place
    assert place.shape[1] == TP
    with ExitStack() as s:
        def sb(name, shape, dt=F32):
            return s.enter_context(nc.sbuf_tensor(digit + name, shape, dt))

        ki = sb("_key_i", [P, T], I32)
        key = sb("_key", [P, T])
        is_digit = sb("_is_digit", [P, K, T])
        rank = sb("_rank", [P, K, T])
        distance = sb("_distance", [P, 2, T])
        cnt = sb("_count", [P, P])
        tot = sb("_total", [P, P])
        base = sb("_base", [P, P])
        ps = s.enter_context(nc.psum_tensor(digit + "_sums", [P, 2, 512], F32))
        block = s.enter_context(nc.Block())
        at = {}

        @block.sync
        def _(sp):
            sp.dma_start(pr[:, 0:T, :], pairs_in.rearrange("(p t) k -> p t k", p=P)).then_inc(loaded, 16)

        @block.vector
        def _(dve):
            link = Chain(dve, step)
            link(dve.memset(pr[:, T:TP, :], 0.0))
            link(dve.memset(place[:], 1.0e6))
            dve.wait_ge(loaded, 16)
            link(dve.tensor_copy(ki[:], pr[:, 0:T, 1]))
            if digit == "lo":
                link(dve.tensor_scalar(ki[:], ki[:], P - 1, None, ALU.bitwise_and))
            else:
                link(dve.tensor_scalar(ki[:], ki[:], 7, None, ALU.arith_shift_right))
            link(dve.tensor_copy(key[:], ki[:]))
            n = link.n

            at["keys"] = n

            def count(j, first):
                for u in range(K):
                    b = bass.ds(j * K + u, 1)
                    if not first:
                        dve.wait_ge(step, j * K + (n + u + 1 - K - NA))
                    dve.tensor_scalar(is_digit[:, u, :], key[:], c.row[:, b], 0.0, ALU.is_equal, ALU.add,
                                      accum_out=cnt[:, b]).then_inc(step, 1)

            count(NA // K, True)
            with dve.Fori(NA // K + 1, nb // K) as j:
                count(j, False)
            link.n = n + nb - NA
            dve.wait_ge(step, link.n)
            at["counts"] = link.n
            dve.wait_ge(summed, 1)
            link(dve.tensor_copy(tot[:, 0:nb], ps[:, 0, 0:nb]))
            link(dve.tensor_tensor_scan(base[:, 0:nb], tot[:, 0:nb], c.zeros[:, 0:nb], -1.0, ALU.add, ALU.add))
            link(dve.tensor_tensor(base[:, 0:nb], base[:, 0:nb], tot[:, 0:nb], ALU.subtract))
            link(dve.tensor_tensor(base[:, 0:nb], base[:, 0:nb], ps[:, 1, 0:nb], ALU.add))
            def run(b, u, first=False):
                if not first:
                    dve.wait_ge(placed, b - (K - 1))
                dve.wait_ge(masked, b + 1)
                dve.tensor_tensor_scan(rank[:, u, :], is_digit[:, u, :], c.zeros[:, 0:T], base[:, bass.ds(b, 1)],
                                       ALU.add, ALU.add).then_inc(ranked, 1)

            def put(b, u, first):
                dve.wait_ge(ranked, b + 1)
                stand_apart(dve, apart)
                if not first:
                    dve.wait_ge(placed, b)
                    stand_apart(dve, apart)
                dve.copy_predicated(place[:, 0:T], is_digit[:, u, :].bitcast(I32), rank[:, u, :]).then_inc(placed, 1)

            def group(j, first):
                for u in range(K):
                    b = j * K + u
                    run(b, u, first)
                    if not (first and u < 1):
                        put(b - 1, (u - 1) % K, first and u == 1)

            group(0, True)
            with dve.Fori(1, nb // K) as j:
                group(j, False)
            put(nb - 1, K - 1, False)
            dve.wait_ge(placed, nb)

        @block.scalar
        def _(act):
            def far(b, u, sem_):
                if not (isinstance(b, int) and b < 2):
                    act.wait_ge(sem_[1], b - 1)
                    stand_apart(act, apart_act)
                act.activation(distance[:, u % 2, :], key[:], ACT.Abs, scale=-1.0, bias=c.row[:, bass.ds(b, 1)]
                               ).then_inc(sem_[0], 1)

            def count(b, u):
                act.wait_ge(distant, b + 1)
                stand_apart(act, apart_act)
                act.activation(distance[:, u % 2, :], distance[:, u % 2, :], ACT.Relu, scale=-1.0, bias=c.ones[:, 0:1],
                               accum_out=cnt[:, bass.ds(b, 1)]).then_inc(counted, 1)

            def mask(b, u):
                if not (isinstance(b, int) and b < K):
                    act.wait_ge(placed, b - (K - 1))
                    stand_apart(act, apart_act)
                act.wait_ge(distant2, b + 1)
                act.activation(is_digit[:, u, :], distance[:, u % 2, :], ACT.Relu, scale=-1.0, bias=c.ones[:, 0:1]
                               ).then_inc(masked, 1)

            def in_order(n, one, sems):
                def group(j):
                    for u in range(K):
                        b = j * K + u
                        far(b, u, sems)
                        if not (isinstance(b, int) and b == 0):
                            one(b - 1, (u - 1) % K)
                group(0)
                group(1)
                with act.Fori(2, n // K) as j:
                    group(j)
                one(n - 1, K - 1)

            act.wait_ge(step, at["keys"])
            in_order(NA, count, (distant, counted))
            act.wait_ge(counted, NA)
            act.wait_ge(step, at["counts"])
            in_order(nb, mask, (distant2, masked))

        @block.tensor
        def _(pe):
            pe.wait_ge(step, at["counts"])
            pe.wait_ge(counted, NA)
            pe.matmul(ps[:, 0, 0:nb], c.ones[:], cnt[:, 0:nb], start=True, stop=True)
            pe.matmul(ps[:, 1, 0:nb], c.before[:], cnt[:, 0:nb], start=True, stop=True).then_inc(summed, 1)

    return Scatter(c, digit, places, pairs_out, room)


class Places:

    def __init__(self, nc, kept):
        def keep(name, shape, dt=F32):
            return kept.enter_context(nc.sbuf_tensor("sort_" + name, shape, dt))

        TP = -(-COLS2 // UNROLL) * UNROLL
        self.pairs = keep("pairs", [P, TP, 2])
        self.place = keep("place", [P, TP])
        self.slot_i = keep("slot_index", [P, UNROLL], I32)
        self.slot_p = keep("slot_pair", [P, UNROLL, 2])


class Scatter:

    def __init__(self, c, digit, places, pairs_out, room):
        self.pr, self.place, self.pairs_out, self.room = places.pairs, places.place, pairs_out, room
        self.loops, self.done_loops = places.place.shape[1] // UNROLL, 0
        self.slot_i, self.slot_p = places.slot_i, places.slot_p
        self.staged, self.apart = (c.held.enter_context(c.nc.semaphore(digit + n)) for n in ("_staged", "_pool_wait_apart"))
        self.scattered = c.ring_done[digit + "_scatter"]

    def half(self, pool, i, k, first):
        lo, hi = k * RING, (k + 1) * RING
        at = bass.ds(i * UNROLL + lo, RING)
        if not first:
            pool.wait_ge(self.scattered[k], i * (16 * RING))
            stand_apart(pool, self.apart)
        pool.tensor_copy(self.slot_i[:, lo:hi], self.place[:, at]).then_inc(self.staged, 1)
        pool.tensor_copy(self.slot_p[:, lo:hi, :], self.pr[:, at, :]).then_inc(self.staged, 1)
        pool.wait_ge(self.staged, i * 4 + 2 * k + 2)
        stand_apart(pool, self.apart)
        for u in range(lo, hi):
            pool.indirect_dma_start(
                out=self.pairs_out, out_offset=bass.IndirectOffsetOnAxis(ap=self.slot_i[:, u:u + 1], axis=0),
                in_=self.slot_p[:, u, :], in_offset=None, bounds_check=self.room - 1,
                oob_is_err=False).then_inc(self.scattered[k], 16)

    def share(self, pool, loops):
        i, end = self.done_loops, min(self.loops, self.done_loops + loops)
        if i == 0:
            for k in range(2):
                self.half(pool, 0, k, True)
            i = 1
        if i < end:
            with pool.Fori(i, end) as i:
                for k in range(2):
                    self.half(pool, i, k, False)
        if end == self.loops and self.done_loops < end:
            for k in range(2):
                pool.wait_ge(self.scattered[k], 16 * RING * self.loops)
        self.done_loops = end


def transposes(nc, pe, act, jobs, ps, given, taken, ident):
    banks = ps.shape[1]
    if pe is not None:
        for j, (ins, _, _) in enumerate(jobs):
            if j >= banks:
                pe.wait_ge(taken, j - banks + 1)
            for q, a in enumerate(ins):
                w = a.free_size()
                last = pe.transpose(ps[0:w, j % banks, q * P:(q + 1) * P], a, ident)
            last.then_inc(given, 1)
    if act is not None:
        for j, (_, o, view) in enumerate(jobs):
            act.wait_ge(given, j + 1)
            act.copy(o, view(ps[:, j % banks, :])).then_inc(taken, 1)


def measure(nc, link, stats, mv, rows, measured, apart, i):
    if not (isinstance(i, int) and i == 0):
        nc.vector.wait_ge(measured, i)
    link(nc.vector.bn_stats(stats, rows))
    stand_apart(nc.vector, apart)
    nc.vector.bn_aggr(mv, stats).then_inc(measured, 1)


def spread_roots(c, engine, measured, rooted, ring):
    def root(i, n):
        engine.wait_ge(measured, i + 1)
        v = ring[:, n, 1:2]
        engine.activation(v, v, ACT.Sqrt, bias=c.eps[:, 0:1]).then_inc(rooted, 1)
    return root


def nodes_in(nc, c, sem, d, x, gw, gas, gad, wqkv, wout, gamma, beside):
    with ExitStack() as s:
        def sb(name, shape, dt=F32):
            return s.enter_context(nc.sbuf_tensor("in_" + name, shape, dt))

        X = sb("x", [P, TILES, D])
        XT = sb("xn_transposed", [P, 2, 2, P])
        WZ = sb("w_graph", [P, 2, D + 2 * H])
        WQ = sb("w_qkv", [P, 2, 3 * D])
        WO = sb("w_out", [P, 2, D])
        GA = sb("gamma", [P, D])
        AS = sb("att", [P, 2, D])
        PROD = sb("att_products", [P, D])
        KM = sb("k_max", [P, D])
        KMT = sb("k_max_column", [P, 2])
        KD = sb("k_max_diagonal", [P, 2, P])
        KB = sb("k_max_everywhere", [P, D])
        CT = sb("context_masked", [P, 2, P])
        CW = sb("context_out", [P, 2, D])
        SUMS = sb("k_sums", [P, 2])

        loaded = [sem("node_loaded%d" % i) for i in range(3)]
        cleared, step = sem("x_cleared"), sem("project_step")
        ahead, turned, copied = sem("xn_ready"), sem("xn_turned"), sem("xn_copied")
        measured, rooted, inverted, apart = (sem("x_" + n) for n in ("measured", "rooted", "inverted", "wait_apart"))
        projected, taken_z, taken_k = sem("projected"), sem("z_taken"), sem("k_taken")
        stored = [sem("z_stored0"), sem("z_stored1")]
        xt_stored = [sem("xt_stored0"), sem("xt_stored1")]

        def rows(ap, i):
            return ap.rearrange("(w i) d -> w i d", i=P)[bass.ds(i, 1)].rearrange("w i d -> (w i) d")

        def load_turned(sp, used, arrived):
            def load(i, n, first):
                if not first:
                    sp.wait_ge(used, i - 1)
                sp.dma_start(XT[:, n].rearrange("p k i -> p (k i)"), rows(d["xt"], i)).then_inc(arrived[n], 16)
            return load
        with ExitStack() as s2:
            XN = s2.enter_context(nc.sbuf_tensor("in_xn", [P, 2, D], F32))
            ST = s2.enter_context(nc.sbuf_tensor("in_stats", [P, 6], F32))
            MV = s2.enter_context(nc.sbuf_tensor("in_mean_var", [P, 2, 2], F32))
            ZO = s2.enter_context(nc.sbuf_tensor("in_z_out", [P, 2, H, D // H + 1], F32))
            PT = s2.enter_context(nc.psum_tensor("ps_in_turn", [P, 2, 512], F32))
            PZ = s2.enter_context(nc.psum_tensor("ps_in_z", [P, 2, 512], F32))
            PK = s2.enter_context(nc.psum_tensor("ps_in_k", [P, 2, 512], F32))
            block = s2.enter_context(nc.Block())

            @block.gpsimd
            def _(pool):
                beside(pool, 21)

            @block.sync
            def _(sp):
                sp.wait_ge(cleared, 1)
                full = TILES - 1
                sp.dma_start(X[:, 0:full, :], x[0:full * P, :].rearrange("(w i) d -> i w d", i=P)).then_inc(loaded[0], 16)
                sp.dma_start(X[0:LAST, full, :], x[full * P:N, :]).then_inc(loaded[1], 16)
                for k in range(2):
                    sp.dma_start(WZ[:, k, 0:D].rearrange("i (h d) -> i h d", h=H),
                                 gw[:, k * P:(k + 1) * P, :].rearrange("h i d -> i h d")).then_inc(loaded[2], 16)
                sp.dma_start(WQ[:], wqkv.rearrange("(k i) d -> i k d", k=2)).then_inc(loaded[2], 16)
                sp.dma_start(WO[:], wout.rearrange("(k i) d -> i k d", k=2)).then_inc(loaded[2], 16)
                sp.dma_start(GA[:], gamma.partition_broadcast(P)).then_inc(loaded[2], 16)
                sp.dma_start(AS[:, 0, :], gas.rearrange("h d -> (h d)").partition_broadcast(P)).then_inc(loaded[2], 16)
                sp.dma_start(AS[:, 1, :], gad.rearrange("h d -> (h d)").partition_broadcast(P)).then_inc(loaded[2], 16)

                def store(i, n):
                    sp.wait_ge(copied, i + 1)
                    sp.dma_start(rows(d["xt"], i), XT[:, n].rearrange("p k i -> p (k i)")).then_inc(xt_stored[n], 16)
                    sp.wait_ge(taken_z, i + 1)
                    sp.dma_start(d["gnn_rows"].rearrange("(w i) d -> w i d", i=P)[bass.ds(i, 1)].rearrange("w i d -> (w i) d"),
                                 ZO[:, n, :, :].rearrange("p h f -> p (h f)")).then_inc(stored[n], 16)

                with sp.Fori(0, TILES // 2) as i:
                    store(i * 2, 0)
                    store(i * 2 + 1, 1)
                store(TILES - 1, 0)
                for q in (stored, xt_stored):
                    sp.wait_ge(q[0], 16 * (TILES // 2 + 1))
                    sp.wait_ge(q[1], 16 * (TILES // 2))

            @block.vector
            def _(dve):
                link = Chain(dve, step)
                dve.memset(X[:, TILES - 1, :], 0.0).then_inc(cleared, 1)
                link(dve.memset(KM[:], -3.0e38))
                link(dve.memset(ZO[:], 1.0))
                dve.wait_ge(loaded[2], 16 * 7)
                for k in range(2):
                    for a in range(2):
                        link(dve.tensor_tensor(PROD[:], WZ[:, k, 0:D], AS[:, a, :], ALU.mult))
                        link(dve.tensor_reduce(WZ[:, k, D + H * a:D + H * (a + 1)],
                                               PROD[:].rearrange("p (h d) -> p h d", h=H), AX.X, ALU.add))
                dve.wait_ge(loaded[0], 16)
                dve.wait_ge(loaded[1], 16)
                base = link.n

                def row_of(i):
                    return X[:, bass.ds(i, 1), :].rearrange("p w d -> p (w d)")

                def stats(i, n):
                    link.n = i + base
                    if not (isinstance(i, int) and i < 2):
                        dve.wait_ge(ahead, i - 1)
                    measure(nc, link, ST[:], MV[:, n, :], row_of(i), measured, apart, i)

                def norm(i, n):
                    if not (isinstance(i, int) and i == TILES - 1):
                        stats(i + 1, 1 - n)
                    mv = MV[:, n, :]
                    dve.wait_ge(rooted, i + 1)
                    dve.reciprocal(mv[:, 1:2], mv[:, 1:2]).then_inc(inverted, 1)
                    dve.wait_ge(inverted, i + 1)
                    if not (isinstance(i, int) and i < 2):
                        dve.wait_ge(turned, i - 1)
                    dve.tensor_scalar(XN[:, n, :], row_of(i), mv[:, 0:1], mv[:, 1:2], ALU.subtract, ALU.mult).then_inc(ahead, 1)

                def take(i, n):
                    dve.wait_ge(projected, i + 1)
                    w = bass.ds(i, 1)
                    rows = LAST if isinstance(i, int) and i == TILES - 1 else P
                    out_ = c.score[:].rearrange("p a hi par h -> p a (hi par) h")[:, :, w, :].rearrange("p a w h -> p a (w h)")
                    dve.tensor_copy(out_, PK[:, n, D:D + 2 * H].rearrange("p (a h) -> p a h", a=2)).then_inc(taken_k, 1)
                    dve.tensor_tensor(KM[0:rows, :], KM[0:rows, :], PK[0:rows, n, 0:D], ALU.max).then_inc(taken_k, 1)
                    dve.wait_ge(taken_k, i * 2 + 2)

                stats(0, 0)
                norm(0, 0)
                norm(1, 1)
                take(0, 0)
                with dve.Fori(1, TILES // 2) as j:
                    norm(j * 2, 0)
                    take(j * 2 - 1, 1)
                    norm(j * 2 + 1, 1)
                    take(j * 2, 0)
                norm(TILES - 1, 0)
                take(TILES - 2, 1)
                take(TILES - 1, 0)
                link.n = base + TILES
                for a in range(2):
                    rest = PROD[:, 0:HIS * H].rearrange("p (hi h) -> p hi h", h=H)
                    for par in range(2):
                        full = c.score[:, a, :, par, :]
                        link(dve.tensor_copy(rest, full))
                        for k in range(3):
                            link(dve.tensor_copy(c.scores[:, k, a, par, :, :], rest))
                            if k < 2:
                                link(dve.tensor_tensor(rest, rest, c.scores[:, k, a, par, :, :], ALU.subtract))

            @block.tensor
            def _(pe):
                pe.wait_ge(step, 10)

                def turn(i, n):
                    pe.wait_ge(ahead, i + 1)
                    if not (isinstance(i, int) and i < 2):
                        pe.wait_ge(copied, i - 1)
                    for k in range(2):
                        last = pe.transpose(PT[:, n, k * P:(k + 1) * P], XN[:, n, k * P:(k + 1) * P], c.ident[:])
                    last.then_inc(turned, 1)

                def project(i, n):
                    pe.wait_ge(copied, i + 1)
                    if not (isinstance(i, int) and i < 2):
                        pe.wait_ge(taken_z, i - 1)
                        pe.wait_ge(taken_k, i * 2 - 2)
                    for k in range(2):
                        cols = XT[:, n, k, :]
                        pe.matmul(PZ[:, n, 0:D], cols, WZ[:, k, 0:D], start=k == 0, stop=k == 1)
                    for k in range(2):
                        cols = XT[:, n, k, :]
                        pe.matmul(PK[:, n, 0:D], cols, WQ[:, k, D:2 * D], start=k == 0, stop=k == 1)
                    for k in range(2):
                        cols = XT[:, n, k, :]
                        last = pe.matmul(PK[:, n, D:D + 2 * H], cols, WZ[:, k, D:D + 2 * H], start=k == 0, stop=k == 1)
                    last.then_inc(projected, 1)

                turn(0, 0)
                turn(1, 1)
                project(0, 0)
                turn(2, 0)
                project(1, 1)
                with pe.Fori(1, TILES // 2) as j:
                    turn(j * 2 + 1, 1)
                    project(j * 2, 0)
                    turn(j * 2 + 2, 0)
                    project(j * 2 + 1, 1)
                project(TILES - 1, 0)

            @block.scalar
            def _(act):
                def copy(i, n):
                    act.wait_ge(turned, i + 1)
                    if not (isinstance(i, int) and i < 2):
                        act.wait_ge(projected, i - 1)
                        act.wait_ge(xt_stored[n], x_count(i, n))
                    act.copy(XT[:, n, :, :], PT[:, n, 0:D].rearrange("p (k i) -> p k i", k=2)).then_inc(copied, 1)

                def take(i, n):
                    act.wait_ge(projected, i + 1)
                    if not (isinstance(i, int) and i < 2):
                        act.wait_ge(stored[n], i // 2 * 16 if isinstance(i, int) else (i - n) * 8)
                    act.copy(ZO[:, n, :, 0:D // H], PZ[:, n, 0:D].rearrange("p (h f) -> p h f", h=H)).then_inc(taken_z, 1)

                root = spread_roots(c, act, measured, rooted, MV)
                for i in range(2):
                    root(i, i)
                copy(0, 0)
                root(2, 0)
                copy(1, 1)
                root(3, 1)
                take(0, 0)
                copy(2, 0)
                root(4, 0)
                take(1, 1)
                copy(3, 1)
                root(5, 1)
                take(2, 0)
                with act.Fori(2, TILES // 2 - 1) as j:
                    copy(j * 2, 0)
                    root(j * 2 + 2, 0)
                    act.wait_ge(projected, j * 2)
                    act.wait_ge(stored[1], j * 16 - 16)
                    act.copy(ZO[:, 1, :, 0:D // H], PZ[:, 1, 0:D].rearrange("p (h f) -> p h f", h=H)).then_inc(taken_z, 1)
                    copy(j * 2 + 1, 1)
                    root(j * 2 + 3, 1)
                    act.wait_ge(projected, j * 2 + 1)
                    act.wait_ge(stored[0], j * 16)
                    act.copy(ZO[:, 0, :, 0:D // H], PZ[:, 0, 0:D].rearrange("p (h f) -> p h f", h=H)).then_inc(taken_z, 1)
                copy(TILES - 3, 0)
                root(TILES - 1, 0)
                take(TILES - 4, 1)
                copy(TILES - 2, 1)
                take(TILES - 3, 0)
                copy(TILES - 1, 0)
                take(TILES - 2, 1)
                take(TILES - 1, 0)

        cs, spread = sem("context_step"), sem("k_max_spread")
        xt_in = [sem("ctx_xt_in0"), sem("ctx_xt_in1")]
        kv, shifted, expd, v_copied, summed = (sem("ctx_" + n) for n in ("kv", "shifted", "exp", "v", "summed"))
        with ExitStack() as s2:
            KS = s2.enter_context(nc.sbuf_tensor("in_k_shifted", [P, 2, D], F32))
            KE = s2.enter_context(nc.sbuf_tensor("in_k_exp", [P, 2, D], F32))
            V = s2.enter_context(nc.sbuf_tensor("in_v", [P, 2, D], F32))
            PX = s2.enter_context(nc.psum_tensor("ps_in_k2", [P, 2, 512], F32))
            PV = s2.enter_context(nc.psum_tensor("ps_in_v", [P, 2, 512], F32))
            PC = s2.enter_context(nc.psum_tensor("ps_in_context", [P, 2, 512], F32))
            PS = s2.enter_context(nc.psum_tensor("ps_in_k_sum", [P, 2, 512], F32))
            PM = PC[:, 0, :]
            block = s2.enter_context(nc.Block())

            @block.gpsimd
            def _(pool):
                beside(pool, 8)

            @block.sync
            def _(sp):
                load = load_turned(sp, kv, xt_in)
                load(0, 0, True)
                load(1, 1, True)
                with sp.Fori(1, TILES // 2) as j:
                    load(j * 2, 0, False)
                    load(j * 2 + 1, 1, False)
                load(TILES - 1, 0, False)

            @block.tensor
            def _(pe):
                for k in range(2):
                    last = pe.transpose(PM[:, k * P:(k + 1) * P], KM[:, k * P:(k + 1) * P], c.ident[:])
                last.then_inc(spread, 1)
                pe.wait_ge(cs, 3)
                for k in range(2):
                    last = pe.matmul(PM[:, k * P:(k + 1) * P], c.ones[:], KD[:, k, :], start=True, stop=True)
                last.then_inc(spread, 1)

                def project(i, n):
                    if not (isinstance(i, int) and i < 2):
                        pe.wait_ge(shifted, i - 1)
                        pe.wait_ge(v_copied, i - 1)
                    pe.wait_ge(xt_in[n], x_count(i, n) + 16)
                    for k in range(2):
                        pe.matmul(PX[:, n, 0:D], XT[:, n, k, :], WQ[:, k, D:2 * D], start=k == 0, stop=k == 1)
                    for k in range(2):
                        last = pe.matmul(PV[:, n, 0:D], XT[:, n, k, :], WQ[:, k, 2 * D:3 * D], start=k == 0, stop=k == 1)
                    last.then_inc(kv, 1)

                def sum_up(i, n):
                    rows = LAST if isinstance(i, int) and i == TILES - 1 else P
                    pe.wait_ge(expd, i + 1)
                    pe.wait_ge(v_copied, i + 1)
                    first = isinstance(i, int) and i == 0
                    end = isinstance(i, int) and i == TILES - 1
                    for k in range(2):
                        cut = slice(k * P, (k + 1) * P)
                        pe.matmul(PC[:, k, 0:P], V[0:rows, n, cut], KE[0:rows, n, cut], start=first, stop=end,
                                  skip_group_check=True)
                        last = pe.matmul(PS[:, k, 0:1], KE[0:rows, n, cut], c.ones[0:rows, 0:1], start=first, stop=end,
                                         skip_group_check=True)
                    last.then_inc(summed, 1)

                project(0, 0)
                project(1, 1)
                sum_up(0, 0)
                with pe.Fori(1, TILES // 2) as j:
                    project(j * 2, 0)
                    sum_up(j * 2 - 1, 1)
                    project(j * 2 + 1, 1)
                    sum_up(j * 2, 0)
                project(TILES - 1, 0)
                sum_up(TILES - 2, 1)
                sum_up(TILES - 1, 0)
                pe.wait_ge(cs, 6)
                for k in range(2):
                    last = pe.matmul(PX[:, k, 0:D], CT[:, k, :], WO[:, k, :], start=True, stop=True)
                last.then_inc(spread, 1)

            @block.vector
            def _(dve):
                link = Chain(dve, cs)
                dve.wait_ge(spread, 1)
                link(dve.tensor_reduce(KMT[:], PM[:, 0:D].rearrange("p (k n) -> p k n", k=2), AX.X, ALU.max))
                for k in range(2):
                    link(dve.tensor_scalar(KD[:, k, :], c.ident[:], KMT[:, k:k + 1], None, ALU.mult))
                dve.wait_ge(spread, 2)
                link(dve.tensor_copy(KB[:], PM[:, 0:D]))

                def shift(i, n):
                    dve.wait_ge(kv, i + 1)
                    if not (isinstance(i, int) and i < 2):
                        dve.wait_ge(expd, i - 1)
                    dve.tensor_tensor(KS[:, n, :], PX[:, n, 0:D], KB[:], ALU.subtract).then_inc(shifted, 1)

                shift(0, 0)
                shift(1, 1)
                with dve.Fori(1, TILES // 2) as j:
                    shift(j * 2, 0)
                    shift(j * 2 + 1, 1)
                shift(TILES - 1, 0)
                dve.wait_ge(summed, TILES)
                for k in range(2):
                    link(dve.tensor_tensor(CT[:, k, :], PC[:, k, 0:P], c.blocks32[:], ALU.mult))
                for k in range(2):
                    link(dve.reciprocal(SUMS[:, k:k + 1], PS[:, k, 0:1]))
                dve.wait_ge(spread, 3)
                for k in range(2):
                    link(dve.tensor_scalar(CW[:, k, :], PX[:, k, 0:D], SUMS[:, k:k + 1], 32 ** -0.5, ALU.mult, ALU.mult))

            @block.scalar
            def _(act):
                def go(i, n):
                    act.wait_ge(kv, i + 1)
                    if not (isinstance(i, int) and i < 2):
                        act.wait_ge(summed, i - 1)
                    act.copy(V[:, n, :], PV[:, n, 0:D]).then_inc(v_copied, 1)
                    act.wait_ge(shifted, i + 1)
                    act.activation(KE[:, n, :], KS[:, n, :], ACT.Exp).then_inc(expd, 1)

                go(0, 0)
                go(1, 1)
                with act.Fori(1, TILES // 2) as j:
                    go(j * 2, 0)
                    go(j * 2 + 1, 1)
                go(TILES - 1, 0)

        ms = sem("mix_step")
        qt_in = [sem("mix_xt_in0"), sem("mix_xt_in1")]
        q_made, q_shift, q_exp, q_norm, q_turn, q_copied, mixed, mix_out = (
            sem("q_" + n) for n in ("made", "shift", "exp", "norm", "turn", "copied", "mixed", "out"))
        mix_stored = [sem("mix_stored0"), sem("mix_stored1")]
        mix_measured, logged, mix_rooted, mix_apart = (
            sem("mix_" + n) for n in ("measured", "logged", "rooted", "wait_apart"))
        with ExitStack() as s2:
            QM = s2.enter_context(nc.sbuf_tensor("in_q_max", [P, 8], F32))
            QE = s2.enter_context(nc.sbuf_tensor("in_q", [P, 2, D], F32))
            QT = s2.enter_context(nc.sbuf_tensor("in_q_turned", [P, 2, D], F32))
            ST = s2.enter_context(nc.sbuf_tensor("in_mstats", [P, 6], F32))
            MV = s2.enter_context(nc.sbuf_tensor("in_mmean_var", [P, 2], F32))
            MO = s2.enter_context(nc.sbuf_tensor("in_mix_out", [P, 2, D], F32))
            PQ = s2.enter_context(nc.psum_tensor("ps_in_q_ps", [P, 2, 512], F32))
            PT = s2.enter_context(nc.psum_tensor("ps_in_qt_ps", [P, 2, 512], F32))
            PM = s2.enter_context(nc.psum_tensor("ps_in_mix_ps", [P, 2, 512], F32))
            block = s2.enter_context(nc.Block())

            @block.gpsimd
            def _(pool):
                beside(pool, 25)

            @block.tensor
            def _(pe):
                def query(i, n):
                    if not (isinstance(i, int) and i < 2):
                        pe.wait_ge(q_shift, i - 1)
                    pe.wait_ge(qt_in[n], x_count(i, n) + 16)
                    for k in range(2):
                        last = pe.matmul(PQ[:, n, 0:D], XT[:, n, k, :], WQ[:, k, 0:D], start=k == 0, stop=k == 1)
                    last.then_inc(q_made, 1)

                def mix(i, n):
                    pe.wait_ge(q_norm, i + 1)
                    if not (isinstance(i, int) and i < 2):
                        pe.wait_ge(q_copied, i - 1)
                        pe.wait_ge(mix_out, i - 1)
                    for k in range(2):
                        last = pe.transpose(PT[:, n, k * P:(k + 1) * P], QE[:, n, k * P:(k + 1) * P], c.ident[:])
                    last.then_inc(q_turn, 1)
                    pe.wait_ge(q_copied, i + 1)
                    for k in range(2):
                        last = pe.matmul(PM[:, n, 0:D], QT[:, n, k * P:(k + 1) * P], CW[:, k, :], start=k == 0, stop=k == 1)
                    last.then_inc(mixed, 1)

                query(0, 0)
                query(1, 1)
                mix(0, 0)
                query(2, 0)
                mix(1, 1)
                with pe.Fori(1, TILES // 2) as j:
                    query(j * 2 + 1, 1)
                    mix(j * 2, 0)
                    query(j * 2 + 2, 0)
                    mix(j * 2 + 1, 1)
                mix(TILES - 1, 0)

            @block.scalar
            def _(act):
                def exp(i, n):
                    act.wait_ge(q_shift, i + 1)
                    act.activation(QE[:, n, :], QE[:, n, :], ACT.Exp).then_inc(q_exp, 1)

                def copy(i, n):
                    act.wait_ge(q_turn, i + 1)
                    if not (isinstance(i, int) and i < 2):
                        act.wait_ge(mixed, i - 1)
                    act.copy(QT[:, n, :], PT[:, n, 0:D]).then_inc(q_copied, 1)

                def root(i):
                    act.wait_ge(mix_measured, i + 1)
                    act.activation(MV[:, 1:2], MV[:, 1:2], ACT.Ln, bias=c.eps[:, 0:1]).then_inc(logged, 1)
                    act.wait_ge(logged, i + 1)
                    act.activation(MV[:, 1:2], MV[:, 1:2], ACT.Exp, scale=-0.5).then_inc(mix_rooted, 1)

                exp(0, 0)
                exp(1, 1)
                copy(0, 0)
                root(0)
                exp(2, 0)
                copy(1, 1)
                root(1)
                with act.Fori(1, TILES // 2) as j:
                    exp(j * 2 + 1, 1)
                    copy(j * 2, 0)
                    root(j * 2)
                    exp(j * 2 + 2, 0)
                    copy(j * 2 + 1, 1)
                    root(j * 2 + 1)
                copy(TILES - 1, 0)
                root(TILES - 1)

            @block.vector
            def _(dve):
                link = Chain(dve, ms)
                PER_SHIFT, PER_NORM, PER_OUT = 1, 2, 3

                def heads(ap):
                    return ap.rearrange("p (h d) -> p h d", h=8)

                def spread8(ap):
                    return bcast(ap.unsqueeze(2), [P, 8, 32])

                def shift(i, n, at):
                    link.n = at
                    dve.wait_ge(q_made, i + 1)
                    link(dve.tensor_reduce(QM[:], heads(PQ[:, n, 0:D]), AX.X, ALU.max))
                    if not (isinstance(i, int) and i < 2):
                        dve.wait_ge(q_turn, i - 1)
                    dve.tensor_tensor(heads(QE[:, n, :]), heads(PQ[:, n, 0:D]), spread8(QM[:]), ALU.subtract).then_inc(q_shift, 1)
                    dve.wait_ge(q_shift, i + 1)

                def norm(i, n, at):
                    link.n = at
                    dve.wait_ge(q_exp, i + 1)
                    link(dve.tensor_reduce(QM[:], heads(QE[:, n, :]), AX.X, ALU.add))
                    link(dve.reciprocal(QM[:], QM[:]))
                    dve.tensor_tensor(heads(QE[:, n, :]), heads(QE[:, n, :]), spread8(QM[:]), ALU.mult).then_inc(q_norm, 1)
                    dve.wait_ge(q_norm, i + 1)

                def finish(i, n, at, before):
                    link.n = at
                    dve.wait_ge(mixed, i + 1)
                    link(dve.bn_stats(ST[:], PM[:, n, 0:D]))
                    stand_apart(dve, mix_apart)
                    dve.bn_aggr(MV[:], ST[:]).then_inc(mix_measured, 1)
                    dve.wait_ge(mix_rooted, i + 1)
                    if before is not None:
                        dve.wait_ge(mix_stored[n], before)
                    link(dve.tensor_scalar(MO[:, n, :], PM[:, n, 0:D], MV[:, 0:1], MV[:, 1:2], ALU.subtract, ALU.mult))
                    link(dve.tensor_tensor(MO[:, n, :], MO[:, n, :], GA[:], ALU.mult))
                    dve.tensor_tensor(MO[:, n, :], MO[:, n, :], X[:, bass.ds(i, 1), :].rearrange("p w d -> p (w d)"),
                                      ALU.add).then_inc(mix_out, 1)
                    dve.wait_ge(mix_out, i + 1)

                per = PER_SHIFT + PER_NORM + PER_OUT
                shift(0, 0, 0)
                norm(0, 0, 1)
                shift(1, 1, 3)
                norm(1, 1, 4)
                finish(0, 0, 6, None)
                shift(2, 0, 9)
                norm(2, 0, 10)
                finish(1, 1, 12, None)
                base = 15
                with dve.Fori(1, TILES // 2) as j:
                    a = (j - 1) * (2 * per) + base
                    shift(j * 2 + 1, 1, a)
                    norm(j * 2 + 1, 1, a + 1)
                    finish(j * 2, 0, a + 3, j * 16)
                    shift(j * 2 + 2, 0, a + per)
                    norm(j * 2 + 2, 0, a + per + 1)
                    finish(j * 2 + 1, 1, a + per + 3, j * 16)
                finish(TILES - 1, 0, base + 2 * per * (TILES // 2 - 1), 16 * (TILES // 2))

            @block.sync
            def _(sp):
                load = load_turned(sp, q_made, qt_in)

                def store(i, n):
                    sp.wait_ge(mix_out, i + 1)
                    sp.dma_start(rows(d["xm"], i), MO[:, n, :]).then_inc(mix_stored[n], 16)

                load(0, 0, True)
                load(1, 1, True)
                load(2, 0, False)
                store(0, 0)
                load(3, 1, False)
                store(1, 1)
                with sp.Fori(1, TILES // 2 - 1) as j:
                    load(j * 2 + 2, 0, False)
                    store(j * 2, 0)
                    load(j * 2 + 3, 1, False)
                    store(j * 2 + 1, 1)
                load(TILES - 1, 0, False)
                store(TILES - 3, 0)
                store(TILES - 2, 1)
                store(TILES - 1, 0)
                sp.wait_ge(mix_stored[0], 16 * (TILES // 2 + 1))
                sp.wait_ge(mix_stored[1], 16 * (TILES // 2))


class EdgeTables:

    def __init__(self, nc, kept, g):
        def keep(name, shape, dt=F32):
            return kept.enter_context(nc.sbuf_tensor(g.tag + name, shape, dt))

        self.dst = keep("_local_dst", [P, g.grid])
        self.src = keep("_src", [P, g.grid])
        self.chunk_i = keep("_chunk_of_step", [P, g.blocks], I32)
        self.window = keep("_window_of_step", [1, g.grid], I32)


def edge_tables(nc, c, sem, d, g, e, beside):
    t = g.tag
    B = g.blocks
    loaded, step, given = sem(t + "_rows_loaded"), sem(t + "_table_step"), sem(t + "_table_pe")
    stored = sem(t + "_tables_stored")
    fetched, fetched_before = c.pool_fetch[2], c.pool_fetch_before[2]
    c.pool_fetch_before[2] += 16 * B
    turned, taken = sem(t + "_cols_turned"), sem(t + "_cols_taken")
    with ExitStack() as s:
        def sb(name, shape, dt=F32):
            return s.enter_context(nc.sbuf_tensor(t + name, shape, dt))

        R = sb("_pair_rows", [P, B, P, 2])
        KI = sb("_keys_i", [P, B, P, 2], I32)
        KB = sb("_keys_b", [P, B, 2, P], BF16)
        ends = sb("_end_cols", [P, 2 * B])
        endT = sb("_end_rows", [2 * B, P])
        cmp1 = sb("_ended", [P, B, TILES + 1])
        sums = sb("_ended_sum", [P, 2, TILES + 1])
        win = sb("_window_edges", [P, TILES + 1])
        AB = sb("_chunks_at", [P, 2, TILES + 1])
        cnt = sb("_steps_of_window", [P, TILES])
        inc = sb("_steps_until", [P, TILES])
        off = sb("_step_offset", [P, TILES])
        doff = sb("_offset_change", [P, TILES])
        sid_i = sb("_step_id_i", [P, B], I32)
        sid = sb("_step_id", [P, B])
        past = sb("_past", [P, B, TILES])
        pastd = sb("_past_change", [P, B, TILES])
        wstep = sb("_window_f", [P, B])
        cstep = sb("_chunk_f", [P, B])
        wrow = sb("_window_rows", [B, P])
        wrow_i = sb("_window_rows_i", [B, P], I32)
        SR = sb("_step_rows", [P, B, P, 2])
        ps = s.enter_context(nc.psum_tensor(t + "_table_ps", [P, 2, 512], F32))
        pt = s.enter_context(nc.psum_tensor(t + "_cols_ps", [P, 2, 512], F32))
        made = sem(t + "_step_iota")
        block = s.enter_context(nc.Block())
        first, last = ends[:, 0:B], ends[:, B:2 * B]
        jobs = []
        for b in range(B):
            cols = slice(b * P, (b + 1) * P)
            jobs.append(([SR[:, b, :, 0]], e.src[:, cols], lambda a: a[:, 0:P]))
            jobs.append(([SR[:, b, :, 1]], e.dst[:, cols], lambda a: a[:, 0:P]))

        at = {}

        @block.vector
        def _(dve):
            link = Chain(dve, step)
            dve.wait_ge(loaded, 16)
            link(dve.tensor_scalar(R[:, :, :, 0], R[:, :, :, 0], float(N - 1), None, ALU.min))
            link(dve.tensor_copy(KI[:], R[:]))
            link(dve.tensor_scalar(KI[:], KI[:], 255, None, ALU.bitwise_and))
            link(dve.tensor_copy(KB[:].rearrange("p b k e -> p b e k"), KI[:]))
            link(dve.tensor_copy(first, R[:, :, 0, 1]))
            link(dve.tensor_copy(last, R[:, :, P - 1, 1]))
            dve.wait_ge(given, 1)
            link(dve.tensor_copy(endT[:], ps[0:2 * B, 0, 0:P]))
            link(dve.tensor_scalar(win[:], c.row[:, 0:TILES + 1], float(P), None, ALU.mult))
            for k, edge in enumerate((last, first)):
                link(dve.tensor_tensor(cmp1[:], bcast(edge.unsqueeze(2), [P, B, TILES + 1]),
                                       bcast(win[:].unsqueeze(1), [P, B, TILES + 1]), ALU.is_lt))
                link(dve.tensor_reduce(sums[:, k, :], cmp1[:].rearrange("p b w -> p w b"), AX.X, ALU.add))
            dve.wait_ge(given, 2)
            link(dve.tensor_copy(AB[:], ps[:, 1, 0:2 * (TILES + 1)].rearrange("p (k w) -> p k w", k=2)))
            link(dve.tensor_tensor(cnt[:], AB[:, 1, 1:TILES + 1], AB[:, 0, 0:TILES], ALU.subtract))
            link(dve.tensor_tensor_scan(inc[:], cnt[:], c.zeros[:, 0:TILES], 0.0, ALU.add, ALU.add))
            link(dve.tensor_tensor(off[:], AB[:, 0, 0:TILES], inc[:], ALU.subtract))
            link(dve.tensor_tensor(off[:], off[:], cnt[:], ALU.add))
            link(dve.memset(doff[:], 0.0))
            link(dve.tensor_tensor(doff[:, 0:TILES - 1], off[:, 1:TILES], off[:, 0:TILES - 1], ALU.subtract))
            dve.wait_ge(made, 1)
            link(dve.tensor_copy(sid[:], sid_i[:]))
            link(dve.tensor_tensor(past[:], bcast(sid[:].unsqueeze(2), [P, B, TILES]),
                                   bcast(inc[:].unsqueeze(1), [P, B, TILES]), ALU.is_ge))
            link(dve.tensor_reduce(wstep[:], past[:], AX.X, ALU.add))
            link(dve.tensor_tensor(pastd[:], past[:], bcast(doff[:].unsqueeze(1), [P, B, TILES]), ALU.mult))
            dve.wait_ge(given, 3)
            if g.in_psum:
                link(dve.tensor_scalar(wrow[:], ps[0:B, 0, 0:P], float(HIS), float(512 - HIS * g.row), ALU.is_ge, ALU.mult))
                link(dve.scalar_tensor_tensor(wrow_i[:], ps[0:B, 0, 0:P], float(g.row), wrow[:], ALU.mult, ALU.add))
            else:
                link(dve.tensor_copy(wrow_i[:], ps[0:B, 0, 0:P]))
            at["windows"] = link.n
            link(dve.tensor_reduce(cstep[:], pastd[:], AX.X, ALU.add))
            link(dve.tensor_tensor(cstep[:], cstep[:], sid[:], ALU.add))
            link(dve.tensor_scalar(cstep[:], cstep[:], off[:, 0:1], float(g.chunks - 1), ALU.add, ALU.min))
            link(dve.tensor_copy(e.chunk_i[:], cstep[:]))
            at["chunks"] = link.n
            link(dve.tensor_scalar(wstep[:], wstep[:], -float(P), None, ALU.mult))
            for b in range(B):
                if b == 0:
                    dve.wait_ge(fetched, 16 * B + fetched_before)
                link(dve.tensor_scalar(SR[:, b, :, 1], SR[:, b, :, 1], wstep[:, b:b + 1], None, ALU.add))
            at["step_rows"] = link.n

        @block.sync
        def _(sp):
            sp.dma_start(R[:].rearrange("p b e k -> p b (e k)"),
                         d[t + "_pairs"].rearrange("(b c e) k -> c b (e k)", c=P, e=P)).then_inc(loaded, 16)
            sp.wait_ge(step, 1)
            sp.dma_start(d[t + "_edge_rows"].rearrange("(b c) x -> c b x", c=P),
                         R[:].rearrange("p b e k -> p b (e k)")).then_inc(stored, 16)
            sp.wait_ge(step, 4)
            sp.dma_start(d[t + "_keys"].rearrange("(b c) x -> c b x", c=P),
                         KB[:].rearrange("p b k e -> p b (k e)")).then_inc(stored, 16)
            sp.wait_ge(step, 7)
            sp.dma_start(d[t + "_ends"].rearrange("k (b c) -> (k b) c", c=P), endT[:]).then_inc(stored, 16)
            sp.wait_ge(step, at["windows"])
            sp.dma_start(d[t + "_windows"].rearrange("(b c) -> b c", c=P), wrow_i[:]).then_inc(stored, 16)
            sp.wait_ge(stored, 64)
            sp.dma_start(e.window[:], d[t + "_windows"].rearrange("(o s) -> o s", o=1)).then_inc(loaded, 16)
            sp.wait_ge(loaded, 32)

        @block.gpsimd
        def _(pool):
            pool.iota(sid_i[:], [[P, B]], 0, 1).then_inc(made, 1)
            if beside:
                beside(pool, 3)
            pool.wait_ge(stored, 64)
            pool.wait_ge(step, at["chunks"])
            for b in range(B):
                pool.indirect_dma_start(out=SR[:, b, :, :].rearrange("p e k -> p (e k)"), out_offset=None,
                                        in_=d[t + "_edge_rows"],
                                        in_offset=bass.IndirectOffsetOnAxis(ap=e.chunk_i[:, b:b + 1], axis=0)
                                        ).then_inc(fetched, 16)

        @block.tensor
        def _(pe):
            pe.wait_ge(step, 6)
            pe.transpose(ps[0:2 * B, 0, 0:P], ends[:], c.ident[:]).then_inc(given, 1)
            pe.wait_ge(step, 12)
            pe.matmul(ps[:, 1, 0:2 * (TILES + 1)], c.ones[:], sums[:].rearrange("p k w -> p (k w)"),
                      start=True, stop=True).then_inc(given, 1)
            pe.wait_ge(step, 22)
            pe.transpose(ps[0:B, 0, 0:P], wstep[:], c.ident[:]).then_inc(given, 1)
            pe.wait_ge(step, at["step_rows"])
            transposes(nc, pe, None, jobs, pt, turned, taken, c.ident[:])

        @block.scalar
        def _(act):
            transposes(nc, None, act, jobs, pt, turned, taken, c.ident[:])


class Scores:

    def __init__(self, nc, kept, g):
        self.hi = kept.enter_context(nc.sbuf_tensor(g.tag + "_hi_cols", [P, g.grid, 2], F32))
        self.cols = kept.enter_context(nc.sbuf_tensor(g.tag + "_scores_cols", [P, g.grid, H], F32))


def hi_columns(nc, c, sem, d, g, sc, beside):
    t = g.tag
    B, GR = g.blocks, g.grid
    hturned, htaken = sem(t + "_hi_turned"), sem(t + "_hi_taken")
    rows_in, hstep = sem(t + "_rows_in"), sem(t + "_hi_step")
    with ExitStack() as s2:
        R = s2.enter_context(nc.sbuf_tensor(t + "_rows2", [P, B, P, 2], F32))
        HIr = sc.cols[:].rearrange("p s h -> p (s h)")[:, 0:GR * 2].bitcast(I32).rearrange("p (b e k) -> p b e k", b=B, k=2)
        pt = s2.enter_context(nc.psum_tensor(t + "_hi_ps", [P, 2, 512], F32))
        block = s2.enter_context(nc.Block())
        jobs = [([R[:, b, :, k]], sc.hi[:, b * P:(b + 1) * P, k], lambda a: a[:, 0:P]) for b in range(B) for k in range(2)]
        at = {}

        @block.vector
        def _(dve):
            link = Chain(dve, hstep)
            dve.wait_ge(rows_in, 16)
            link(dve.tensor_copy(HIr, R[:]))
            link(dve.tensor_scalar(HIr, HIr, 8, None, ALU.arith_shift_right))
            link(dve.tensor_copy(R[:], HIr))
            at["hi"] = link.n
            link(dve.memset(sc.cols[:], 0.0))

        @block.sync
        def _(sp):
            sp.dma_start(R[:].rearrange("p b e k -> p b (e k)"),
                         d[t + "_edge_rows"].rearrange("(b c) x -> c b x", c=P)).then_inc(rows_in, 16)

        @block.tensor
        def _(pe):
            pe.wait_ge(hstep, at["hi"])
            transposes(nc, pe, None, jobs, pt, hturned, htaken, c.ident[:])

        @block.scalar
        def _(act):
            transposes(nc, None, act, jobs, pt, hturned, htaken, c.ident[:])

        @block.gpsimd
        def _(pool):
            beside(pool, 2)


def score_rows(nc, c, sem, g, sc, ER):
    t = g.tag
    turned, taken, leaky = sem(t + "_sc_turned"), sem(t + "_sc_taken"), sem(t + "_leaky")
    with ExitStack() as s2:
        pt = s2.enter_context(nc.psum_tensor(t + "_rows_ps", [P, 4, 512], F32))
        block = s2.enter_context(nc.Block())
        EC = sc.cols
        jobs = []
        for h in range(H):
            for b0 in range(0, g.blocks, 4):
                bs = list(range(b0, min(g.blocks, b0 + 4)))
                jobs.append(([EC[:, b * P:(b + 1) * P, h] for b in bs],
                             ER[:, h, bs[0]:bs[-1] + 1, :].rearrange("p b e -> p (b e)"),
                             lambda a, n=len(bs): a[:, 0:n * P]))

        @block.vector
        def _(dve):
            dve.scalar_tensor_tensor(EC[:], EC[:], g.slope, EC[:], ALU.mult, ALU.max).then_inc(leaky, 1)

        @block.tensor
        def _(pe):
            pe.wait_ge(leaky, 1)
            transposes(nc, pe, None, jobs, pt, turned, taken, c.ident[:])

        @block.scalar
        def _(act):
            transposes(nc, None, act, jobs, pt, turned, taken, c.ident[:])


def look_up_scores(nc, c, sem, d, g, sc, start, nb, beside, rounds):
    t = "%s_from%d" % (g.tag, start)
    CH = 4
    assert nb % 4 == 0
    EC, HC = sc.cols, sc.hi
    keys_in = [sem(t + "_keys_in%d" % i) for i in range(4)]
    onehot, onehot_too, distant, looked, summed, hi_made, picked = (
        sem(t + n) for n in ("_onehot", "_onehot_too", "_distance", "_looked_up", "_score_masked", "_hi_made", "_score_picked"))
    with ExitStack() as s2:
        def sb(name, shape, dt=F32):
            return s2.enter_context(nc.sbuf_tensor(t + name, shape, dt))

        KB = sb("_keys_everywhere", [P, 4, CH * 2 * P], BF16)
        OH = sb("_lo_onehot", [P, 2, 2, CH * 2 * P], BF16)
        HH = sb("_hi_onehot", [P, 2, CH, 2 * HIS])
        PR = sb("_masked", [P, CH, 2 * HIS, H])
        DI = sb("_distance", [P, 2, CH * 2 * P], BF16)
        ps = s2.enter_context(nc.psum_tensor(t + "_lookup_ps", [P, 2, CH, 256], F32))
        block = s2.enter_context(nc.Block())

        @block.vector
        def _(dve):
            def masks(i, n, m, j):
                dve.wait_ge(keys_in[n], j * 16 + 16)
                if not (isinstance(i, int) and i < 2):
                    dve.wait_ge(looked, i - 1)
                dve.tensor_scalar(OH[:, m, 0, :], KB[:, n, :], c.lo[:, 0:1], None, ALU.is_equal).then_inc(onehot, 1)

            def high(i, m):
                hc = HC[:, bass.ds((i + start) * CH, CH), :]
                if not (isinstance(i, int) and i < 2):
                    dve.wait_ge(summed, i - 1)
                dve.tensor_tensor(HH[:, m].rearrange("p u (k h) -> p (u k) h", k=2),
                                  bcast(hc.rearrange("p u k -> p (u k)").unsqueeze(2), [P, CH * 2, HIS]),
                                  bcast(c.row[:, 0:HIS].unsqueeze(1), [P, CH * 2, HIS]),
                                  ALU.is_equal).then_inc(hi_made, 1)

            def pick(i, m, ahead=True):
                dve.wait_ge(hi_made, i + 1)
                dve.wait_ge(looked, i + 1)
                if not (isinstance(i, int) and i < 1):
                    dve.wait_ge(picked, i)
                dve.tensor_tensor(PR[:], ps[:, m, :, 0:2 * HIS * H].rearrange("p u (x h) -> p u x h", h=H),
                                  bcast(HH[:, m].unsqueeze(3), [P, CH, 2 * HIS, H]), ALU.mult).then_inc(summed, 1)
                if ahead:
                    high(i + 1, 1 - m)
                dve.wait_ge(summed, i + 1)
                dve.tensor_reduce(EC[:, bass.ds((i + start) * CH, CH), :], PR[:].rearrange("p u x h -> p u h x"), AX.X,
                                  ALU.add).then_inc(picked, 1)

            high(0, 0)
            for i in range(4):
                masks(i, i, i % 2, 0)
                if i:
                    pick(i - 1, (i - 1) % 2)
            with dve.Fori(1, nb // 4) as j:
                for n in range(4):
                    masks(j * 4 + n, n, n % 2, j)
                    pick(j * 4 + n - 1, (n - 1) % 2)
            pick(nb - 1, (nb - 1) % 2, False)

        @block.sync
        def _(sp):
            keys = d[g.tag + "_keys"].rearrange("(n u) x -> n (u x)", u=CH)

            def load(i, n, first):
                if not first:
                    sp.wait_ge(onehot, i - 3)
                    sp.wait_ge(distant, i - 3)
                src_ = keys[bass.ds(i + start, 1), :].rearrange("n x -> (n x)").partition_broadcast(P)
                sp.dma_start(KB[:, n, :], src_).then_inc(keys_in[n], 16)

            for n in range(4):
                load(n, n, True)
            with sp.Fori(1, nb // 4) as j:
                for n in range(4):
                    load(j * 4 + n, n, False)

        @block.tensor
        def _(pe):
            def look(i, m):
                pe.wait_ge(onehot, i + 1)
                pe.wait_ge(onehot_too, i + 1)
                if not (isinstance(i, int) and i < 2):
                    pe.wait_ge(summed, i - 1)
                for u in range(CH):
                    for k in range(2):
                        to = ps[:, m, u, k * HIS * H:(k + 1) * HIS * H]
                        for par in range(2):
                            for q in range(3):
                                last = pe.matmul(to, OH[:, m, par, (u * 2 + k) * P:(u * 2 + k + 1) * P],
                                                 c.scores[:, q, k, par, :, :].rearrange("p a h -> p (a h)"),
                                                 start=par == 0 and q == 0, stop=par == 1 and q == 2)
                last.then_inc(looked, 1)

            for i in range(4):
                look(i, i % 2)
            with pe.Fori(1, nb // 4) as j:
                for n in range(4):
                    look(j * 4 + n, n % 2)

        @block.gpsimd
        def _(pool):
            beside(pool, rounds)

        @block.scalar
        def _(act):
            def masks(i, n, m, j):
                act.wait_ge(keys_in[n], j * 16 + 16)
                if not (isinstance(i, int) and i < 2):
                    act.wait_ge(onehot_too, i - 1)
                act.activation(DI[:, m, :], KB[:, n, :], ACT.Abs, scale=-1.0, bias=c.lo[:, 1:2]).then_inc(distant, 1)
                if not (isinstance(i, int) and i < 2):
                    act.wait_ge(looked, i - 1)
                act.wait_ge(distant, i + 1)
                act.activation(OH[:, m, 1, :], DI[:, m, :], ACT.Relu, scale=-1.0, bias=c.ones[:, 0:1]
                               ).then_inc(onehot_too, 1)

            for i in range(4):
                masks(i, i, i % 2, 0)
            with act.Fori(1, nb // 4) as j:
                for n in range(4):
                    masks(j * 4 + n, n, n % 2, j)


def subtract_maximum(nc, c, sem, d, g, ER, beside, rounds):
    t = g.tag
    B, GR = g.blocks, g.grid
    step, given = sem(t + "_max_step"), sem(t + "_max_pe")
    loaded, stored, ends_in = sem(t + "_max_loaded"), sem(t + "_max_stored"), sem(t + "_ends_in")
    weights, saved = sem(t + "_weights"), sem(t + "_weights_saved")
    with ExitStack() as s2:
        def sb(name, shape, dt=F32):
            return s2.enter_context(nc.sbuf_tensor(t + name, shape, dt))

        X = [sb("_max_fwd", [P, H, B, P]), sb("_max_bwd", [P, H, B, P])]
        DR = sb("_dst_rows", [P, B, P])
        RS = [sb("_reset_fwd", [P, B, P]), sb("_reset_bwd", [P, B, P])]
        TC = sb("_tails_cols", [P, 2, H * B])
        TR = sb("_tails_rows", [H * B, 2, P])
        Q = 32 + H
        FL = sb("_ends_line", [Q, 2, GR])
        A, U, V = (X[1][0:Q, h].rearrange("p b c -> p (b c)") for h in range(3))
        pm = s2.enter_context(nc.psum_tensor(t + "_max_ps", [P, 2, 512], F32))
        block = s2.enter_context(nc.Block())
        fwd, bwd = slice(0, H), slice(32, 32 + H)
        pairs = X[0][:, 0:2].rearrange("p h b e -> p (h b e)").rearrange("p (b e k) -> p b e k", b=B, k=2)
        at = {}

        def flat(ap):
            return ap.rearrange("p b e -> p (b e)")

        def scans(dve, link):
            for h in range(H):
                a = flat(X[0][:, h])
                link(dve.tensor_tensor_scan(a, flat(RS[0][:]), a, -BIG, ALU.add, ALU.max))
                a = flat(X[1][:, h])[:, ::-1]
                link(dve.tensor_tensor_scan(a, flat(RS[1][:])[:, ::-1], a, -BIG, ALU.add, ALU.max))

        @block.vector
        def _(dve):
            link = Chain(dve, step)
            dve.wait_ge(ends_in, 48)
            link(dve.tensor_copy(DR[:], pairs[:, :, :, 1]))
            for k, r in enumerate(RS):
                link(dve.memset(r[:], 1.0))
                link(dve.tensor_tensor(r[:, :, 1 - k:P - k], DR[:, :, 1:P], DR[:, :, 0:P - 1], ALU.not_equal))
                link(dve.tensor_scalar(r[:], r[:], -BIG, None, ALU.mult))
            for k in range(2):
                link(dve.tensor_copy(X[k][:], ER[:]))
            scans(dve, link)
            link(dve.tensor_copy(TC[:, 0, :].rearrange("p (h b) -> p h b", h=H), X[0][:, :, :, P - 1]))
            link(dve.tensor_copy(TC[:, 1, :].rearrange("p (h b) -> p h b", h=H), X[1][:, :, :, 0]))
            at["tail_cols"] = link.n
            for part in (fwd, bwd):
                link(dve.tensor_tensor(V[part], FL[part, 0, :], FL[part, 1, :], ALU.is_equal))
                link(dve.tensor_tensor(U[part, 1:GR], FL[part, 0, 1:GR], FL[part, 1, 0:GR - 1], ALU.is_equal))
                link(dve.memset(U[part, 0:1], 0.0))
                link(dve.tensor_scalar(FL[part, 0, :], U[part], 1.0, BIG, ALU.subtract, ALU.mult))
            link(dve.tensor_tensor(A[fwd], V[fwd], U[fwd], ALU.mult))
            link(dve.memset(A[bwd], 0.0))
            link(dve.tensor_tensor(A[bwd, 0:GR - 1], V[bwd, 0:GR - 1], U[bwd, 1:GR], ALU.mult))
            for part in (fwd, bwd):
                link(dve.tensor_scalar(A[part], A[part], 1.0, BIG, ALU.subtract, ALU.mult))
            at["line_free"] = link.n
            dve.wait_ge(given, 1)
            link(dve.tensor_copy(TR[:], pm[0:H * B, 0, 0:2 * P].rearrange("p (k c) -> p k c", k=2)))
            at["tails"] = link.n
            dve.wait_ge(loaded, 32)
            a = U[fwd]
            link(dve.tensor_tensor_scan(a, A[fwd], a, -BIG, ALU.add, ALU.max))
            a = U[bwd][:, ::-1]
            link(dve.tensor_tensor_scan(a, A[bwd][:, ::-1], a, -BIG, ALU.add, ALU.max))
            for part in (fwd, bwd):
                link(dve.memset(V[part], -BIG))
            link(dve.tensor_tensor(V[fwd, 1:GR], U[fwd, 0:GR - 1], FL[fwd, 0, 1:GR], ALU.add))
            link(dve.tensor_tensor(V[bwd, 0:GR - 1], U[bwd, 1:GR], FL[bwd, 0, 1:GR], ALU.add))
            at["carries"] = link.n
            dve.wait_ge(given, 2)
            for k in range(2):
                link(dve.tensor_copy(X[k][:], ER[:]))
            for k in range(2):
                edge = X[k][:, :, :, (P - 1) * k]
                link(dve.tensor_tensor(edge, edge, pm[:, 1, k * H * B:(k + 1) * H * B].rearrange("p (h b) -> p h b", h=H), ALU.max))
            scans(dve, link)
            link(dve.tensor_tensor(X[0][:], X[0][:], X[1][:], ALU.max))
            link(dve.tensor_tensor(X[0][:], ER[:], X[0][:], ALU.subtract))
            at["shifted"] = link.n

        @block.sync
        def _(sp):
            sp.dma_start(pairs.rearrange("p b e k -> p b (e k)"),
                         d[t + "_edge_rows"].rearrange("(b c) x -> c b x", c=P)).then_inc(ends_in, 16)
            for part in (fwd, bwd):
                sp.dma_start(FL[part], d[t + "_ends"].partition_broadcast(H)).then_inc(ends_in, 16)
            sp.wait_ge(step, at["tails"])
            sp.dma_start(d[t + "_tails"].rearrange("k h (b c) -> (h b) k c", c=P), TR[:]).then_inc(stored, 16)
            sp.wait_ge(stored, 16)
            for k, part in enumerate((fwd, bwd)):
                sp.dma_start(U[part], d[t + "_tails"][k]).then_inc(loaded, 16)
            sp.wait_ge(step, at["carries"])
            for k, part in enumerate((fwd, bwd)):
                sp.dma_start(d[t + "_carries"][k], V[part]).then_inc(stored, 16)
            sp.wait_ge(stored, 48)
            sp.dma_start(TR[:], d[t + "_carries"].rearrange("k h (b c) -> (h b) k c", c=P)).then_inc(loaded, 16)
            sp.wait_ge(weights, 1)
            rows = d[t + "_weight_rows"].rearrange("(b c) (h e) -> h c b e", c=P, h=H)
            for h in range(H):
                sp.dma_start(rows[h], X[0][:, h]).then_inc(saved, 16)
            sp.wait_ge(saved, 64)

        @block.tensor
        def _(pe):
            pe.wait_ge(step, at["tail_cols"])
            for k in range(2):
                last = pe.transpose(pm[0:H * B, 0, k * P:(k + 1) * P], TC[:, k, :], c.ident[:])
            last.then_inc(given, 1)
            pe.wait_ge(loaded, 48)
            for k in range(2):
                last = pe.transpose(pm[:, 1, k * H * B:(k + 1) * H * B], TR[:, k, :], c.ident[0:H * B, 0:H * B])
            last.then_inc(given, 1)

        @block.scalar
        def _(act):
            act.wait_ge(step, at["shifted"])
            act.activation(X[0][:], X[0][:], ACT.Exp).then_inc(weights, 1)

        @block.gpsimd
        def _(pool):
            beside(pool, rounds)


def fetch_weights(nc, s, c, sem, d, g, e):
    t = g.tag
    B = g.blocks
    W = s.enter_context(nc.sbuf_tensor(t + "_weights", [P, g.grid, H], F32))
    fetched, before = c.pool_fetch[0:2], c.pool_fetch_before[0:2]
    for n in range(2):
        c.pool_fetch_before[n] += 16 * ((B + 1 - n) // 2)
    turned, taken = sem(t + "_weights_turned"), sem(t + "_weights_taken")
    with ExitStack() as s2:
        WR = s2.enter_context(nc.sbuf_tensor(t + "_weight_rows_in", [P, 2, H * P], F32))
        pt = s2.enter_context(nc.psum_tensor(t + "_weights_ps", [P, 2, 512], F32))
        block = s2.enter_context(nc.Block())

        @block.gpsimd
        def _(pool):
            for b in range(B):
                if b >= 2:
                    pool.wait_ge(turned, b - 1)
                pool.indirect_dma_start(out=WR[:, b % 2, :], out_offset=None, in_=d[t + "_weight_rows"],
                                        in_offset=bass.IndirectOffsetOnAxis(ap=e.chunk_i[:, b:b + 1], axis=0)
                                        ).then_inc(fetched[b % 2], 16)

        @block.tensor
        def _(pe):
            for b in range(B):
                pe.wait_ge(fetched[b % 2], 16 * (b // 2 + 1) + before[b % 2])
                if b >= 2:
                    pe.wait_ge(taken, b - 1)
                for h in range(H):
                    last = pe.transpose(pt[:, b % 2, h * P:(h + 1) * P], WR[:, b % 2, h * P:(h + 1) * P], c.ident[:])
                last.then_inc(turned, 1)

        @block.scalar
        def _(act):
            for b in range(B):
                act.wait_ge(turned, b + 1)
                act.copy(W[:, b * P:(b + 1) * P, :].rearrange("p s h -> p h s"),
                         pt[:, b % 2, :].rearrange("p (h s) -> p h s", h=H)).then_inc(taken, 1)
    return W


def aggregate(nc, ctx, c, sem, d, g, e):
    t = g.tag
    F = g.width + 1
    ACC = ctx.enter_context(nc.sbuf_tensor(t + "_sums", [P, TILES + 1, g.row], F32))
    AH = 3
    act_apart, scaled_too = sem(t + "_act_wait_apart"), sem(t + "_rows_scaled_too")
    cleared, pool_apart, staged, scaled, multiplied, added = (
        sem(t + n) for n in ("_sums_cleared", "_pool_wait_apart", "_index_staged", "_rows_scaled", "_step_summed", "_step_added"))
    got = c.ring_done[t + "_gather"]
    loops = g.steps // UNROLL
    Q = UNROLL // len(got)
    BUF = 4
    with ExitStack() as s2:
        W = fetch_weights(nc, s2, c, sem, d, g, e)
        slot = s2.enter_context(nc.sbuf_tensor(t + "_index_slots", [P, UNROLL], I32))
        G = s2.enter_context(nc.sbuf_tensor(t + "_gathered", [P, UNROLL, g.row], F32))
        ZW = s2.enter_context(nc.sbuf_tensor(t + "_scaled", [P, BUF, g.row], F32))
        OH = s2.enter_context(nc.sbuf_tensor(t + "_dst_onehot", [P, BUF, P], F32))
        ps = s2.enter_context(nc.psum_tensor(t + "_step_ps", [P, BUF, 512], F32))
        block = s2.enter_context(nc.Block())

        @block.scalar
        def _(act):
            def scale(i, u, first):
                st = i * UNROLL + u
                if not (first and u < BUF):
                    act.wait_ge(multiplied, st - (BUF - 1))
                    stand_apart(act, act_apart)
                if u % Q == 0:
                    act.wait_ge(got[u // Q], i * (16 * Q) + 16 * Q)
                    stand_apart(act, act_apart)
                for h in range(AH):
                    last = act.activation(ZW[:, u % BUF, h * F:(h + 1) * F], G[:, u, h * F:(h + 1) * F], ACT.Copy,
                                          scale=W[:, bass.ds(st, 1), h])
                last.then_inc(scaled_too, 1)

            for u in range(UNROLL):
                scale(0, u, True)
            with act.Fori(1, loops) as i:
                for u in range(UNROLL):
                    scale(i, u, False)

        @block.gpsimd
        def _(pool):
            def gather(i, k, first):
                lo = k * Q
                if not first:
                    for q in (scaled, scaled_too):
                        pool.wait_ge(q, i * UNROLL + (lo + Q - UNROLL))
                        stand_apart(pool, pool_apart)
                pool.tensor_copy(slot[:, lo:lo + Q], e.src[:, bass.ds(i * UNROLL + lo, Q)]).then_inc(staged, 1)
                pool.wait_ge(staged, i * (UNROLL // Q) + (k + 1))
                stand_apart(pool, pool_apart)
                for u in range(lo, lo + Q):
                    pool.indirect_dma_start(out=G[:, u, :], out_offset=None, in_=d[t + "_rows"],
                                            in_offset=bass.IndirectOffsetOnAxis(ap=slot[:, u:u + 1], axis=0)
                                            ).then_inc(got[k], 16)

            for k in range(UNROLL // Q):
                gather(0, k, True)
            with pool.Fori(1, loops) as i:
                for k in range(UNROLL // Q):
                    gather(i, k, False)

        @block.vector
        def _(dve):
            dve.memset(ACC[:], 0.0).then_inc(cleared, 1)
            dve.wait_ge(cleared, 1)

            def scale(i, u, first):
                st = i * UNROLL + u
                if not (first and u < BUF):
                    dve.wait_ge(multiplied, st - (BUF - 1))
                dve.tensor_scalar(OH[:, u % BUF, :], c.row[:], e.dst[:, bass.ds(st, 1)], None, ALU.is_equal)
                if u % Q == 0:
                    dve.wait_ge(got[u // Q], i * (16 * Q) + 16 * Q)
                dve.tensor_scalar(ZW[:, u % BUF, AH * F:H * F], G[:, u, AH * F:H * F], W[:, bass.ds(st, 1), AH], None,
                                  ALU.mult).then_inc(scaled, 1)

            def add(i, u, first, w):
                st = i * UNROLL + u
                to = ACC[:, bass.ds(w, 1), :].rearrange("p w f -> p (w f)")
                dve.wait_ge(multiplied, st + 1)
                if not (first and u == 0):
                    dve.wait_ge(added, st)
                dve.tensor_tensor(to, to, ps[:, u % BUF, 0:g.row], ALU.add).then_inc(added, 1)

            def group(i, first):
                _, windows = nc.values_load_multi_w_load_instructions(e.window[0:1, bass.ds(i * UNROLL, UNROLL)],
                                               engines=[mybir.EngineType.DVE], min_val=0, max_val=TILES,
                                               skip_runtime_bounds_check_because="counts of windows passed")
                for u in range(UNROLL):
                    scale(i, u, first)
                    if u >= 2:
                        add(i, u - 2, first, windows[u - 2])
                for u in range(UNROLL - 2, UNROLL):
                    add(i, u, first, windows[u])

            group(0, True)
            with dve.Fori(1, loops) as i:
                group(i, False)
            dve.wait_ge(added, g.steps)

        @block.tensor
        def _(pe):
            def group(i, first):
                for u in range(UNROLL):
                    st = i * UNROLL + u
                    pe.wait_ge(scaled, st + 1)
                    pe.wait_ge(scaled_too, st + 1)
                    if not (first and u < BUF):
                        pe.wait_ge(added, st - (BUF - 1))
                    pe.matmul(ps[:, u % BUF, 0:g.row], OH[:, u % BUF, :], ZW[:, u % BUF, :], start=True,
                              stop=True).then_inc(multiplied, 1)

            group(0, True)
            with pe.Fori(1, loops) as i:
                group(i, False)
    return ACC


class Gather:

    def __init__(self, nc, kept, c, d, g, e):
        t = g.tag
        self.rows, self.src, self.loops, self.done_loops = d[t + "_rows"], e.src, g.steps // UNROLL, 0
        self.out = kept.enter_context(nc.sbuf_tensor(t + "_gathered", [P, g.steps, g.width * H], F32))
        self.slot = kept.enter_context(nc.sbuf_tensor(t + "_slot_index", [P, UNROLL], I32))
        self.room = kept.enter_context(nc.sbuf_tensor(t + "_slot_rows", [P, UNROLL, g.width * H], F32))
        self.staged, self.moved, self.apart = (c.held.enter_context(nc.semaphore(t + n)) for n in (
            "_slots_staged", "_rows_moved", "_gather_wait_apart"))
        self.got = c.ring_done[t + "_gather"]

    def issue(self, pool, i, k):
        lo = k * RING
        pool.tensor_copy(self.slot[:, lo:lo + RING], self.src[:, bass.ds(i * UNROLL + lo, RING)]
                         ).then_inc(self.staged, 1)
        pool.wait_ge(self.staged, i * 2 + (k + 1))
        stand_apart(pool, self.apart)
        for u in range(lo, lo + RING):
            pool.indirect_dma_start(out=self.room[:, u, :], out_offset=None, in_=self.rows,
                                    in_offset=bass.IndirectOffsetOnAxis(ap=self.slot[:, u:u + 1], axis=0)
                                    ).then_inc(self.got[k], 16)

    def move(self, pool, i, k):
        lo = k * RING
        pool.wait_ge(self.got[k], i * (16 * RING) + 16 * RING)
        stand_apart(pool, self.apart)
        pool.tensor_copy(self.out[:, bass.ds(i * UNROLL + lo, RING), :], self.room[:, lo:lo + RING, :]
                         ).then_inc(self.moved, 1)
        pool.wait_ge(self.moved, i * 2 + (k + 1))
        stand_apart(pool, self.apart)

    def share(self, pool, loops):
        i, end = self.done_loops, min(self.loops, self.done_loops + loops)
        if i == 0:
            for k in range(2):
                self.issue(pool, 0, k)
            i = 1
        if i < end:
            with pool.Fori(i, end) as i:
                for k in range(2):
                    self.move(pool, i - 1, k)
                    self.issue(pool, i, k)
        if end == self.loops and self.done_loops < end:
            for k in range(2):
                self.move(pool, end - 1, k)
        self.done_loops = end


def add_up(nc, kept, c, sem, d, g, e, gather):
    t = g.tag
    F = g.width
    S = 8
    ACC = kept.enter_context(nc.sbuf_tensor(t + "_sums", [P, 2 * HIS, g.row], F32))
    act_apart = sem(t + "_act_wait_apart")
    masked, scaled, weighed, zeroed, multiplied, whole = (
        sem(t + n) for n in ("_masked", "_scaled", "_weighed", "_zeroed", "_multiplied", "_whole"))
    loops = g.steps // UNROLL
    with ExitStack() as s2:
        W = fetch_weights(nc, s2, c, sem, d, g, e)
        ZW = s2.enter_context(nc.sbuf_tensor(t + "_scaled_rows", [P, 2, S, H, F + 1], F32))
        OH = s2.enter_context(nc.sbuf_tensor(t + "_dst_onehot", [P, 2, S, P], F32))
        ps = s2.enter_context(nc.psum_tensor(t + "_sums_ps", [P, 2 * 512], F32))
        block = s2.enter_context(nc.Block())

        def rounds(engine, batch):
            for k in range(2):
                batch(0, k, True)
            with engine.Fori(1, loops) as i:
                for k in range(2):
                    batch(i, k, False)

        @block.vector
        def _(dve):
            def batch(i, k, first):
                at = bass.ds(i * UNROLL + k * S, S)
                if not first:
                    dve.wait_ge(multiplied, i * 2 + (k - 1))
                dve.tensor_tensor(OH[:, k], bcast(e.dst[:, at].unsqueeze(2), [P, S, P]),
                                  bcast(c.row[:].unsqueeze(1), [P, S, P]), ALU.is_equal).then_inc(masked, 1)
                dve.wait_ge(gather.moved, i * 2 + (k + 1))
                dve.tensor_tensor(ZW[:, k, :, :, 0:F], gather.out[:, at, :].rearrange("p s (h f) -> p s h f", h=H),
                                  bcast(W[:, at, :].unsqueeze(3), [P, S, H, F]), ALU.mult).then_inc(scaled, 1)

            rounds(dve, batch)
            dve.wait_ge(whole, 1)
            for k in range(2):
                dve.tensor_copy(ACC[:, k * HIS:(k + 1) * HIS, :],
                                ps[:, k * 512:k * 512 + HIS * g.row].rearrange("p (w f) -> p w f", f=g.row))

        @block.scalar
        def _(act):
            def batch(i, k, first):
                if not first:
                    act.wait_ge(multiplied, i * 2 + (k - 1))
                    stand_apart(act, act_apart)
                act.copy(ZW[:, k, :, :, F], W[:, bass.ds(i * UNROLL + k * S, S), :]).then_inc(weighed, 1)

            rounds(act, batch)

        @block.gpsimd
        def _(pool):
            gather.share(pool, REST)

        @block.tensor
        def _(pe):
            for k in range(2):
                last = pe.matmul(ps[:, k * 512:(k + 1) * 512], c.zeros[:, 0:P], c.zeros[:, 0:512], start=True, stop=False,
                                 skip_group_check=True)
            last.then_inc(zeroed, 1)
            pe.wait_ge(zeroed, 1)
            at = []

            def batch(i, k, first):
                if k == 0:
                    _, at[:] = nc.values_load_multi_w_load_instructions(
                        e.window[0:1, bass.ds(i * UNROLL, UNROLL)], engines=[mybir.EngineType.PE], min_val=0,
                        max_val=1024 - g.row, skip_runtime_bounds_check_because="places of the windows passed")
                for q in (masked, scaled, weighed):
                    pe.wait_ge(q, i * 2 + (k + 1))
                for u in range(S):
                    last = pe.matmul(ps[:, bass.ds(at[k * S + u], g.row)], OH[:, k, u, :],
                                     ZW[:, k, u].rearrange("p h f -> p (h f)"), start=False, stop=False,
                                     skip_group_check=True)
                last.then_inc(multiplied, 1)

            rounds(pe, batch)
            pe.wait_ge(multiplied, 2 * loops)
            pe.sem_inc(whole, 1)
    return ACC


def nodes_between(nc, c, sem, d, acc, wgat, fas, fad):
    W = D // H
    E = 4
    GT = 7
    GROUPS = TILES // GT
    BANKS = 4
    assert GROUPS * GT == TILES and GROUPS % 2 == 1
    step, loaded, made, x_out, turned, copied, projected, scored, rows_out = (
        sem("mid_" + n) for n in ("step", "loaded", "xn", "x1", "turned", "copied", "projected", "scored", "rows_out"))
    measured, rooted, apart, act_apart = (sem("mid_" + n) for n in ("measured", "rooted", "wait_apart", "act_wait_apart"))
    xm_in = [sem("mid_xm_in0"), sem("mid_xm_in1")]
    x_stored = [sem("mid_x_stored0"), sem("mid_x_stored1")]
    h_stored = [sem("mid_h_stored0"), sem("mid_h_stored1")]

    def groups(engine, body):
        body(0, 0, True)
        body(1, 1, True)
        body(2, 0, False)
        with engine.Fori(1, GROUPS // 2) as j:
            body(j * 2 + 1, 1, False)
            body(j * 2 + 2, 0, False)

    def last_user(q):
        return BANKS if q >= BANKS else GT - max(p for p in range(GT) if p % BANKS == q) + q

    with ExitStack() as s:
        def sb(name, shape, dt=F32):
            return s.enter_context(nc.sbuf_tensor("mid_" + name, shape, dt))

        WG = sb("w_gat", [P, 2, 24])
        AT = sb("att", [P, 2, 16])
        PR = sb("att_products", [P, 16])
        XM = sb("xm", [P, 2, GT, D])
        X1 = sb("x1", [P, 2, GT, D])
        XN = sb("xn", [P, 2, GT, D])
        XT = sb("xn_turned", [P, BANKS, D])
        DEN = sb("den", [P, TILES * H])
        ST = sb("stats", [P, GT, 6])
        MV = sb("mean_var", [P, 2, GT, 2])
        HO = sb("h_out", [P, 2, GT, H * E])
        REST_OF = sb("rest", [P, HIS, H])
        PT = s.enter_context(nc.psum_tensor("mid_turn_ps", [P, BANKS, 512], F32))
        PH = s.enter_context(nc.psum_tensor("mid_h_ps", [P, BANKS, 512], F32))
        block = s.enter_context(nc.Block())
        at = {}
        sums = acc[:, 0:TILES, :].rearrange("p w (h f) -> p (w h) f", h=H)

        @block.vector
        def _(dve):
            link = Chain(dve, step)
            dve.wait_ge(loaded, 48)
            for k in range(2):
                for a in range(2):
                    link(dve.tensor_tensor(PR[:], WG[:, k, 0:16], AT[:, a, :], ALU.mult))
                    link(dve.tensor_reduce(WG[:, k, 16 + H * a:16 + H * (a + 1)],
                                           PR[:].rearrange("p (h e) -> p h e", h=H), AX.X, ALU.add))
            at["w"] = link.n
            link(dve.tensor_scalar(DEN[:].unsqueeze(2), sums[:, :, W:W + 1], 1e-30, None, ALU.max))
            link(dve.reciprocal(DEN[:], DEN[:]))
            base = link.n

            def group(i, n, early):
                link.n = i * (3 + GT) + base
                if not early:
                    dve.wait_ge(x_stored[n], x_count(i, n))
                    dve.wait_ge(made, (i - 1) * GT)
                link(dve.tensor_tensor(X1[:, n].rearrange("p t (h f) -> p (t h) f", h=H),
                                       sums[:, bass.ds(i * (GT * H), GT * H), 0:W],
                                       bcast(DEN[:, bass.ds(i * (GT * H), GT * H)].unsqueeze(2), [P, GT * H, W]), ALU.mult))
                dve.wait_ge(xm_in[n], x_count(i, n) + 16)
                dve.tensor_tensor(X1[:, n], X1[:, n], XM[:, n], ALU.add).then_inc(x_out, 1)
                dve.wait_ge(x_out, i + 1)
                if not (isinstance(i, int) and i == 0):
                    dve.wait_ge(measured, i * GT)
                for q in range(GT):
                    dve.bn_stats(ST[:, q, :], X1[:, n, q, :]).then_inc(step, 1)
                link.n = link.n + GT
                dve.wait_ge(step, link.n)
                stand_apart(dve, apart)
                for q in range(GT):
                    dve.bn_aggr(MV[:, n, q, :], ST[:, q, :]).then_inc(measured, 1)
                dve.wait_ge(rooted, i + 1)
                link(dve.reciprocal(MV[:, n, :, 1], MV[:, n, :, 1]))
                link(dve.tensor_scalar(c.spread[:, bass.ds(i * GT, GT), :], MV[:, n], 1.0, None, ALU.mult))
                if not early:
                    dve.wait_ge(turned, (i - 1) * GT)
                for q in range(GT):
                    dve.tensor_scalar(XN[:, n, q, :], X1[:, n, q, :], MV[:, n, q, 0:1], MV[:, n, q, 1:2], ALU.subtract,
                                      ALU.mult).then_inc(made, 1)

            groups(dve, group)
            dve.wait_ge(scored, TILES)
            link.n = base + (3 + GT) * GROUPS
            for a in range(2):
                for par in range(2):
                    link(dve.tensor_copy(REST_OF[:], c.score[:, a, :, par, :]))
                    for k in range(3):
                        link(dve.tensor_copy(c.scores[:, k, a, par, :, :], REST_OF[:]))
                        if k < 2:
                            link(dve.tensor_tensor(REST_OF[:], REST_OF[:], c.scores[:, k, a, par, :, :], ALU.subtract))

        @block.sync
        def _(sp):
            sp.dma_start(WG[:, :, 0:16], wgat.rearrange("(k i) e -> i k e", k=2)).then_inc(loaded, 16)
            sp.dma_start(AT[:, 0, :], fas.rearrange("h e -> (h e)").partition_broadcast(P)).then_inc(loaded, 16)
            sp.dma_start(AT[:, 1, :], fad.rearrange("h e -> (h e)").partition_broadcast(P)).then_inc(loaded, 16)

            def rows(ap, i):
                return ap.rearrange("(g t i) d -> g i t d", t=GT, i=P)[bass.ds(i, 1)].rearrange("g i t d -> (g i) t d")

            def go(i, n, early):
                if not early:
                    sp.wait_ge(x_out, i - 1)
                sp.dma_start(XM[:, n], rows(d["xm"], i)).then_inc(xm_in[n], 16)
                if not (isinstance(i, int) and i == 0):
                    store(i - 1, 1 - n)

            def store(i, n):
                sp.wait_ge(x_out, i + 1)
                sp.dma_start(rows(d["x1"], i), X1[:, n]).then_inc(x_stored[n], 16)
                sp.wait_ge(rows_out, (i + 1) * GT)
                sp.dma_start(rows(d["ffn_rows"], i), HO[:, n]).then_inc(h_stored[n], 16)

            groups(sp, go)
            store(GROUPS - 1, 0)
            for q in (x_stored, h_stored):
                sp.wait_ge(q[0], 16 * (GROUPS // 2 + 1))
                sp.wait_ge(q[1], 16 * (GROUPS // 2))

        @block.tensor
        def _(pe):
            pe.wait_ge(step, at["w"])

            def turn(i, n, q, first):
                v = i * GT + q
                pe.wait_ge(made, v + 1)
                if not (first and q < BANKS):
                    pe.wait_ge(copied, v + (1 - last_user(q)))
                for k in range(2):
                    last = pe.transpose(PT[:, q % BANKS, k * P:(k + 1) * P], XN[:, n, q, k * P:(k + 1) * P], c.ident[:])
                last.then_inc(turned, 1)

            def project(i, n, q, first):
                v = i * GT + q
                pe.wait_ge(copied, v + 1)
                if not (first and q < BANKS):
                    pe.wait_ge(scored, v + (1 - last_user(q)))
                    pe.wait_ge(rows_out, v + (1 - last_user(q)))
                for k in range(2):
                    last = pe.matmul(PH[:, q % BANKS, 0:24], XT[:, q % BANKS, k * P:(k + 1) * P], WG[:, k, :],
                                     start=k == 0, stop=k == 1)
                last.then_inc(projected, 1)

            def group(i, n, early):
                first = isinstance(i, int) and i == 0
                for q in range(GT):
                    turn(i, n, q, first)
                    if q:
                        project(i, n, q - 1, first)
                project(i, n, GT - 1, first)

            groups(pe, group)

        @block.scalar
        def _(act):
            score = c.score[:].rearrange("p a hi par h -> p a (hi par) h")

            def copy(i, n, q, first):
                v = i * GT + q
                act.wait_ge(turned, v + 1)
                if not (first and q < BANKS):
                    act.wait_ge(projected, v + (1 - last_user(q)))
                act.copy(XT[:, q % BANKS, :], PT[:, q % BANKS, 0:D]).then_inc(copied, 1)

            def take(i, n, q, early):
                v = i * GT + q
                act.wait_ge(projected, v + 1)
                stand_apart(act, act_apart)
                act.copy(score[:, :, bass.ds(v, 1), :].rearrange("p a w h -> p a (w h)"),
                         PH[:, q % BANKS, 16:24].rearrange("p (a h) -> p a h", a=2)).then_inc(scored, 1)
                if q == 0 and not early:
                    act.wait_ge(h_stored[n], x_count(i, n))
                act.copy(HO[:, n, q, :], PH[:, q % BANKS, 0:16]).then_inc(rows_out, 1)

            def group(i, n, early):
                first = isinstance(i, int) and i == 0
                act.wait_ge(measured, (i + 1) * GT)
                act.activation(MV[:, n, :, 1], MV[:, n, :, 1], ACT.Sqrt, bias=c.eps[:, 0:1]).then_inc(rooted, 1)
                for q in range(GT):
                    copy(i, n, q, first)
                    if q:
                        take(i, n, q - 1, early)
                take(i, n, GT - 1, early)

            groups(act, group)


def x_count(i, n):
    return i // 2 * 16 if isinstance(i, int) else (i - n) * 8


def gates(nc, c, sem, acc, gate, bgat, lng, lnb):
    step, loaded, rooted, expd = sem("gate_step"), sem("gate_loaded"), sem("gate_rooted"), sem("gate_exp")
    E = 4
    with ExitStack() as s:
        def sb(name, shape):
            return s.enter_context(nc.sbuf_tensor("gate_" + name, shape, F32))

        BP = sb("b_gamma_beta", [P, 3, 16])
        A = sb("agg", [P, TILES, 16])
        SQ = sb("squares", [P, TILES, 16])
        DEN = sb("den", [P, TILES, H])
        M = sb("mean", [P, TILES])
        V = sb("var", [P, TILES])
        SC = sb("scores", [P, TILES, E])
        RK = sb("rank", [P, TILES, E])
        C1 = sb("cmp", [P, TILES])
        SUM = sb("sum", [P, TILES])
        block = s.enter_context(nc.Block())
        at = {}

        @block.vector
        def _(dve):
            link = Chain(dve, step)
            dve.wait_ge(loaded, 48)
            a4 = acc[:, 0:TILES, :].rearrange("p w (h f) -> p w h f", h=H)
            A4 = A[:].rearrange("p w (h e) -> p w h e", h=H)

            def row(k):
                return bcast(BP[:, k, :].unsqueeze(1), [P, TILES, 16])

            def tile(ap, n=16):
                return bcast(ap.unsqueeze(2), [P, TILES, n])

            link(dve.tensor_scalar(DEN[:].unsqueeze(3), a4[:, :, :, E:E + 1], 1e-16, None, ALU.add))
            link(dve.reciprocal(DEN[:], DEN[:]))
            link(dve.tensor_tensor(A4, a4[:, :, :, 0:E], bcast(DEN[:].unsqueeze(3), [P, TILES, H, E]), ALU.mult))
            link(dve.tensor_tensor(A[:], A[:], row(0), ALU.add))
            link(dve.tensor_reduce(M[:], A[:], AX.X, ALU.add))
            link(dve.tensor_scalar(M[:], M[:], 1.0 / 16, None, ALU.mult))
            link(dve.tensor_tensor(A[:], A[:], tile(M[:]), ALU.subtract))
            link(dve.tensor_tensor(SQ[:], A[:], A[:], ALU.mult))
            link(dve.tensor_reduce(V[:], SQ[:], AX.X, ALU.add))
            at["squared"] = link.n
            dve.wait_ge(rooted, 1)
            link(dve.reciprocal(V[:], V[:]))
            link(dve.tensor_tensor(A[:], A[:], tile(V[:]), ALU.mult))
            link(dve.tensor_tensor(A[:], A[:], row(1), ALU.mult))
            link(dve.tensor_tensor(A[:], A[:], row(2), ALU.add))
            link(dve.tensor_reduce(SC[:], A[:].rearrange("p w (h e) -> p w e h", h=H), AX.X, ALU.add))
            link(dve.tensor_scalar(SC[:], SC[:], 1.0 / H, None, ALU.mult))
            link(dve.memset(RK[:], 0.0))
            for a in range(E):
                for b in range(E):
                    if a != b:
                        op = ALU.is_ge if b < a else ALU.is_gt
                        link(dve.tensor_tensor(C1[:], SC[:, :, b], SC[:, :, a], op))
                        link(dve.tensor_tensor(RK[:, :, a], RK[:, :, a], C1[:], ALU.add))
            link(dve.tensor_scalar(RK[:], RK[:], 2.0, None, ALU.is_lt))
            link(dve.tensor_reduce(M[:], SC[:], AX.X, ALU.max))
            link(dve.tensor_tensor(SC[:], SC[:], tile(M[:], E), ALU.subtract))
            at["shifted"] = link.n
            dve.wait_ge(expd, 1)
            link(dve.tensor_tensor(SC[:], SC[:], RK[:], ALU.mult))
            link(dve.tensor_reduce(SUM[:], SC[:], AX.X, ALU.add))
            link(dve.reciprocal(SUM[:], SUM[:]))
            link(dve.tensor_tensor(gate[:], SC[:], tile(SUM[:], E), ALU.mult))

        @block.sync
        def _(sp):
            for k, a in enumerate((bgat, lng, lnb)):
                sp.dma_start(BP[:, k, :], a.partition_broadcast(P)).then_inc(loaded, 16)

        @block.scalar
        def _(act):
            act.wait_ge(step, at["squared"])
            act.activation(V[:], V[:], ACT.Sqrt, bias=c.eps[:, 0:1], scale=1.0 / 16).then_inc(rooted, 1)
            act.wait_ge(step, at["shifted"])
            act.activation(SC[:], SC[:], ACT.Exp).then_inc(expd, 1)


def experts(nc, c, sem, d, out, gate, w1, b1, w2, b2):
    E, HID, GT = 4, 512, 4
    HC = HID // P
    FULL = TILES // GT
    assert TILES == FULL * GT + 1 and FULL % 2 == 0
    PG = GT * E
    b1_in, b2_in, w1_in, w2_in = (sem("exp_%s_loaded" % n) for n in ("b1", "b2", "w1", "w2"))
    step, prepared, made, turned, copied, hidden, gelu, product, added = (
        sem("exp_" + n) for n in ("step", "prepared", "xn", "turned", "copied", "hidden", "gelu", "product",
                                  "added"))
    x_in = [sem("exp_x_in0"), sem("exp_x_in1")]
    stored = [sem("exp_stored0"), sem("exp_stored1")]
    with ExitStack() as s:
        def sb(name, shape, dt=F32):
            return s.enter_context(nc.sbuf_tensor("exp_" + name, shape, dt))

        W1 = sb("w1", [P, E, 2, HID])
        W2 = sb("w2", [P, E, HC, D])
        B1 = sb("b1", [P, E, HC])
        B2 = sb("b2", [P, E, D])
        X = sb("x", [P, 2, GT, D])
        XN = sb("xn", [P, GT, D])
        XT = sb("xn_turned", [P, 2, 2, GT * P])
        HT = sb("hidden", [P, 2, HC, GT * P])
        O = sb("out", [P, 2, GT, D])
        PT = s.enter_context(nc.psum_tensor("exp_turn_ps", [P, 2, 512], F32))
        PH = s.enter_context(nc.psum_tensor("exp_hidden_ps", [P, 2, 512], F32))
        PO = s.enter_context(nc.psum_tensor("exp_out_ps", [P, 2, 512], F32))
        block = s.enter_context(nc.Block())

        def groups(engine, body):
            body(0, 0, GT, GT)
            with engine.Fori(0, FULL // 2 - 1) as j:
                body(j * 2 + 1, 1, GT, GT)
                body(j * 2 + 2, 0, GT, GT)
            body(FULL - 1, 1, GT, 1)
            body(FULL, 0, 1, 0)

        def static(i, n):
            return isinstance(i, int) and i < n

        @block.sync
        def _(sp):
            x4 = d["x1"][0:FULL * GT * P, :].rearrange("(g t i) d -> g i t d", t=GT, i=P)
            o4 = out[0:FULL * GT * P, :].rearrange("(g t i) d -> g i t d", t=GT, i=P)
            sp.dma_start(X[:, 0, :, :], x4[0]).then_inc(x_in[0], 16)
            sp.dma_start(B2[:], b2.partition_broadcast(P)).then_inc(b2_in, 16)
            sp.dma_start(B1[:], b1.rearrange("e (c i) -> i e c", c=HC)).then_inc(b1_in, 16)
            sp.dma_start(W1[:], w1.rearrange("e (k i) h -> i e k h", k=2)).then_inc(w1_in, 16)
            sp.dma_start(W2[:], w2.rearrange("e (c i) o -> i e c o", c=HC)).then_inc(w2_in, 16)

            def go(i, n, tiles, after):
                if after:
                    if not static(i, 1):
                        sp.wait_ge(prepared, i)
                    if after == GT:
                        sp.dma_start(X[:, 1 - n, :, :], x4[bass.ds(i + 1, 1)].rearrange("g i t d -> (g i) t d")
                                     ).then_inc(x_in[1 - n], 16)
                    else:
                        sp.dma_start(X[:, 1 - n, 0, :], d["x1"][FULL * GT * P:NPAD, :]).then_inc(x_in[1 - n], 16)
                sp.wait_ge(added, i * PG + tiles * E)
                if tiles == GT:
                    sp.dma_start(o4[bass.ds(i, 1)].rearrange("g i t d -> (g i) t d"), O[:, n, :, :]).then_inc(stored[n], 16)
                else:
                    sp.dma_start(out[FULL * GT * P:N, :], O[0:LAST, n, 0, :]).then_inc(stored[n], 16)

            groups(sp, go)
            sp.wait_ge(stored[0], 16 * (FULL // 2 + 1))
            sp.wait_ge(stored[1], 16 * (FULL // 2))

        @block.vector
        def _(dve):
            link = Chain(dve, step)
            LINKS = GT * E

            def gate_at(i, q, ei):
                return gate[:, bass.ds(i * GT + q, 1), ei]

            def prepare(i, n, tiles):
                link.n = i * LINKS
                dve.wait_ge(x_in[n], x_count(i, n) + 16)
                for q in range(tiles):
                    v = i * GT + q
                    mv = c.spread[:, bass.ds(v, 1), :].rearrange("p w s -> p (w s)")
                    if not static(i, 1):
                        dve.wait_ge(turned, v - GT + 1)
                    dve.tensor_scalar(XN[:, q, :], X[:, n, q, :], mv[:, 0:1], mv[:, 1:2], ALU.subtract,
                                      ALU.mult).then_inc(made, 1)
                    dve.wait_ge(made, v + 1)
                if not static(i, 2):
                    dve.wait_ge(stored[n], x_count(i, n))
                for q in range(tiles):
                    for ei in range(E):
                        of = X[:, n, q, :] if ei == 0 else O[:, n, q, :]
                        link(dve.scalar_tensor_tensor(O[:, n, q, :], B2[:, ei, :], gate_at(i, q, ei), of, ALU.mult, ALU.add))
                dve.sem_inc(prepared, 1)

            def go(i, n, tiles, after):
                if after:
                    prepare(i + 1, 1 - n, after)
                for ei in range(E):
                    for q in range(tiles):
                        v = i * PG + (ei * tiles + q)
                        dve.wait_ge(product, v + 1)
                        if ei:
                            dve.wait_ge(added, v - tiles + 1)
                        dve.scalar_tensor_tensor(O[:, n, q, :], PO[:, (ei * tiles + q) % 2, 0:D], gate_at(i, q, ei),
                                                 O[:, n, q, :], ALU.mult, ALU.add).then_inc(added, 1)

            dve.wait_ge(b2_in, 16)
            prepare(0, 0, GT)
            groups(dve, go)

        @block.tensor
        def _(pe):
            def turn(i, n, tiles):
                for q in range(tiles):
                    v = i * GT + q
                    pe.wait_ge(made, v + 1)
                    if not (static(i, 1) and q < 2):
                        pe.wait_ge(copied, v - 1)
                    for k in range(2):
                        last = pe.transpose(PT[:, q % 2, k * P:(k + 1) * P], XN[:, q, k * P:(k + 1) * P], c.ident[:])
                    last.then_inc(turned, 1)

            def up(i, n, tiles, ei):
                for h in range(HC):
                    v = i * PG + (ei * HC + h)
                    if not (static(i, 1) and ei == 0 and h < 2):
                        pe.wait_ge(gelu, v - 1)
                    for k in range(2):
                        last = pe.matmul(PH[:, h % 2, 0:tiles * P], W1[:, ei, k, h * P:(h + 1) * P],
                                         XT[:, n, k, 0:tiles * P], start=k == 0, stop=k == 1)
                    last.then_inc(hidden, 1)

            def down(i, n, tiles, ei):
                pe.wait_ge(gelu, i * PG + (ei + 1) * HC)
                for q in range(tiles):
                    p = ei * tiles + q
                    if not (static(i, 1) and p < 2):
                        pe.wait_ge(added, i * PG + p - 1)
                    for h in range(HC):
                        last = pe.matmul(PO[:, p % 2, 0:D], HT[:, ei % 2, h, q * P:(q + 1) * P], W2[:, ei, h, :],
                                         start=h == 0, stop=h == HC - 1)
                    last.then_inc(product, 1)

            def go(i, n, tiles, after):
                pe.wait_ge(copied, i * GT + tiles)
                up(i, n, tiles, 0)
                if after:
                    turn(i + 1, 1 - n, after)
                for ei in range(1, E):
                    up(i, n, tiles, ei)
                    if static(i, 1) and ei == 1:
                        pe.wait_ge(w2_in, 16)
                    down(i, n, tiles, ei - 1)
                down(i, n, tiles, E - 1)

            turn(0, 0, GT)
            pe.wait_ge(w1_in, 16)
            groups(pe, go)

        @block.scalar
        def _(act):
            def copy(i, n, tiles):
                for q in range(tiles):
                    act.wait_ge(turned, i * GT + q + 1)
                    act.copy(XT[:, n, :, q * P:(q + 1) * P], PT[:, q % 2, 0:D].rearrange("p (k i) -> p k i", k=2)
                             ).then_inc(copied, 1)

            def go(i, n, tiles, after):
                for ei in range(E):
                    done = (ei - 1) * tiles if ei >= 2 else (ei - 1) * GT
                    if not (static(i, 1) and ei < 2):
                        act.wait_ge(product, i * PG + done)
                    for h in range(HC):
                        act.wait_ge(hidden, i * PG + (ei * HC + h + 1))
                        act.activation(HT[:, ei % 2, h, 0:tiles * P], PH[:, h % 2, 0:tiles * P], ACT.Gelu,
                                       bias=B1[:, ei, h:h + 1]).then_inc(gelu, 1)
                    if ei == 0 and after:
                        copy(i + 1, 1 - n, after)

            copy(0, 0, GT)
            act.wait_ge(b1_in, 16)
            groups(act, go)


_INS = ["x", "src", "dst", "L0_gnn_W", "L0_gnn_a_src", "L0_gnn_a_dst", "L0_mix_Wqkv", "L0_mix_Wout", "L0_mix_gamma",
        "L0_ffn_W_gat", "L0_ffn_att_src", "L0_ffn_att_dst", "L0_ffn_b_gat", "L0_ffn_ln_gamma", "L0_ffn_ln_beta",
        "L0_ffn_W1", "L0_ffn_b1", "L0_ffn_W2", "L0_ffn_b2", "L0_ffn_edge_index"]
_OUTS = [((N, D), "float32")]


def kernel(**inputs):
    import numpy as _np
    import concourse.bacc as _bacc
    from concourse import mybir as _mybir
    from concourse.bass_utils import run_bass_kernel_spmd as _run

    nc = _bacc.Bacc("TRN2", target_bir_lowering=False, num_devices=1)
    arrays, args = {}, []
    for name in _INS:
        a = _np.ascontiguousarray(inputs[name])
        arrays[f"in_{name}_dram"] = a
        args.append(nc.dram_tensor(f"in_{name}_dram", a.shape, _mybir.dt.from_np(a.dtype), kind="ExternalInput").ap())
    for i, (shape, dtype) in enumerate(_OUTS):
        dt = _mybir.dt.from_np(_np.dtype(dtype))
        args.append(nc.dram_tensor(f"out_{i}_dram", shape, dt, kind="ExternalOutput").ap())
    build_program(nc, *args)
    r = _run(nc, [arrays], core_ids=[0])
    got = tuple(r.results[0][f"out_{i}_dram"] for i in range(len(_OUTS)))
    return got[0]
```
